# Optimizing a Trainium2 kernel written in Bass

```python
import numpy as np
import jax
import jax.numpy as jnp

def _softmax(x, axis=-1):
    return jax.nn.softmax(x, axis=axis)

def _gelu(x):
    return jax.nn.gelu(x, approximate=True)

def _silu(x):
    return jax.nn.silu(x)

def _sigmoid(x):
    return jax.nn.sigmoid(x)

def _layernorm(x, axis=-1, eps=1e-05):
    m = jnp.mean(x, axis=axis, keepdims=True)
    v = jnp.var(x, axis=axis, keepdims=True)
    return (x - m) / jnp.sqrt(v + eps)

def _scatter_add(tgt, idx, src, axis=0):
    return tgt.at[idx].add(src)

def _segment_sum(src, seg, n):
    return jax.ops.segment_sum(src, seg, n)
kernel_name = 'mk_perceiver_d2_seqx_r8_e2ea0e'

def setup_inputs(seed: int=0):
    np.random.seed(seed)
    _w = jnp.asarray

    def _rec_inputs():
        import jax
        import jax.numpy as jnp
        _rk = jax.random.key(seed)
        x = -0.0002928 + 1 * jax.random.normal(jax.random.fold_in(_rk, 1), (8, 32, 128), jnp.float32)
        _lenS = 32 - jax.random.randint(jax.random.fold_in(_rk, 7), (8,), 0, max(1, 32 // 4) + 1, jnp.int32)
        _lenS2 = 512 - jax.random.randint(jax.random.fold_in(_rk, 8), (8,), 0, max(1, 512 // 4) + 1, jnp.int32)
        _ctx_1024P = jax.random.normal(jax.random.fold_in(_rk, 11), (8, 16, 128), jnp.float32)
        _ctx_1024c = jax.random.dirichlet(jax.random.fold_in(_rk, 511), 0.3 * jnp.ones((16,), jnp.float32), (8, 512))
        _ctx_1024t = jnp.einsum('bsk,bkd->bsd', _ctx_1024c, _ctx_1024P)
        _ctx_1024t = _ctx_1024t * jax.lax.rsqrt(jnp.mean(jnp.square(_ctx_1024t)) + 1e-12) * 0.953939
        ctx_1024 = -0.000191848 + 0.999787 * (_ctx_1024t + 0.3 * jax.random.normal(jax.random.fold_in(_rk, 611), (8, 512, 128), jnp.float32))
        _validS = jnp.arange(32)[None, :] < _lenS[:, None]
        _validS2 = jnp.arange(512)[None, :] < _lenS2[:, None]
        _causal = jnp.tril(jnp.ones((32, 32), dtype=bool))
        mask_BxS2_bk0 = jnp.logical_not(jnp.broadcast_to(_validS2[:, :], (8, 512)))
        return (x, ctx_1024, mask_BxS2_bk0)
    x, ctx_1024, mask_BxS2_bk0 = _rec_inputs()

    def _L0_xattn_setup():
        import jax, jax.numpy as jnp
        import numpy as np
        NUM_HEADS = 16
        EPS = 1e-06

        def _ln(t, w, b):
            mu = jnp.mean(t, axis=-1, keepdims=True)
            var = jnp.mean(jnp.square(t - mu), axis=-1, keepdims=True)
            return (t - mu) * jax.lax.rsqrt(var + EPS) * w + b
        key = jax.random.key(seed)
        ks = jax.random.split(key, 10)
        b, s1, s2, qdim, kdim = (2, 256, 384, 128, 128)
        d = qdim // NUM_HEADS
        x = jax.random.normal(ks[0], (b, s1, qdim), dtype=jnp.float32)
        y = jax.random.normal(ks[1], (b, s2, kdim), dtype=jnp.float32)
        padding_mask = jax.random.randint(ks[2], (b, s2), 0, 2) > 0
        padding_mask = padding_mask.at[:, 0].set(True)
        w = 0.02
        Wq = jax.random.normal(ks[3], (qdim, qdim), dtype=jnp.float32) * w
        bq = jnp.zeros((qdim,), jnp.float32)
        Wkv = jax.random.normal(ks[4], (2 * qdim, kdim), dtype=jnp.float32) * w
        bkv = jnp.zeros((2 * qdim,), jnp.float32)
        qn_w = jnp.ones((d,), jnp.float32)
        qn_b = jnp.zeros((d,), jnp.float32)
        kn_w = jnp.ones((d,), jnp.float32)
        kn_b = jnp.zeros((d,), jnp.float32)
        Wo = jax.random.normal(ks[5], (qdim, qdim), dtype=jnp.float32) * w
        bo = jnp.zeros((qdim,), jnp.float32)
        return {'x': x, 'y': y, 'padding_mask': padding_mask, 'Wq': Wq, 'bq': bq, 'Wkv': Wkv, 'bkv': bkv, 'qn_w': qn_w, 'qn_b': qn_b, 'kn_w': kn_w, 'kn_b': kn_b, 'Wo': Wo, 'bo': bo}
    _L0_xattn_all = _L0_xattn_setup()
    _L0_xattn_in = {k: v for k, v in _L0_xattn_all.items() if k in ('Wq', 'bq', 'Wkv', 'bkv', 'qn_w', 'qn_b', 'kn_w', 'kn_b', 'Wo', 'bo')}
    del _L0_xattn_all

    def _L0_attn_setup():
        import jax, jax.numpy as jnp
        import numpy as np
        B, N, DIM = (4, 128, 128)
        H, D = (16, 64)
        SW = 32
        ROPE_BASE = 10000.0
        LN_EPS = 1e-05

        def _layernorm(x, w, b):
            mu = jnp.mean(x, axis=-1, keepdims=True)
            var = jnp.mean((x - mu) ** 2, axis=-1, keepdims=True)
            return (x - mu) * jax.lax.rsqrt(var + LN_EPS) * w + b

        def _rotate_half(x):
            x1, x2 = jnp.split(x, 2, axis=-1)
            return jnp.concatenate([-x2, x1], axis=-1)
        key = jax.random.key(seed)
        ks = jax.random.split(key, 8)
        s = 0.02
        return {'x': jax.random.normal(ks[0], (B, N, DIM), dtype=jnp.float32), 'qkv_w': jax.random.normal(ks[1], (3 * H * D, DIM), dtype=jnp.float32) * s, 'qn_w': jnp.ones((D,), jnp.float32), 'qn_b': jnp.zeros((D,), jnp.float32), 'kn_w': jnp.ones((D,), jnp.float32), 'kn_b': jnp.zeros((D,), jnp.float32), 'sinks': jax.random.normal(ks[2], (H,), dtype=jnp.float32), 'proj_w': jax.random.normal(ks[3], (DIM, H * D), dtype=jnp.float32) * s, 'proj_b': jnp.zeros((DIM,), jnp.float32)}
    _L0_attn_all = _L0_attn_setup()
    _L0_attn_in = {k: v for k, v in _L0_attn_all.items() if k in ('qkv_w', 'qn_w', 'qn_b', 'kn_w', 'kn_b', 'sinks', 'proj_w', 'proj_b')}
    del _L0_attn_all

    def _L0_ffn_setup():
        import jax, jax.numpy as jnp
        import numpy as np
        B, S, H = (2, 256, 128)
        F = 512
        E = 8
        TOP_K = 2
        SHARED_SCALE = 0.1
        EPS = 1e-09

        def _moe_forward(x3, Wg, W1, b1, W2, b2, Ws1, bs1, Ws2, bs2):
            b, s, h = x3.shape
            x = x3.reshape(-1, h)
            T = x.shape[0]
            logits = x @ Wg
            probs = jax.nn.softmax(logits, axis=-1)
            vals, idx = jax.lax.top_k(probs, TOP_K)
            weights = vals / (jnp.sum(vals, axis=-1, keepdims=True) + EPS)
            cw = jnp.zeros((T, E), dtype=x.dtype).at[jnp.arange(T)[:, None], idx].set(weights)
            hpre = jnp.einsum('th,ehf->tef', x, W1) + b1
            act = jax.nn.silu(hpre)
            y = jnp.einsum('tef,efh->teh', act, W2) + b2
            out = jnp.einsum('te,teh->th', cw, y)
            shared = jax.nn.silu(x @ Ws1 + bs1) @ Ws2 + bs2
            out = out + SHARED_SCALE * shared
            return out.reshape(b, s, h)
        key = jax.random.key(seed)
        ks = jax.random.split(key, 10)
        sc = 0.02
        return {'hidden_states': jax.random.normal(ks[0], (B, S, H), dtype=jnp.float32), 'Wg': jax.random.normal(ks[1], (H, E), dtype=jnp.float32) * sc, 'W1': jax.random.normal(ks[2], (E, H, F), dtype=jnp.float32) * sc, 'b1': jnp.zeros((E, F), dtype=jnp.float32), 'W2': jax.random.normal(ks[3], (E, F, H), dtype=jnp.float32) * sc, 'b2': jnp.zeros((E, H), dtype=jnp.float32), 'Ws1': jax.random.normal(ks[4], (H, F), dtype=jnp.float32) * sc, 'bs1': jnp.zeros((F,), dtype=jnp.float32), 'Ws2': jax.random.normal(ks[5], (F, H), dtype=jnp.float32) * sc, 'bs2': jnp.zeros((H,), dtype=jnp.float32)}
    _L0_ffn_all = _L0_ffn_setup()
    _L0_ffn_in = {k: v for k, v in _L0_ffn_all.items() if k in ('Wg', 'W1', 'b1', 'W2', 'b2', 'Ws1', 'bs1', 'Ws2', 'bs2')}
    del _L0_ffn_all

    def _L1_xattn_setup():
        import jax, jax.numpy as jnp
        import numpy as np
        key = jax.random.key(seed)
        ks = jax.random.split(key, 8)
        B, T, S = (32, 128, 128)
        Din, H, C = (128, 128, 128)
        s = 0.02
        return {'x': jax.random.normal(ks[0], (B, T, Din), jnp.float32), 'context': jax.random.normal(ks[1], (B, S, C), jnp.float32), 'W_ih': jax.random.normal(ks[2], (4 * H, Din + H), jnp.float32) * s, 'W_hh': jax.random.normal(ks[3], (4 * H, H), jnp.float32) * s, 'b_ih': jnp.zeros((4 * H,), jnp.float32), 'b_hh': jnp.zeros((4 * H,), jnp.float32), 'Wq': jax.random.normal(ks[4], (C, H), jnp.float32) * s, 'Wout': jax.random.normal(ks[5], (H, C + H), jnp.float32) * s, 'b_out': jnp.zeros((H,), jnp.float32)}
    _L1_xattn_all = _L1_xattn_setup()
    _L1_xattn_in = {k: v for k, v in _L1_xattn_all.items() if k in ('W_ih', 'W_hh', 'b_ih', 'b_hh', 'Wq', 'Wout', 'b_out')}
    del _L1_xattn_all

    def _L1_attn_setup():
        import jax, jax.numpy as jnp
        import numpy as np
        D_MODEL = 128
        N_LAYERS = 4
        D_STATE = 16
        D_CONV = 4
        EXPAND = 2
        D_INNER = EXPAND * D_MODEL
        DT_RANK = D_MODEL // 16
        B_SZ = 2
        SEQ = 128
        EPS = 1e-05

        def _layer_norm(x, w, b):
            m = x.mean(-1, keepdims=True)
            v = x.var(-1, keepdims=True)
            return (x - m) * jax.lax.rsqrt(v + EPS) * w + b

        def _mamba(x, in_w, cw, cb, xpw, dtw, dtb, A_log, Dp, ow):
            B, L, _ = x.shape
            xz = x @ in_w
            u, z = jnp.split(xz, 2, axis=-1)
            up = jnp.pad(u, ((0, 0), (D_CONV - 1, 0), (0, 0)))
            uc = cb + sum((up[:, k:k + L, :] * cw[:, k] for k in range(D_CONV)))
            u = jax.nn.silu(uc)
            proj = u @ xpw
            dt = proj[..., :DT_RANK]
            Bm = proj[..., DT_RANK:DT_RANK + D_STATE]
            Cm = proj[..., DT_RANK + D_STATE:]
            delta = jax.nn.softplus(dt @ dtw + dtb)
            A = -jnp.exp(A_log)

            def step(h, inp):
                d_t, b_t, c_t, u_t = inp
                dA = jnp.exp(d_t[..., None] * A)
                h = dA * h + (d_t * u_t)[..., None] * b_t[:, None, :]
                y = jnp.einsum('bdn,bn->bd', h, c_t)
                return (h, y)
            h0 = jnp.zeros((B, D_INNER, D_STATE), x.dtype)
            xs = (jnp.moveaxis(delta, 1, 0), jnp.moveaxis(Bm, 1, 0), jnp.moveaxis(Cm, 1, 0), jnp.moveaxis(u, 1, 0))
            _, ys = jax.lax.scan(step, h0, xs)
            y = jnp.moveaxis(ys, 0, 1) + u * Dp
            y = y * jax.nn.silu(z)
            return y @ ow
        key = jax.random.key(seed)
        ks = jax.random.split(key, 8)

        def nrm(k, shape, s=0.02):
            return jax.random.normal(k, shape, jnp.float32) * s
        x = jax.random.normal(ks[0], (B_SZ, SEQ, D_MODEL), jnp.float32)
        in_proj_w = nrm(ks[1], (N_LAYERS, D_MODEL, 2 * D_INNER))
        conv_w = nrm(ks[2], (N_LAYERS, D_INNER, D_CONV), 0.1)
        conv_b = jnp.zeros((N_LAYERS, D_INNER), jnp.float32)
        x_proj_w = nrm(ks[3], (N_LAYERS, D_INNER, DT_RANK + 2 * D_STATE))
        dt_proj_w = nrm(ks[4], (N_LAYERS, DT_RANK, D_INNER), 0.1)
        dt_proj_b = jax.random.uniform(ks[5], (N_LAYERS, D_INNER), jnp.float32, -4.0, -2.0)
        A_log = jnp.tile(jnp.log(jnp.arange(1, D_STATE + 1, dtype=jnp.float32)), (N_LAYERS, D_INNER, 1))
        D = jnp.ones((N_LAYERS, D_INNER), jnp.float32)
        out_proj_w = nrm(ks[6], (N_LAYERS, D_INNER, D_MODEL))
        ln_w = jnp.ones((N_LAYERS, D_MODEL), jnp.float32)
        ln_b = jnp.zeros((N_LAYERS, D_MODEL), jnp.float32)
        return dict(x=x, in_proj_w=in_proj_w, conv_w=conv_w, conv_b=conv_b, x_proj_w=x_proj_w, dt_proj_w=dt_proj_w, dt_proj_b=dt_proj_b, A_log=A_log, D=D, out_proj_w=out_proj_w, ln_w=ln_w, ln_b=ln_b)
    _L1_attn_all = _L1_attn_setup()
    _L1_attn_in = {k: v for k, v in _L1_attn_all.items() if k in ('in_proj_w', 'conv_w', 'conv_b', 'x_proj_w', 'dt_proj_w', 'dt_proj_b', 'A_log', 'D', 'out_proj_w', 'ln_w', 'ln_b')}
    del _L1_attn_all

    def _L1_ffn_setup():
        import jax, jax.numpy as jnp
        import numpy as np
        B, S, D, F, E, R = (4, 256, 128, 512, 8, 4)
        key = jax.random.key(seed)
        ks = jax.random.split(key, 8)
        s_in = 1.0 / np.sqrt(D)
        s_ff = 1.0 / np.sqrt(F)
        return {'hidden_states': jax.random.normal(ks[0], (B, S, D), jnp.float32), 'gate_W': jax.random.normal(ks[1], (E, D), jnp.float32) * s_in, 'gate_b': jnp.zeros((E,), jnp.float32), 'wi_W': jax.random.normal(ks[2], (F, D), jnp.float32) * s_in, 'wi_b': jnp.zeros((F,), jnp.float32), 'wo_W': jax.random.normal(ks[3], (D, F), jnp.float32) * s_ff, 'wo_b': jnp.zeros((D,), jnp.float32), 'lora_A': jax.random.normal(ks[4], (E, R, D), jnp.float32) * s_in, 'lora_B': jax.random.normal(ks[5], (E, F, R), jnp.float32) * 0.02}
    _L1_ffn_all = _L1_ffn_setup()
    _L1_ffn_in = {k: v for k, v in _L1_ffn_all.items() if k in ('gate_W', 'gate_b', 'wi_W', 'wi_b', 'wo_W', 'wo_b', 'lora_A', 'lora_B')}
    del _L1_ffn_all
    return {'x': x, 'ctx_1024': ctx_1024, 'mask_BxS2_bk0': mask_BxS2_bk0, 'L0_xattn_Wq': _L0_xattn_in['Wq'], 'L0_xattn_bq': _L0_xattn_in['bq'], 'L0_xattn_Wkv': _L0_xattn_in['Wkv'], 'L0_xattn_bkv': _L0_xattn_in['bkv'], 'L0_xattn_qn_w': _L0_xattn_in['qn_w'], 'L0_xattn_qn_b': _L0_xattn_in['qn_b'], 'L0_xattn_kn_w': _L0_xattn_in['kn_w'], 'L0_xattn_kn_b': _L0_xattn_in['kn_b'], 'L0_xattn_Wo': _L0_xattn_in['Wo'], 'L0_xattn_bo': _L0_xattn_in['bo'], 'L0_attn_qkv_w': _L0_attn_in['qkv_w'], 'L0_attn_qn_w': _L0_attn_in['qn_w'], 'L0_attn_qn_b': _L0_attn_in['qn_b'], 'L0_attn_kn_w': _L0_attn_in['kn_w'], 'L0_attn_kn_b': _L0_attn_in['kn_b'], 'L0_attn_sinks': _L0_attn_in['sinks'], 'L0_attn_proj_w': _L0_attn_in['proj_w'], 'L0_attn_proj_b': _L0_attn_in['proj_b'], 'L0_ffn_Wg': _L0_ffn_in['Wg'], 'L0_ffn_W1': _L0_ffn_in['W1'], 'L0_ffn_b1': _L0_ffn_in['b1'], 'L0_ffn_W2': _L0_ffn_in['W2'], 'L0_ffn_b2': _L0_ffn_in['b2'], 'L0_ffn_Ws1': _L0_ffn_in['Ws1'], 'L0_ffn_bs1': _L0_ffn_in['bs1'], 'L0_ffn_Ws2': _L0_ffn_in['Ws2'], 'L0_ffn_bs2': _L0_ffn_in['bs2'], 'L1_xattn_W_ih': _L1_xattn_in['W_ih'], 'L1_xattn_W_hh': _L1_xattn_in['W_hh'], 'L1_xattn_b_ih': _L1_xattn_in['b_ih'], 'L1_xattn_b_hh': _L1_xattn_in['b_hh'], 'L1_xattn_Wq': _L1_xattn_in['Wq'], 'L1_xattn_Wout': _L1_xattn_in['Wout'], 'L1_xattn_b_out': _L1_xattn_in['b_out'], 'L1_attn_in_proj_w': _L1_attn_in['in_proj_w'], 'L1_attn_conv_w': _L1_attn_in['conv_w'], 'L1_attn_conv_b': _L1_attn_in['conv_b'], 'L1_attn_x_proj_w': _L1_attn_in['x_proj_w'], 'L1_attn_dt_proj_w': _L1_attn_in['dt_proj_w'], 'L1_attn_dt_proj_b': _L1_attn_in['dt_proj_b'], 'L1_attn_A_log': _L1_attn_in['A_log'], 'L1_attn_D': _L1_attn_in['D'], 'L1_attn_out_proj_w': _L1_attn_in['out_proj_w'], 'L1_attn_ln_w': _L1_attn_in['ln_w'], 'L1_attn_ln_b': _L1_attn_in['ln_b'], 'L1_ffn_gate_W': _L1_ffn_in['gate_W'], 'L1_ffn_gate_b': _L1_ffn_in['gate_b'], 'L1_ffn_wi_W': _L1_ffn_in['wi_W'], 'L1_ffn_wi_b': _L1_ffn_in['wi_b'], 'L1_ffn_wo_W': _L1_ffn_in['wo_W'], 'L1_ffn_wo_b': _L1_ffn_in['wo_b'], 'L1_ffn_lora_A': _L1_ffn_in['lora_A'], 'L1_ffn_lora_B': _L1_ffn_in['lora_B']}

def reference(x, ctx_1024, mask_BxS2_bk0, L0_xattn_Wq, L0_xattn_bq, L0_xattn_Wkv, L0_xattn_bkv, L0_xattn_qn_w, L0_xattn_qn_b, L0_xattn_kn_w, L0_xattn_kn_b, L0_xattn_Wo, L0_xattn_bo, L0_attn_qkv_w, L0_attn_qn_w, L0_attn_qn_b, L0_attn_kn_w, L0_attn_kn_b, L0_attn_sinks, L0_attn_proj_w, L0_attn_proj_b, L0_ffn_Wg, L0_ffn_W1, L0_ffn_b1, L0_ffn_W2, L0_ffn_b2, L0_ffn_Ws1, L0_ffn_bs1, L0_ffn_Ws2, L0_ffn_bs2, L1_xattn_W_ih, L1_xattn_W_hh, L1_xattn_b_ih, L1_xattn_b_hh, L1_xattn_Wq, L1_xattn_Wout, L1_xattn_b_out, L1_attn_in_proj_w, L1_attn_conv_w, L1_attn_conv_b, L1_attn_x_proj_w, L1_attn_dt_proj_w, L1_attn_dt_proj_b, L1_attn_A_log, L1_attn_D, L1_attn_out_proj_w, L1_attn_ln_w, L1_attn_ln_b, L1_ffn_gate_W, L1_ffn_gate_b, L1_ffn_wi_W, L1_ffn_wi_b, L1_ffn_wo_W, L1_ffn_wo_b, L1_ffn_lora_A, L1_ffn_lora_B):
    import jax
    import jax.numpy as jnp

    def _L0_xattn_ref(x, y, padding_mask, Wq, bq, Wkv, bkv, qn_w, qn_b, kn_w, kn_b, Wo, bo):
        import jax, jax.numpy as jnp
        import numpy as np
        NUM_HEADS = 16
        EPS = 1e-06

        def _ln(t, w, b):
            mu = jnp.mean(t, axis=-1, keepdims=True)
            var = jnp.mean(jnp.square(t - mu), axis=-1, keepdims=True)
            return (t - mu) * jax.lax.rsqrt(var + EPS) * w + b
        b, s1, c = x.shape
        s2 = y.shape[1]
        h, d = (NUM_HEADS, c // NUM_HEADS)
        scale = d ** (-0.5)
        q = (x @ Wq.T + bq).reshape(b, s1, h, d)
        kv = (y @ Wkv.T + bkv).reshape(b, s2, 2, h, d)
        k, v = (kv[:, :, 0], kv[:, :, 1])
        q = _ln(q, qn_w, qn_b) * scale
        k = _ln(k, kn_w, kn_b)
        attn = jnp.einsum('bihd,bjhd->bhij', q, k)
        attn = jnp.where(padding_mask[:, None, None, :], attn, -jnp.inf)
        p = jax.nn.softmax(attn, axis=-1)
        ctx = jnp.einsum('bhij,bjhd->bihd', p, v).reshape(b, s1, c)
        out = ctx @ Wo.T + bo
        return out

    def _L0_attn_ref(x, qkv_w, qn_w, qn_b, kn_w, kn_b, sinks, proj_w, proj_b):
        import jax, jax.numpy as jnp
        import numpy as np
        B, N, DIM = (4, 128, 128)
        H, D = (16, 64)
        SW = 32
        ROPE_BASE = 10000.0
        LN_EPS = 1e-05

        def _layernorm(x, w, b):
            mu = jnp.mean(x, axis=-1, keepdims=True)
            var = jnp.mean((x - mu) ** 2, axis=-1, keepdims=True)
            return (x - mu) * jax.lax.rsqrt(var + LN_EPS) * w + b

        def _rotate_half(x):
            x1, x2 = jnp.split(x, 2, axis=-1)
            return jnp.concatenate([-x2, x1], axis=-1)
        Bx, Nx, _ = x.shape
        qkv = (x @ qkv_w.T).reshape(Bx, Nx, 3, H, D).transpose(2, 0, 3, 1, 4)
        q, k, v = (qkv[0], qkv[1], qkv[2])
        q = _layernorm(q, qn_w, qn_b)
        k = _layernorm(k, kn_w, kn_b)
        inv_freq = 1.0 / ROPE_BASE ** (jnp.arange(0, D, 2, dtype=jnp.float32) / D)
        freqs = jnp.arange(Nx, dtype=jnp.float32)[:, None] * inv_freq[None, :]
        emb = jnp.concatenate([freqs, freqs], axis=-1)
        cos, sin = (jnp.cos(emb), jnp.sin(emb))
        q = q * cos + _rotate_half(q) * sin
        k = k * cos + _rotate_half(k) * sin
        sm_scale = 1.0 / np.sqrt(D)
        scores = jnp.einsum('bhqd,bhkd->bhqk', q, k) * sm_scale
        i = jnp.arange(Nx)[:, None]
        j = jnp.arange(Nx)[None, :]
        allowed = (j <= i) & (j > i - SW)
        scores = jnp.where(allowed, scores, -jnp.inf)
        sink_col = jnp.broadcast_to(sinks[None, :, None, None], (Bx, H, Nx, 1))
        logits = jnp.concatenate([scores, sink_col], axis=-1)
        probs = jax.nn.softmax(logits, axis=-1)[..., :-1]
        out = jnp.einsum('bhqk,bhkd->bhqd', probs, v)
        out = out.transpose(0, 2, 1, 3).reshape(Bx, Nx, H * D)
        return out @ proj_w.T + proj_b

    def _L0_ffn_ref(hidden_states, Wg, W1, b1, W2, b2, Ws1, bs1, Ws2, bs2):
        import jax, jax.numpy as jnp
        import numpy as np
        B, S, H = (2, 256, 128)
        F = 512
        E = 8
        TOP_K = 2
        SHARED_SCALE = 0.1
        EPS = 1e-09

        def _moe_forward(x3, Wg, W1, b1, W2, b2, Ws1, bs1, Ws2, bs2):
            b, s, h = x3.shape
            x = x3.reshape(-1, h)
            T = x.shape[0]
            logits = x @ Wg
            probs = jax.nn.softmax(logits, axis=-1)
            vals, idx = jax.lax.top_k(probs, TOP_K)
            weights = vals / (jnp.sum(vals, axis=-1, keepdims=True) + EPS)
            cw = jnp.zeros((T, E), dtype=x.dtype).at[jnp.arange(T)[:, None], idx].set(weights)
            hpre = jnp.einsum('th,ehf->tef', x, W1) + b1
            act = jax.nn.silu(hpre)
            y = jnp.einsum('tef,efh->teh', act, W2) + b2
            out = jnp.einsum('te,teh->th', cw, y)
            shared = jax.nn.silu(x @ Ws1 + bs1) @ Ws2 + bs2
            out = out + SHARED_SCALE * shared
            return out.reshape(b, s, h)
        return _moe_forward(hidden_states, Wg, W1, b1, W2, b2, Ws1, bs1, Ws2, bs2)

    def _L1_xattn_ref(x, context, W_ih, W_hh, b_ih, b_hh, Wq, Wout, b_out):
        import jax, jax.numpy as jnp
        import numpy as np
        B, T, Din = x.shape
        H = W_hh.shape[1]

        def attend(h):
            q = h @ Wq.T
            scores = jnp.einsum('bc,bsc->bs', q, context)
            alpha = jax.nn.softmax(scores, axis=-1)
            ctx = jnp.einsum('bs,bsc->bc', alpha, context)
            return jnp.tanh(jnp.concatenate([ctx, h], axis=-1) @ Wout.T + b_out)

        def step(carry, x_t):
            h, c, attn = carry
            inp = jnp.concatenate([x_t, attn], axis=-1)
            gates = inp @ W_ih.T + b_ih + h @ W_hh.T + b_hh
            i, f, g, o = jnp.split(gates, 4, axis=-1)
            c = jax.nn.sigmoid(f) * c + jax.nn.sigmoid(i) * jnp.tanh(g)
            h = jax.nn.sigmoid(o) * jnp.tanh(c)
            out = attn_out = attend(h)
            return ((h, c, attn_out), out)
        h0 = jnp.zeros((B, H), x.dtype)
        init = (h0, h0, h0)
        xs = jnp.swapaxes(x, 0, 1)
        _, outs = jax.lax.scan(step, init, xs)
        return jnp.swapaxes(outs, 0, 1)

    def _L1_attn_ref(x, in_proj_w, conv_w, conv_b, x_proj_w, dt_proj_w, dt_proj_b, A_log, D, out_proj_w, ln_w, ln_b):
        import jax, jax.numpy as jnp
        import numpy as np
        D_MODEL = 128
        N_LAYERS = 4
        D_STATE = 16
        D_CONV = 4
        EXPAND = 2
        D_INNER = EXPAND * D_MODEL
        DT_RANK = D_MODEL // 16
        B_SZ = 2
        SEQ = 128
        EPS = 1e-05

        def _layer_norm(x, w, b):
            m = x.mean(-1, keepdims=True)
            v = x.var(-1, keepdims=True)
            return (x - m) * jax.lax.rsqrt(v + EPS) * w + b

        def _mamba(x, in_w, cw, cb, xpw, dtw, dtb, A_log, Dp, ow):
            B, L, _ = x.shape
            xz = x @ in_w
            u, z = jnp.split(xz, 2, axis=-1)
            up = jnp.pad(u, ((0, 0), (D_CONV - 1, 0), (0, 0)))
            uc = cb + sum((up[:, k:k + L, :] * cw[:, k] for k in range(D_CONV)))
            u = jax.nn.silu(uc)
            proj = u @ xpw
            dt = proj[..., :DT_RANK]
            Bm = proj[..., DT_RANK:DT_RANK + D_STATE]
            Cm = proj[..., DT_RANK + D_STATE:]
            delta = jax.nn.softplus(dt @ dtw + dtb)
            A = -jnp.exp(A_log)

            def step(h, inp):
                d_t, b_t, c_t, u_t = inp
                dA = jnp.exp(d_t[..., None] * A)
                h = dA * h + (d_t * u_t)[..., None] * b_t[:, None, :]
                y = jnp.einsum('bdn,bn->bd', h, c_t)
                return (h, y)
            h0 = jnp.zeros((B, D_INNER, D_STATE), x.dtype)
            xs = (jnp.moveaxis(delta, 1, 0), jnp.moveaxis(Bm, 1, 0), jnp.moveaxis(Cm, 1, 0), jnp.moveaxis(u, 1, 0))
            _, ys = jax.lax.scan(step, h0, xs)
            y = jnp.moveaxis(ys, 0, 1) + u * Dp
            y = y * jax.nn.silu(z)
            return y @ ow
        for i in range(in_proj_w.shape[0]):
            y = _mamba(x, in_proj_w[i], conv_w[i], conv_b[i], x_proj_w[i], dt_proj_w[i], dt_proj_b[i], A_log[i], D[i], out_proj_w[i])
            x = _layer_norm(y + x, ln_w[i], ln_b[i])
        return x

    def _L1_ffn_ref(hidden_states, gate_W, gate_b, wi_W, wi_b, wo_W, wo_b, lora_A, lora_B):
        import jax, jax.numpy as jnp
        import numpy as np
        B, S, D, F, E, R = (4, 256, 128, 512, 8, 4)
        x = hidden_states
        logits = jnp.einsum('bsd,ed->bse', x, gate_W) + gate_b
        top1 = jnp.argmax(jax.nn.softmax(logits, axis=-1), axis=-1)
        base = jnp.einsum('bsd,fd->bsf', x, wi_W) + wi_b
        out = jnp.zeros_like(x)
        for i in range(lora_A.shape[0]):
            lora = jnp.einsum('bsr,fr->bsf', jnp.einsum('bsd,rd->bsr', x, lora_A[i]), lora_B[i])
            inter = jax.nn.relu(base + lora)
            expert_out = jnp.einsum('bsf,df->bsd', inter, wo_W) + wo_b
            mask = (top1 == i).astype(x.dtype)[..., None]
            out = out + mask * expert_out
        return out
    x = x + _L0_xattn_ref(_layernorm(x, axis=-1), ctx_1024, mask_BxS2_bk0, L0_xattn_Wq, L0_xattn_bq, L0_xattn_Wkv, L0_xattn_bkv, L0_xattn_qn_w, L0_xattn_qn_b, L0_xattn_kn_w, L0_xattn_kn_b, L0_xattn_Wo, L0_xattn_bo)
    x = x + _L0_attn_ref(_layernorm(x, axis=-1), L0_attn_qkv_w, L0_attn_qn_w, L0_attn_qn_b, L0_attn_kn_w, L0_attn_kn_b, L0_attn_sinks, L0_attn_proj_w, L0_attn_proj_b)
    x = x + _L0_ffn_ref(_layernorm(x, axis=-1), L0_ffn_Wg, L0_ffn_W1, L0_ffn_b1, L0_ffn_W2, L0_ffn_b2, L0_ffn_Ws1, L0_ffn_bs1, L0_ffn_Ws2, L0_ffn_bs2)
    x = x + _L1_xattn_ref(_layernorm(x, axis=-1), ctx_1024, L1_xattn_W_ih, L1_xattn_W_hh, L1_xattn_b_ih, L1_xattn_b_hh, L1_xattn_Wq, L1_xattn_Wout, L1_xattn_b_out)
    x = x + _L1_attn_ref(_layernorm(x, axis=-1), L1_attn_in_proj_w, L1_attn_conv_w, L1_attn_conv_b, L1_attn_x_proj_w, L1_attn_dt_proj_w, L1_attn_dt_proj_b, L1_attn_A_log, L1_attn_D, L1_attn_out_proj_w, L1_attn_ln_w, L1_attn_ln_b)
    x = x + _L1_ffn_ref(_layernorm(x, axis=-1), L1_ffn_gate_W, L1_ffn_gate_b, L1_ffn_wi_W, L1_ffn_wi_b, L1_ffn_wo_W, L1_ffn_wo_b, L1_ffn_lora_A, L1_ffn_lora_B)
    return x

_drawn_inputs = setup_inputs


def setup_inputs(seed=0):
    import zlib

    import numpy as np

    out = dict(_drawn_inputs(seed))
    spreads = {'L0_xattn_bq': (0.0, 0.8),
     'L0_xattn_bkv': (0.0, 0.354),
     'L0_xattn_qn_w': (1.0, 0.6),
     'L0_xattn_qn_b': (0.0, 0.8),
     'L0_xattn_kn_w': (1.0, 0.6),
     'L0_xattn_kn_b': (0.0, 0.8),
     'L0_xattn_bo': (0.0, 0.1),
     'L0_attn_qn_w': (1.0, 0.6),
     'L0_attn_qn_b': (0.0, 0.8),
     'L0_attn_kn_w': (1.0, 0.6),
     'L0_attn_kn_b': (0.0, 0.8),
     'L0_attn_proj_b': (0.0, 0.1),
     'L0_ffn_b1': (0.0, 0.491),
     'L0_ffn_b2': (0.0, 0.1),
     'L0_ffn_bs1': (0.0, 0.8),
     'L0_ffn_bs2': (0.0, 0.8),
     'L1_xattn_b_ih': (0.0, 0.731),
     'L1_xattn_b_hh': (0.0, 0.716),
     'L1_xattn_b_out': (0.0, 0.1),
     'L1_attn_conv_b': (0.0, 0.8),
     'L1_attn_D': (1.0, 0.6),
     'L1_attn_ln_w': (1.0, 0.2),
     'L1_attn_ln_b': (0.0, 0.1),
     'L1_ffn_gate_b': (0.0, 0.8),
     'L1_ffn_wi_b': (0.0, 0.1),
     'L1_ffn_wo_b': (0.0, 0.1)}
    factors = {'L0_xattn_Wq': 4.938,
     'L0_attn_sinks': 6.586,
     'L0_ffn_Ws1': 8.0,
     'L0_ffn_Ws2': 8.0,
     'L1_xattn_W_ih': 3.847,
     'L1_xattn_W_hh': 8.0,
     'L1_xattn_Wq': 5.75,
     'L1_attn_in_proj_w': 8.0,
     'L1_attn_conv_w': 8.0,
     'L1_attn_x_proj_w': 8.0,
     'L1_attn_dt_proj_w': 8.0,
     'L1_attn_dt_proj_b': 8.0,
     'L1_attn_A_log': 8.0,
     'L1_attn_out_proj_w': 8.0,
     'L1_ffn_gate_W': 4.729,
     'L1_ffn_lora_A': 4.426,
     'L1_ffn_lora_B': 4.294}
    for name, (base, spread) in spreads.items():
        noise = np.random.default_rng([zlib.crc32(name.encode()), seed]).standard_normal(out[name].shape)
        drawn = base * np.exp(spread * noise) if base else spread * noise
        out[name] = jnp.asarray(drawn.astype(out[name].dtype))
    for name, factor in factors.items():
        out[name] = (out[name] * factor).astype(out[name].dtype)
    return out
```

```python
from contextlib import ExitStack

import concourse.bass as bass
import numpy as np
from concourse import mybir

ALU = mybir.AluOpType
ACT = mybir.ActivationFunctionType
AX = mybir.AxisListType.X
F32 = mybir.dt.float32
BF16 = mybir.dt.bfloat16
U32 = mybir.dt.uint32
U8 = mybir.dt.uint8

P = 128
B, S, D = 8, 32, 128
SK = 512
TOK = B * S
NJ = TOK // P
BT = B // NJ
XH, XD = 16, 8
XG = 4
AH, AD = 16, 64
E, F = 8, 512
FC = F // P
ML, MI, MN, MR, MK = 4, 256, 16, 8, 4
MC = MI // P
LR = 4
KC = SK // P
MASKED = -1e30
FLOOR = -1e29

C_ID, C_CB8, C_BLK8, C_CB64, C_BLK64, C_ROT, C_COS, C_SIN, C_CAUSAL, C_HM, C_HM16, C_IOTA, C_NEG, C_SEL = np.cumsum(
    [0, P, P, P, P, P, P, S, S, S, 4, 16, 8, B * KC]).tolist()
C_END = C_SEL + 2 * MN

V_NAMES = [("bq", 1), ("bk", 1), ("bv", 1), ("qw", 1), ("qb", 1), ("kw", 1), ("kb", 1), ("aqw", 1), ("aqb", 1),
           ("akw", 1), ("akb", 1), ("sink", AH), ("b1", E * FC), ("bs1", FC), ("bih", 4), ("bhh", 4),
           ("bout", 1), ("convw", ML * MC * MK), ("convb", ML * MC), ("dtb", ML * MC), ("mD", ML * MC),
           ("alog", ML * MC * MN), ("wib", FC)]
V_AT = dict(zip([n for n, _ in V_NAMES], np.cumsum([0] + [w for _, w in V_NAMES]).tolist()))
V_END = sum(w for _, w in V_NAMES)

R_NAMES = [("bo", D), ("projb", D), ("bs2", D), ("wob", D), ("gateb", E), ("lnw", ML * D), ("lnb", ML * D)]
R_AT = dict(zip([n for n, _ in R_NAMES], np.cumsum([0] + [w for _, w in R_NAMES]).tolist()))
R_END = sum(w for _, w in R_NAMES)


def shape_constants():
    p = np.arange(P)
    c = np.zeros((P, C_END), np.float32)
    c[:, C_ID:C_ID + P] = np.eye(P)
    for size, centre, mean in ((XD, C_CB8, C_BLK8), (AD, C_CB64, C_BLK64)):
        same = (p[:, None] // size == p[None, :] // size) / size
        c[:, mean:mean + P] = same
        c[:, centre:centre + P] = np.eye(P) - same
    half = AD // 2
    for m in range(P):
        k = m + half if m % AD < half else m - half
        c[k, C_ROT + m] = -1.0 if m % AD < half else 1.0
    freq = (1.0 / np.float32(10000.0) ** (np.arange(0, AD, 2, dtype=np.float32) / AD)).astype(np.float32)
    angle = np.arange(S, dtype=np.float32)[None, :] * freq[(p % half)][:, None]
    c[:, C_COS:C_COS + S] = np.cos(angle)
    c[:, C_SIN:C_SIN + S] = np.sin(angle)
    c[:, C_CAUSAL:C_CAUSAL + S] = np.where(np.arange(S)[None, :] <= (p % S)[:, None], 0.0, MASKED)
    c[:, C_HM:C_HM + 4] = (p[:, None] % 32) // XD == np.arange(4)[None, :]
    c[:, C_HM16:C_HM16 + 16] = (p[:, None] // XD == np.arange(16)[None, :]) * np.float32(XD ** -0.5)
    c[:, C_IOTA:C_IOTA + 8] = np.arange(8)[None, :]
    c[:, C_NEG:C_NEG + B * KC] = -1.0 * (p[:, None] == np.arange(B * KC)[None, :] // KC)
    c[:, C_SEL:C_SEL + 2 * MN] = (p[:, None] % 32 == np.arange(32)[None, :]) * (p[:, None] < 96)
    return c


LOG1P = [2.000000007681758, 0.6666632164140144, 0.40024595229818943, 0.2796515775679465, 0.28157778313522575]

def pat(t, dims, off=0):
    return bass.AP(tensor=t.tensor, offset=t.offset + off, ap=[list(t.ap[0])] + [list(d) for d in dims])


class Steps:

    def __init__(self, eng, sem):
        self.eng, self.sem, self.n, self.base = eng, sem, 0, 0

    def __call__(self, ins):
        self.mark(ins)
        self.sync()

    def mark(self, ins):
        ins.then_inc(self.sem, 1)
        self.n += 1

    def sync(self):
        self.eng.wait_ge(self.sem, self.base + self.n)


def build(nc, arr, out, upto=99):
    with ExitStack() as ctx:
        def sb(name, shape, dt=F32):
            return ctx.enter_context(nc.sbuf_tensor(name, shape, dt))

        sem = {}

        def sems(*names):
            for n in names:
                sem[n] = ctx.enter_context(nc.semaphore(n))

        cst = sb("cst", [P, C_END])
        vec = sb("vec", [P, V_END])
        rows = sb("rows", [P, R_END])
        wx = sb("wx", [P, 4 * D])
        ident = cst[:, C_ID:C_ID + P]

        def v(name, i=0, n=1):
            return vec[:, V_AT[name] + i:V_AT[name] + i + n]

        def r(name, i=0, n=D):
            return rows[:, R_AT[name] + i:R_AT[name] + i + n]

        wqkv = sb("wqkv", [P, 3 * AH * AD])
        projT = sb("projT", [P, AH * AD])
        w1 = sb("w1", [P, E * F])
        w2 = sb("w2", [P, E * F])
        ws = sb("ws", [P, 2 * F])
        wg = sb("wg", [P, E])
        b2 = sb("b2", [E, D])
        x_in = sb("x_in", [P, NJ, D])
        xres = sb("xres", [P, NJ, D])
        xbias = sb("xbias", [P, NJ, D])
        xn = sb("xn", [P, NJ, D])
        xnT = sb("xnT", [P, TOK])
        bn = sb("bn", [P, NJ, 6])
        mv = sb("mv", [P, NJ, 2])
        lnv = sb("lnv", [P, NJ])
        rs = sb("rs", [P, NJ])

        ctxT = sb("ctxT", [P, B * SK])
        kT = sb("kT", [P, B * SK])
        vx = sb("vx", [P, B * KC, D])
        qblk = sb("qblk", [P, XG, B, 4, S])
        T = sb("T", [P, 16, 512])
        maskb = sb("maskb", [P, B * SK], BF16)
        mask8 = T[:, 12:14, :].rearrange("p n k -> p (n k)").bitcast(U8)
        xw = sb("xw", [P, 2 * D + 2])
        oT = sb("oT", [P, TOK])
        xmax = sb("xmax", [P, B * XG])
        xneg = sb("xneg", [P, B * XG])
        xz = sb("xz", [P, B * XG])
        xrz = sb("xrz", [P, B * XG])

        eps5 = sb("eps5", [P, 1])
        eps6 = sb("eps6", [P, 1])
        wmean = sb("wmean", [P, 2 * AH])
        am = sb("am", [P, NJ, AH])
        asink = sb("asink", [P, NJ, AH])
        az = sb("az", [P, NJ, AH])
        lg = sb("lg", [P, NJ, E])
        gm = sb("gm", [P, NJ])
        gz = sb("gz", [P, NJ])
        m8 = sb("m8", [P, NJ, E])
        i8 = sb("i8", [P, NJ, E], U32)
        i8f = sb("i8f", [P, NJ, E])
        gw = sb("gw", [P, NJ, 2])
        cw = sb("cw", [P, 3, NJ, E])
        cwT = sb("cwT", [E * LR, TOK])
        facc = sb("facc", [P, NJ, D])
        avals = vx[:, :, :].rearrange("p n d -> p (n d)")[:, 0:NJ * AH * AD].rearrange("p (j n) -> p j n", j=NJ)
        aprobT = bass.AP(tensor=qblk[:, 0, 0, 0, 0:1].tensor, offset=0, ap=[[XG * B * 4 * S, P], [AH * P, NJ], [P, AH], [1, P]])
        lw = sb("lw", [P, 3 * 4 * D + 3 * D])
        bf = [t.bitcast(BF16) for t in (kT[:, :], qblk[:, :, :, :, :].rearrange("p a b c d -> p (a b c d)"),
                                        vx[:, :, :].rearrange("p n d -> p (n d)"))]
        half_b = B * SK
        ks = [bf[0][:, 0:half_b], bf[0][:, half_b:2 * half_b], maskb[:, :]]
        vs = [bf[1][:, 0:half_b], bf[1][:, half_b:2 * half_b], bf[2][:, 0:half_b]]
        lsp = sb("lsp", [P, 3, 9 * D], BF16)
        gbias = sb("gbias", [P, 4])
        gx = sb("gx", [P, S + 1, 4, B])
        yT = sb("yT", [P, B, S])
        ones = sb("ones", [P, P], BF16)
        hsp = sb("hsp", [P, 3, B], BF16)
        asp = sb("asp", [P, 3, B], BF16)
        esp = sb("esp", [P, 3, B * KC], BF16)
        negmax = sb("negmax", [P, B * KC], BF16)
        (h32, a32, c2, tanhc, fc2, ig, hrest, arest, mc, zs, rz, oh, opre) = [
            sb(n, [P, B]) for n in ("h32", "a32", "c2", "tanhc", "fc2", "ig", "hrest", "arest", "mc", "zs", "rz",
                                    "oh", "opre")]
        m1 = sb("m1", [B, 1])
        (gsum, gact, ssum, e32, erest) = [sb(n, [P, B * KC]) for n in ("gsum", "gact", "ssum", "e32", "erest")]
        MNP = MN // 2
        mw = w1[:, 0:ML * (2 * MI + MC * (6 * MN + MR) + MC * D)]
        m_in = mw[:, 0:ML * 2 * MI]
        m_x = mw[:, ML * 2 * MI:ML * 2 * MI + ML * MC * (6 * MN + MR)]
        m_out = mw[:, ML * 2 * MI + ML * MC * (6 * MN + MR):]
        dtw = projT[0:MR, 0:ML * MI]
        decay = [ctxT[:, :], kT[:, :]]
        state = [qblk[:, :, :, :, :].rearrange("p a b c d -> p (a b c d)"), vx[:, :, :].rearrange("p n d -> p (n d)")]
        up = sb("up", [P, MC, B, S + MK - 1])
        aneg = sb("aneg", [P, ML * MC * MN])
        bcs = sb("bcs", [6 * MN, TOK], BF16)
        sel = sb("sel", [6 * MN, 2 * MN], BF16)
        dts = sb("dts", [MR, TOK])
        two = sb("two", [P, 1])
        fw = wqkv[:, 0:E + E * LR + F + FC * D]
        lb = wqkv[0:E * LR, 2048:2048 + F]
        oneh = sb("oneh", [P, NJ, E])
        loraa = sb("loraa", [P, NJ, E * LR])
        bank = [ctx.enter_context(nc.psum_tensor(f"bank{i}", [P, 512], F32)) for i in range(8)]

        sems("d_par", "d_rows", "d_x", "d_mask", "d_out",
             "pe_step", "act_step", "dve_step", "pool_step",
             "ln_var", "ln_rstd", "ln_xn", "ln_tr", "ln_xT",
             "xw_ps", "xw_sb", "k_proj", "k_sq", "k_var", "k_rstd", "k_hat", "k_done", "v_proj", "v_evac",
             "eps_ready", "mask_ready", "qblk_ready", "x_score", "x_max", "x_exp", "x_norm", "x_tr", "x_pt", "x_pv",
             "x_oT", "x_o", "xb_ready", "x_res")
        d_ctx = [ctx.enter_context(nc.semaphore(f"d_ctx{b}")) for b in range(B)]

        sems("d_attn", "d_ffn", 
             "a_wmean", "a_wc", "a_proj", "a_sq", "a_var", "a_rstd", "a_z0", "a_z", "a_rot", "a_t2", "a_rope",
             "a_vproj", "a_vev", "a_score", "a_sub", "a_exp", "a_zero", "a_pt", "a_pv", "a_oT", "a_oTd", "a_o",
             "f_gate", "f_sub", "f_exp", "f_cw", "f_cwps", "f_cwT", "f_h", "f_act", "f_y", "f_acc", "f_b2")
        sems("d_lw", "l_w", "l_kv", "l_hi", "l_rest", "l_split", "l_gbias", "l_gxps", "l_gx", "l_zero",
             "g_ps", "g_sum", "g_act", "c_new", "c_tanh", "h_hi", "h_mid", "h_lo", "s_hi", "m_c", "m_t", "m_d", "s_ps",
             "s_sum", "e_hi", "e_32", "e_mid", "e_lo", "oh_ps", "z_ps", "v_ps", "o_pre", "at_hi", "at_32", "at_mid",
             "at_lo", "y_st", "y_tr")
        sems("d_late", "m_const", "m_uz", "m_up", "m_zs", "m_conv", "m_convp", "m_us", "m_bc",
             "m_dts", "m_bcs", "m_dps", "m_e", "m_delta", "m_bps", "m_cps", "m_bsb", "m_csb", "m_dA", "m_dbu0",
             "m_dbu1", "m_scan0", "m_scan1", "m_hc0", "m_hc1", "m_y", "m_ys", "m_o",
             "r_gate", "r_a", "r_am", "r_amps", "r_amT", "r_h", "r_act", "r_o")
        N_OUT = 6
        LSTM_STEPS = 12
        block = ctx.enter_context(nc.Block())

        def both(t):
            return t.rearrange("p (n k) -> p n k", n=2)

        def pairs(t, i):
            return both(t[:, i * 2 * TOK:(i + 1) * 2 * TOK])

        def over_pair(t):
            return pat(t, [[0, 2], [1, TOK]])

        def conv(eng, step, l, ch):
            acc = T[:, 0, ch * TOK:(ch + 1) * TOK].rearrange("p (b t) -> p b t", b=B)
            at = (l * MC + ch) * MK
            eng.wait_ge(sem["m_up"], l + 1)
            step(eng.tensor_scalar(acc, up[:, ch, :, 0:S], v("convw", at), v("convb", l * MC + ch), ALU.mult, ALU.add))
            for k in range(1, MK):
                if ch == 0:
                    ins = eng.scalar_tensor_tensor(out=acc, in0=up[:, ch, :, k:k + S], scalar=v("convw", at + k), in1=acc,
                                                   op0=ALU.mult, op1=ALU.add)
                else:
                    tap = T[:, 14, TOK:2 * TOK].rearrange("p (b t) -> p b t", b=B)
                    step(eng.tensor_scalar(tap, up[:, ch, :, k:k + S], v("convw", at + k), 0.0, ALU.mult, ALU.add))
                    ins = eng.tensor_tensor(acc, acc, tap, ALU.add)
                if k < MK - 1:
                    step(ins)
            return ins

        @block.sync
        def _(sp):
            sp.dma_start(x_in[:, :, :], arr["x"].rearrange("(j p) d -> p j d", p=P)).then_inc(sem["d_x"], 16)
            sp.dma_start(cst[:, :], arr["cst"]).then_inc(sem["d_par"], 16)
            sp.dma_start(wx[:, :], arr["wx"]).then_inc(sem["d_par"], 16)
            for b in range(B):
                sp.dma_start(ctxT[:, b * SK:(b + 1) * SK], arr["ctxT"][:, b * SK:(b + 1) * SK]) \
                  .then_inc(d_ctx[b], 16)
            sp.dma_start(wg[:, :], arr["wg"]).then_inc(sem["d_ffn"], 16)
            sp.dma_start(b2[:, :], arr["b2"]).then_inc(sem["d_ffn"], 16)
            sp.dma_start(ws[:, :], arr["ws"]).then_inc(sem["d_ffn"], 16)
            sp.dma_start(w1[:, :], arr["w1"]).then_inc(sem["d_ffn"], 16)
            sp.dma_start(w2[:, :], arr["w2"]).then_inc(sem["d_ffn"], 16)
            sp.dma_start(lw[:, :], arr["lw"]).then_inc(sem["d_lw"], 16)
            sp.wait_ge(sem["a_o"], 1)
            sp.dma_start(dtw, arr["dtw"]).then_inc(sem["d_late"], 16)
            sp.dma_start(fw, arr["fw"]).then_inc(sem["d_late"], 16)
            sp.dma_start(lb, arr["lb"]).then_inc(sem["d_late"], 16)
            sp.wait_ge(sem["f_y"], E + 1)
            sp.dma_start(mw, arr["mw"]).then_inc(sem["d_late"], 16)
            sp.wait_ge(sem["x_res"], N_OUT)
            sp.dma_start(out.rearrange("(j p) d -> p j d", p=P), xres[:, :, :]).then_inc(sem["d_out"], 16)
            sp.wait_ge(sem["d_out"], 16)

        @block.gpsimd
        def _(pool):
            step = Steps(pool, sem["pool_step"])
            pool.wait_ge(sem["d_mask"], 16)
            pool.tensor_scalar(maskb[:, :], mask8[:, :], -MASKED, MASKED, ALU.mult, ALU.add) \
                .then_inc(sem["mask_ready"], 1)
            pool.wait_ge(sem["d_par"], 48)
            for s in range(1 + B):
                pool.wait_ge(sem["k_hat"], s + 1)
                if s == 0:
                    ins = pool.tensor_scalar(T[:, 10, 0:TOK], T[:, 8, 0:TOK], 1.0, v("qb"), ALU.mult, ALU.add)
                else:
                    ins = pool.tensor_scalar(kT[:, (s - 1) * SK:s * SK], T[:, 8 + s % 2, :], 1.0, v("kb"),
                                             ALU.mult, ALU.add)
                ins.then_inc(sem["k_done"], 1)
            pool.wait_ge(sem["d_rows"], 16)
            pool.wait_ge(sem["d_x"], 16)
            pool.tensor_tensor(xbias[:, :, :], x_in[:, :, :], pat(r("bo"), [[0, NJ], [1, D]]), ALU.add) \
                .then_inc(sem["xb_ready"], 1)

            pool.wait_ge(sem["x_res"], 1)
            pool.tensor_tensor(xbias[:, :, :], xres[:, :, :], pat(r("projb"), [[0, NJ], [1, D]]), ALU.add) \
                .then_inc(sem["xb_ready"], 1)
            pool.wait_ge(sem["a_wmean"], 1)
            wqk = wqkv[:, 0:2 * AH * AD].rearrange("p (h d) -> p h d", d=AD)
            pool.tensor_tensor(wqk, wqk, pat(wmean[:, :], [[1, 2 * AH], [0, AD]]), ALU.subtract) \
                .then_inc(sem["a_wc"], 1)
            pool.memset(qblk[:, :, :, :, :], 0.0).then_inc(sem["a_zero"], 1)
            for m in range(8):
                pool.wait_ge(sem["a_z0"], m + 1)
                if m >= 2:
                    pool.wait_ge(sem["a_t2"], m - 1)
                pool.tensor_scalar(T[:, 8 + m % 2, :], T[:, 6 + m % 2, :], 1.0, v("aqb" if m < 4 else "akb"),
                                   ALU.mult, ALU.add).then_inc(sem["a_z"], 1)

            pool.wait_ge(sem["x_res"], 2)
            step(pool.tensor_scalar(T[:, 15, 0:D], r("bs2"), 0.1, 0.0, ALU.mult, ALU.add))
            pool.tensor_tensor(facc[:, :, :], xres[:, :, :], pat(T[:, 15, :], [[0, NJ], [1, D]]), ALU.add) \
                .then_inc(sem["xb_ready"], 1)

            pool.wait_ge(sem["d_lw"], 16)
            pool.tensor_scalar(lw[:, 8 * D:13 * D], lw[:, 8 * D:13 * D], 0.5, 0.0, ALU.mult, ALU.add) \
                .then_inc(sem["l_w"], 1)
            pool.memset(gx[:, S, :, :], 0.0).then_inc(sem["l_zero"], 1)
            for i in range(2 * B + 1):
                if i < 2 * B:
                    b = i // 2
                    parts = [t[:, b * SK:(b + 1) * SK] for t in (vs if i % 2 else ks)]
                    rest = T[:, 8 + i % 2, :]
                else:
                    parts = [lsp[:, k, :] for k in range(3)]
                    rest = T[:, 10:13, :].rearrange("p n d -> p (n d)")[:, 0:9 * D]
                pool.wait_ge(sem["l_rest"], i + 1)
                step(pool.tensor_scalar(parts[1], rest, 1.0, 0.0, ALU.mult, ALU.add))
                pool.tensor_tensor(parts[2], rest, parts[1], ALU.subtract).then_inc(sem["l_split"], 1)

            pool.wait_ge(sem["x_res"], 4)
            for ch in range(MC):
                pool.memset(decay[ch].rearrange("p (n s) -> p n s", s=S)[:, :, 0], 0.0).then_inc(sem["m_const"], 1)
            for l in range(ML):
                conv(pool, step, l, 1).then_inc(sem["m_convp"], 1)
                pool.wait_ge(sem["m_delta"], l + 1)
                for i in range(MNP + 1):
                    if i < MNP:
                        if l:
                            pool.wait_ge(sem["m_y"], l)
                        pool.wait_ge(sem["m_bsb"], l * MNP + i + 1)
                        pool.tensor_tensor(pairs(state[1], i), over_pair(T[:, 7, TOK:2 * TOK]), both(T[:, 8 + i % 2, :]),
                                           ALU.mult).then_inc(sem["m_dbu1"], 1)
                    if i >= 1:
                        pool.wait_ge(sem["m_csb"], l * MNP + i)
                        pool.wait_ge(sem["m_scan1"], l * MNP + i)
                        pool.tensor_tensor(pairs(state[1], i - 1), pairs(state[1], i - 1), both(T[:, 10 + (i - 1) % 2, :]),
                                           ALU.mult).then_inc(sem["m_hc1"], 1)

        @block.scalar
        def _(act):
            step = Steps(act, sem["act_step"])
            act.dma_start(vec[:, :], arr["vec"]).then_inc(sem["d_par"], 16)
            act.dma_start(mask8[:, :], bass.AP(tensor=arr["mask"].tensor, offset=0, ap=[[0, P], [1, B * SK]])) \
               .then_inc(sem["d_mask"], 16)
            act.dma_start(rows[:, :], arr["rows"]).then_inc(sem["d_rows"], 16)
            act.dma_start(wqkv[:, :], arr["qkvT"]).then_inc(sem["d_attn"], 16)
            act.dma_start(projT[:, :], arr["projT"]).then_inc(sem["d_attn"], 16)

            def ln_rstd(n):
                act.wait_ge(sem["ln_var"], n + 1)
                step(act.activation(lnv[:, :], mv[:, :, 1], ACT.Ln, bias=eps5[:, :]))
                act.activation(rs[:, :], lnv[:, :], ACT.Exp, scale=-0.5).then_inc(sem["ln_rstd"], 1)

            act.preload_act_table_set("natural_log_exp_and_others")
            act.wait_ge(sem["eps_ready"], 2)
            act.wait_ge(sem["d_par"], 48)
            ln_rstd(0)

            def k_square(s):
                w, p = (TOK if s == 0 else SK), s % 2
                act.wait_ge(sem["k_proj"], s + 1)
                if s == 0:
                    act.wait_ge(sem["xw_sb"], 1)
                if s >= 2:
                    act.wait_ge(sem["k_hat"], s - 1)
                bias = xw[:, 2 * D:2 * D + 1] if s == 0 else xw[:, 2 * D + 1:2 * D + 2]
                act.activation(T[:, p, 0:w], bank[p][:, 0:w], ACT.Identity, bias=bias)
                act.activation(T[:, 2 + p, 0:w], bank[p][:, 0:w], ACT.Square, bias=bias).then_inc(sem["k_sq"], 1)

            def k_rstd(s):
                w, p = (TOK if s == 0 else SK), s % 2
                act.wait_ge(sem["k_var"], s + 1)
                step(act.activation(T[:, 4 + p, 0:w], bank[2 + p][:, 0:w], ACT.Ln, bias=eps6[:, :]))
                act.activation(T[:, 6 + p, 0:w], T[:, 4 + p, 0:w], ACT.Exp, scale=-0.5).then_inc(sem["k_rstd"], 1)

            for s in range(2 + B):
                if s <= B:
                    k_square(s)
                if s >= 1:
                    k_rstd(s - 1)

            def x_exp(i):
                act.wait_ge(sem["x_max"], i + 1)
                if i >= 2:
                    act.wait_ge(sem["x_norm"], i - 1)
                act.activation(T[:, 2 + i % 2, :], T[:, i % 2, :], ACT.Exp, bias=xneg[:, i:i + 1],
                               accum_out=xz[:, i:i + 1]).then_inc(sem["x_exp"], 1)

            def x_copy_pt(i):
                act.wait_ge(sem["x_tr"], i + 1)
                if i >= 2:
                    act.wait_ge(sem["x_pv"], i - 1)
                act.activation(T[:, 6 + i % 2, :], bank[2 + i % 2][:, :], ACT.Copy).then_inc(sem["x_pt"], 1)

            for i in range(B * XG + 2):
                if i < B * XG:
                    x_exp(i)
                if i >= 2:
                    x_copy_pt(i - 2)

            ln_rstd(1)

            def a_square(m):
                act.wait_ge(sem["a_proj"], m + 1)
                if m >= 2:
                    act.wait_ge(sem["a_var"], m - 1)
                act.activation(T[:, m % 2, :], bank[m % 2][:, :], ACT.Square).then_inc(sem["a_sq"], 1)

            def a_rstd(m):
                act.wait_ge(sem["a_var"], m + 1)
                step(act.activation(T[:, 2 + m % 2, :], bank[2 + m % 2][:, :], ACT.Ln, bias=eps5[:, :]))
                if m >= 2:
                    act.wait_ge(sem["a_z0"], m - 1)
                act.activation(T[:, 4 + m % 2, :], T[:, 2 + m % 2, :], ACT.Exp, scale=-0.5).then_inc(sem["a_rstd"], 1)

            def a_vev(n):
                act.wait_ge(sem["a_vproj"], n + 1)
                act.activation(avals[:, n // 2, (n % 2) * 512:(n % 2) * 512 + 512], bank[6][:, :], ACT.Copy) \
                   .then_inc(sem["a_vev"], 1)

            for m in range(9):
                if m < 8:
                    a_square(m)
                if m >= 1:
                    a_rstd(m - 1)
                if m >= 5:
                    a_vev(m - 5)
            for j in range(NJ):
                act.wait_ge(sem["a_sub"], j + 1)
                act.activation(T[:, 4 + j, :], T[:, 2 + j, :], ACT.Exp)
                act.activation(asink[:, j, :], asink[:, j, :], ACT.Exp).then_inc(sem["a_exp"], 1)
            for j in range(NJ):
                act.wait_ge(sem["a_pv"], j + 1)
                act.activation(T[:, 8 + 2 * j, :], bank[2 + 2 * j][:, :], ACT.Copy).then_inc(sem["a_oT"], 1)

            def l_high(i):
                act.wait_ge(sem["l_kv"], i + 1)
                at = i // 2 * SK
                act.activation((vs if i % 2 else ks)[0][:, at:at + SK], bank[6 + i % 2][:, :], ACT.Copy) \
                   .then_inc(sem["l_hi"], 1)

            ln_rstd(2)
            act.wait_ge(sem["f_sub"], 1)
            act.activation(lg[:, :, :], lg[:, :, :], ACT.Exp).then_inc(sem["f_exp"], 1)
            act.preload_act_table_set("silu_and_others")
            for e in range(E + 1):
                for q in range(2):
                    act.wait_ge(sem["f_h"], 2 * e + q + 1)
                    if e >= 2:
                        act.wait_ge(sem["f_y"], e - 1)
                    for fc in (2 * q, 2 * q + 1):
                        half = slice((fc % 2) * TOK, (fc % 2) * TOK + TOK)
                        bias = v("b1", e * FC + fc) if e < E else v("bs1", fc)
                        ins = act.activation(T[:, 2 * (e % 2) + q, half], bank[2 * (e % 2) + q][:, half], ACT.Silu,
                                             bias=bias)
                    ins.then_inc(sem["f_act"], 1)
                if e >= 2:
                    l_high(2 * (e - 2))
                    l_high(2 * (e - 2) + 1)
            l_high(2 * B - 2)
            l_high(2 * B - 1)
            act.wait_ge(sem["l_w"], 1)
            act.activation(lsp[:, 0, :], lw[:, 4 * D:13 * D], ACT.Copy).then_inc(sem["l_hi"], 1)
            act.preload_act_table_set("natural_log_exp_and_others")

            ln_rstd(3)
            act.wait_ge(sem["l_gbias"], 1)
            act.wait_ge(sem["l_gxps"], 1)
            for g in range(4):
                ins = act.activation(pat(gx[:, 0, g, :], [[1, B], [4 * B, S]]),
                                     bank[g // 2][:, (g % 2) * TOK:(g % 2 + 1) * TOK].rearrange("p (b t) -> p b t", b=B),
                                     ACT.Identity, bias=gbias[:, g:g + 1])
            ins.then_inc(sem["l_gx"], 1)
            act.preload_act_table_set("exp_and_others")
            with act.Fori(0, S) as t:
                act.wait_ge(sem["g_sum"], t + 1)
                act.activation(gact[:, 0:3 * B], gsum[:, 0:3 * B], ACT.Tanh, scale=0.5)
                act.activation(gact[:, 3 * B:4 * B], gsum[:, 3 * B:4 * B], ACT.Tanh).then_inc(sem["g_act"], 1)
                act.wait_ge(sem["c_new"], t + 1)
                act.activation(tanhc[:, :], c2[:, :], ACT.Tanh, scale=0.5).then_inc(sem["c_tanh"], 1)
                act.wait_ge(sem["s_sum"], t + 1)
                act.activation(esp[:, 0, :], ssum[:, :], ACT.Exp, scale=0.5).then_inc(sem["e_hi"], 1)
                act.activation(e32[:, :], ssum[:, :], ACT.Exp, scale=0.5).then_inc(sem["e_32"], 1)
                act.wait_ge(sem["o_pre"], t + 1)
                act.activation(asp[:, 0, :], opre[:, :], ACT.Tanh, bias=v("bout")).then_inc(sem["at_hi"], 1)
                act.activation(a32[:, :], opre[:, :], ACT.Tanh, bias=v("bout")).then_inc(sem["at_32"], 1)
                act.activation(yT[:, :, bass.ds(t, 1)].rearrange("p b t -> p (b t)"), opre[:, :], ACT.Tanh, bias=v("bout")).then_inc(sem["y_st"], 1)

            act.preload_act_table_set("natural_log_exp_and_others")
            ln_rstd(4)
            step(act.activation(aneg[:, :], v("alog", 0, ML * MC * MN), ACT.Exp))
            step(act.activation(aneg[:, :], aneg[:, :], ACT.Copy, scale=-1.0))
            for l in range(ML):
                act.preload_act_table_set("silu_and_others")
                act.wait_ge(sem["m_uz"], l + 1)
                act.wait_ge(sem["m_const"], MC + 3)
                act.activation(up[:, :, :, MK - 1:], bank[0][:, :].rearrange("p (c b t) -> p c b t", c=MC, b=B), ACT.Copy) \
                   .then_inc(sem["m_up"], 1)
                act.activation(T[:, 2, :], bank[1][:, :], ACT.Silu).then_inc(sem["m_zs"], 1)
                act.wait_ge(sem["m_conv"], l + 1)
                act.wait_ge(sem["m_convp"], l + 1)
                act.activation(T[:, 1, :], T[:, 0, :], ACT.Silu).then_inc(sem["m_us"], 1)
                act.preload_act_table_set("natural_log_exp_and_others")
                act.wait_ge(sem["m_dps"], l + 1)
                for ch in range(MC):
                    half = slice(ch * TOK, (ch + 1) * TOK)
                    step.mark(act.activation(T[:, 3, half], bank[4][:, half], ACT.Abs, bias=v("dtb", l * MC + ch)))
                    step.mark(act.activation(T[:, 12, half], bank[4][:, half], ACT.Relu, bias=v("dtb", l * MC + ch)))
                step.sync()
                step(act.activation(T[:, 4, :], T[:, 3, :], ACT.Exp, scale=-1.0))
                step(act.activation(T[:, 5, :], T[:, 4, :], ACT.Ln, bias=two[:, :]))
                act.activation(T[:, 5, :], T[:, 5, :], ACT.Exp, scale=-1.0).then_inc(sem["m_e"], 1)
                act.wait_ge(sem["m_delta"], l + 1)
                for i in range(MNP):
                    n = l * MNP + i
                    act.wait_ge(sem["m_bps"], n + 1)
                    if n >= 2:
                        act.wait_ge(sem["m_dbu0"], n - 1)
                        act.wait_ge(sem["m_dbu1"], n - 1)
                    act.activation(T[:, 8 + i % 2, :], bank[2 + i % 2][:, :], ACT.Copy).then_inc(sem["m_bsb"], 1)
                    for ch in range(MC):
                        for k in range(2):
                            at = (l * MC + ch) * MN + 2 * i + k
                            seqs = decay[ch][:, (2 * i + k) * TOK:(2 * i + k + 1) * TOK].rearrange("p (b t) -> p b t", b=B)
                            ins = act.activation(seqs[:, :, 1:], T[:, 6, ch * TOK:(ch + 1) * TOK]
                                                 .rearrange("p (b t) -> p b t", b=B)[:, :, 1:],
                                                 ACT.Exp, scale=aneg[:, at:at + 1])
                        ins.then_inc(sem["m_dA"], 1)
                    act.wait_ge(sem["m_cps"], n + 1)
                    if n >= 2:
                        act.wait_ge(sem["m_hc0"], n - 1)
                        act.wait_ge(sem["m_hc1"], n - 1)
                    act.activation(T[:, 10 + i % 2, :], bank[5 + i % 2][:, :], ACT.Copy).then_inc(sem["m_csb"], 1)
                ln_rstd(5 + l)

            ln_rstd(5 + ML)
            act.wait_ge(sem["f_sub"], 2)
            act.activation(lg[:, :, :], lg[:, :, :], ACT.Exp).then_inc(sem["f_exp"], 1)
            for fc in range(FC):
                half = slice((fc % 2) * TOK, (fc % 2) * TOK + TOK)
                act.wait_ge(sem["r_h"], fc + 1)
                act.activation(T[:, fc // 2, half], bank[fc][:, 0:TOK], ACT.Relu, bias=v("wib", fc)) \
                   .then_inc(sem["r_act"], 1)

        @block.vector
        def _(dve):
            step = Steps(dve, sem["dve_step"])
            dve.memset(eps5[:, :], 1e-5).then_inc(sem["eps_ready"], 1)
            dve.memset(eps6[:, :], 1e-6).then_inc(sem["eps_ready"], 1)

            def layernorm(n, src, affine=None):
                for j in range(NJ):
                    step.mark(dve.bn_stats(bn[:, j, :], src[:, j, :]))
                step.sync()
                for j in range(NJ):
                    ins = dve.bn_aggr(mv[:, j, :], bn[:, j, :])
                    if j < NJ - 1:
                        step.mark(ins)
                ins.then_inc(sem["ln_var"], 1)
                dve.wait_ge(sem["ln_rstd"], n + 1)
                step.sync()
                for j in range(NJ):
                    ins = dve.tensor_scalar(xn[:, j, :], src[:, j, :], mv[:, j, 0:1], rs[:, j:j + 1],
                                            ALU.subtract, ALU.mult)
                    if affine is not None:
                        step.mark(ins)
                if affine is not None:
                    step.sync()
                    step(dve.tensor_tensor(xn[:, :, :], xn[:, :, :], pat(r("lnw", affine * D), [[0, NJ], [1, D]]), ALU.mult))
                    ins = dve.tensor_tensor(xn[:, :, :], xn[:, :, :], pat(r("lnb", affine * D), [[0, NJ], [1, D]]), ALU.add)
                ins.then_inc(sem["ln_xn"], 1)
                dve.wait_ge(sem["ln_tr"], n + 1)
                dve.tensor_copy(xnT[:, :], bank[7][:, 0:TOK]).then_inc(sem["ln_xT"], 1)

            step(dve.memset(qblk[:, :, :, :, :], 0.0))
            dve.wait_ge(sem["d_x"], 16)
            layernorm(0, x_in)
            dve.wait_ge(sem["xw_ps"], 1)
            dve.tensor_copy(xw[:, :], bank[6][:, 0:2 * D + 2]).then_inc(sem["xw_sb"], 1)
            dve.wait_ge(sem["d_par"], 48)

            def k_hat(s):
                w, p = (TOK if s == 0 else SK), s % 2
                dve.wait_ge(sem["k_rstd"], s + 1)
                if s >= 2:
                    dve.wait_ge(sem["k_done"], s - 1)
                dve.scalar_tensor_tensor(out=T[:, 8 + p, 0:w], in0=T[:, p, 0:w], scalar=v("qw" if s == 0 else "kw"),
                                         in1=T[:, 6 + p, 0:w], op0=ALU.mult, op1=ALU.mult) \
                   .then_inc(sem["k_hat"], 1)

            def v_evac(b):
                dve.wait_ge(sem["v_proj"], b + 1)
                dve.tensor_copy(pat(vx[:, b * KC, :], [[1, SK]]), bank[4 + b % 2][:, :]).then_inc(sem["v_evac"], 1)

            def q_blocks():
                dve.wait_ge(sem["k_done"], 1)
                for h in range(XH):
                    ins = dve.tensor_scalar(qblk[:, h // 4, :, h % 4, :], T[:, 10, 0:TOK].rearrange("p (b s) -> p b s", b=B),
                                            cst[:, C_HM16 + h:C_HM16 + h + 1], None, ALU.mult)
                ins.then_inc(sem["qblk_ready"], 1)

            for s in range(1 + B):
                k_hat(s)
                if s == 1:
                    q_blocks()
                if s >= 1:
                    v_evac(s - 1)

            def x_max(i):
                b = i // XG
                if i == 0:
                    dve.wait_ge(sem["mask_ready"], 1)
                dve.wait_ge(sem["x_score"], i + 1)
                if i >= 2:
                    dve.wait_ge(sem["x_exp"], i - 1)
                step(dve.tensor_tensor_reduce(T[:, i % 2, :], bank[i % 2][:, :], maskb[:, b * SK:(b + 1) * SK],
                                              1.0, FLOOR, ALU.add, ALU.max, xmax[:, i:i + 1]))
                dve.tensor_scalar(xneg[:, i:i + 1], xmax[:, i:i + 1], -1.0, None, ALU.mult) \
                   .then_inc(sem["x_max"], 1)

            def x_norm(i):
                dve.wait_ge(sem["x_exp"], i + 1)
                step(dve.reciprocal(xrz[:, i:i + 1], xz[:, i:i + 1]))
                if i >= 2:
                    dve.wait_ge(sem["x_tr"], i - 1)
                dve.tensor_scalar(T[:, 4 + i % 2, :], T[:, 2 + i % 2, :], xrz[:, i:i + 1], None, ALU.mult) \
                   .then_inc(sem["x_norm"], 1)

            def x_heads(b):
                dve.wait_ge(sem["x_pv"], XG * (b + 1))
                dve.wait_ge(sem["x_oT"], b) if b else None
                o = bank[4 + b % 2]
                step(dve.tensor_tensor(T[:, 8, 0:P].rearrange("p (h q) -> p h q", h=4),
                                       o[:, 0:P].rearrange("p (h q) -> p h q", h=4),
                                       pat(cst[:, C_HM:C_HM + 4], [[1, 4], [0, S]]), ALU.mult))
                dve.tensor_reduce(oT[:, b * S:(b + 1) * S], pat(T[:, 8, :], [[1, S], [S, 4]]), AX, ALU.add) \
                   .then_inc(sem["x_oT"], 1)

            for i in range(B * XG + 4):
                if i < B * XG:
                    x_max(i)
                if 1 <= i <= B * XG:
                    x_norm(i - 1)
                if i >= 4 and (i - 4) % XG == XG - 1:
                    x_heads((i - 4) // XG)
            dve.wait_ge(sem["x_oT"], B)
            dve.tensor_scalar(oT[:, :], oT[:, :], v("bv"), None, ALU.add).then_inc(sem["x_oT"], 1)
            dve.wait_ge(sem["xb_ready"], 1)
            dve.wait_ge(sem["x_o"], 1)
            dve.tensor_tensor(xres[:, :, :], xbias[:, :, :], bank[6][:, 0:TOK].rearrange("p (j d) -> p j d", j=NJ),
                              ALU.add).then_inc(sem["x_res"], 1)

            dve.wait_ge(sem["d_attn"], 32)
            step(dve.tensor_reduce(wmean[:, :], wqkv[:, 0:2 * AH * AD].rearrange("p (h d) -> p h d", d=AD), AX, ALU.add))
            dve.tensor_scalar(wmean[:, :], wmean[:, :], 1.0 / AD, None, ALU.mult).then_inc(sem["a_wmean"], 1)
            dve.wait_ge(sem["x_res"], 1)
            layernorm(1, xres)
            cos = pat(cst[:, C_COS:C_COS + S], [[0, 2 * B], [1, S]])
            sin = pat(cst[:, C_SIN:C_SIN + S], [[0, 2 * B], [1, S]])

            def by_time(t):
                return t.rearrange("p (n s) -> p n s", s=S)

            def a_z0(m):
                dve.wait_ge(sem["a_rstd"], m + 1)
                if m >= 2:
                    dve.wait_ge(sem["a_z"], m - 1)
                dve.scalar_tensor_tensor(out=T[:, 6 + m % 2, :], in0=bank[m % 2][:, :],
                                         scalar=v("aqw" if m < 4 else "akw"), in1=T[:, 4 + m % 2, :],
                                         op0=ALU.mult, op1=ALU.mult).then_inc(sem["a_z0"], 1)

            def a_rope(m):
                p = m % 2
                dve.wait_ge(sem["a_z"], m + 1)
                if m >= 2:
                    dve.wait_ge(sem["a_rope"], m - 1)
                step.mark(dve.tensor_tensor(by_time(T[:, 10 + p, :]), by_time(T[:, 8 + p, :]), cos, ALU.mult))
                dve.wait_ge(sem["a_rot"], m + 1)
                dve.tensor_tensor(by_time(T[:, 12 + p, :]), by_time(bank[4 + p][:, :]), sin, ALU.mult) \
                   .then_inc(sem["a_t2"], 1)
                step.sync()
                dve.wait_ge(sem["a_t2"], m + 1)
                dve.tensor_tensor(kT[:, m * 512:(m + 1) * 512], T[:, 10 + p, :], T[:, 12 + p, :], ALU.add) \
                   .then_inc(sem["a_rope"], 1)

            for m in range(9):
                if m < 8:
                    a_z0(m)
                if m >= 1:
                    a_rope(m - 1)
            dve.wait_ge(sem["a_rope"], 8)

            def heads(t):
                return t.rearrange("p (h k) -> p h k", h=AH)

            def over_keys(t):
                return pat(t, [[1, AH], [0, S]])

            for j in range(NJ):
                dve.wait_ge(sem["a_score"], j + 1)
                for odd in range(2):
                    step.mark(dve.scalar_tensor_tensor(
                        out=pat(T[:, j, :], [[2 * S, AH // 2], [1, S]], odd * S),
                        in0=bank[j + 2 * odd][:, 0:AH // 2 * S].rearrange("p (h k) -> p h k", k=S), scalar=AD ** -0.5,
                        in1=pat(cst[:, C_CAUSAL:C_CAUSAL + S], [[0, AH // 2], [1, S]]), op0=ALU.mult, op1=ALU.add))
                step.sync()
                step(dve.tensor_reduce(am[:, j, :], heads(T[:, j, :]), AX, ALU.max))
                step(dve.tensor_tensor(am[:, j, :], am[:, j, :], v("sink", 0, AH), ALU.max))
                step.mark(dve.tensor_tensor(asink[:, j, :], v("sink", 0, AH), am[:, j, :], ALU.subtract))
                step.sync()
                dve.tensor_tensor(heads(T[:, 2 + j, :]), heads(T[:, j, :]), over_keys(am[:, j, :]), ALU.subtract) \
                   .then_inc(sem["a_sub"], 1)
            for j in range(NJ):
                dve.wait_ge(sem["a_exp"], j + 1)
                step(dve.tensor_reduce(az[:, j, :], heads(T[:, 4 + j, :]), AX, ALU.add))
                step(dve.tensor_tensor(az[:, j, :], az[:, j, :], asink[:, j, :], ALU.add))
                step(dve.reciprocal(az[:, j, :], az[:, j, :]))
                step(dve.tensor_tensor(heads(T[:, 6 + j, :]), heads(T[:, 4 + j, :]), over_keys(az[:, j, :]), ALU.mult))
                dve.wait_ge(sem["a_zero"], 1)
                for b in range(BT):
                    part = slice(b * S, (b + 1) * S)
                    ins = dve.transpose(aprobT[part, j, :, part], heads(T[part, 6 + j, :]))
                ins.then_inc(sem["a_pt"], 1)
            for j in range(NJ):
                dve.wait_ge(sem["a_pv"], j + 1)
                dve.tensor_copy(T[:, 9 + 2 * j, :], bank[3 + 2 * j][:, :]).then_inc(sem["a_oTd"], 1)
            dve.wait_ge(sem["xb_ready"], 2)
            dve.wait_ge(sem["a_o"], 1)
            dve.tensor_tensor(xres[:, :, :], xbias[:, :, :], bank[6][:, 0:TOK].rearrange("p (j d) -> p j d", j=NJ),
                              ALU.add).then_inc(sem["x_res"], 1)

            dve.wait_ge(sem["x_res"], 2)
            layernorm(2, xres)

            def over_experts(t):
                return pat(t, [[1, NJ], [0, E]])

            def gate_softmax():
                step(dve.tensor_reduce(gm[:, :], lg[:, :, :], AX, ALU.max))
                dve.tensor_tensor(lg[:, :, :], lg[:, :, :], over_experts(gm[:, :]), ALU.subtract).then_inc(sem["f_sub"], 1)
                gate_softmax.n += 1
                dve.wait_ge(sem["f_exp"], gate_softmax.n)
                step(dve.tensor_reduce(gz[:, :], lg[:, :, :], AX, ALU.add))
                step(dve.reciprocal(gz[:, :], gz[:, :]))
                step(dve.tensor_tensor(lg[:, :, :], lg[:, :, :], over_experts(gz[:, :]), ALU.mult))
                for j in range(NJ):
                    step.mark(dve.max(m8[:, j, :], lg[:, j, :]))
                step.sync()
                for j in range(NJ):
                    step.mark(dve.max_index(i8[:, j, :], m8[:, j, :], lg[:, j, :]))
                step.sync()
                step(dve.tensor_copy(i8f[:, :, :], i8[:, :, :]))

            gate_softmax.n = 0
            def l_rest(i):
                dve.wait_ge(sem["l_hi"], i + 1)
                if i >= 2:
                    dve.wait_ge(sem["l_split"], i - 1)
                at = i // 2 * SK
                dve.tensor_tensor(T[:, 8 + i % 2, :], bank[6 + i % 2][:, :], (vs if i % 2 else ks)[0][:, at:at + SK],
                                  ALU.subtract).then_inc(sem["l_rest"], 1)

            iota = cst[:, C_IOTA:C_IOTA + E]
            dve.wait_ge(sem["f_gate"], 1)
            step(dve.tensor_copy(lg[:, :, :], bank[6][:, 0:NJ * E].rearrange("p (j e) -> p j e", j=NJ)))
            gate_softmax()
            step(dve.tensor_reduce(gm[:, :], m8[:, :, 0:2], AX, ALU.add))
            step(dve.tensor_scalar(gm[:, :], gm[:, :], 1e-9, None, ALU.add))
            step(dve.reciprocal(gm[:, :], gm[:, :]))
            step(dve.tensor_tensor(gw[:, :, :], m8[:, :, 0:2], pat(gm[:, :], [[1, NJ], [0, 2]]), ALU.mult))
            for j in range(NJ):
                for k in range(2):
                    step.mark(dve.tensor_scalar(cw[:, k, j, :], iota, i8f[:, j, k:k + 1], gw[:, j, k:k + 1],
                                                ALU.is_equal, ALU.mult))
            step.sync()
            dve.tensor_tensor(cw[:, 2, :, :], cw[:, 0, :, :], cw[:, 1, :, :], ALU.add).then_inc(sem["f_cw"], 1)
            dve.wait_ge(sem["f_cwps"], 1)
            dve.tensor_copy(cwT[0:E, :], bank[7][0:E, 0:TOK]).then_inc(sem["f_cwT"], 1)
            dve.wait_ge(sem["xb_ready"], 3)
            dve.wait_ge(sem["f_cw"], 1)
            for e in range(E + 1):
                dve.wait_ge(sem["f_y"], e + 1)
                if e:
                    dve.wait_ge(sem["f_acc"], NJ * e)
                for j in range(NJ):
                    ins = (dve.scalar_tensor_tensor(out=facc[:, j, :], in0=bank[4 + e % 2][:, j * D:(j + 1) * D],
                                                       scalar=cw[:, 2, j, e:e + 1] if e < E else 0.1,
                                                       in1=facc[:, j, :], op0=ALU.mult, op1=ALU.add))
                    ins.then_inc(sem["f_acc"], 1)
                if e >= 1:
                    l_rest(2 * (e - 1))
                    l_rest(2 * (e - 1) + 1)
            dve.wait_ge(sem["f_acc"], NJ * (E + 1))
            dve.wait_ge(sem["f_b2"], 1)
            dve.tensor_tensor(xres[:, :, :], facc[:, :, :], bank[6][:, 0:TOK].rearrange("p (j d) -> p j d", j=NJ),
                              ALU.add).then_inc(sem["x_res"], 1)

            dve.wait_ge(sem["l_hi"], 2 * B + 1)
            dve.tensor_tensor(T[:, 10:13, :].rearrange("p n d -> p (n d)")[:, 0:9 * D], lw[:, 4 * D:13 * D],
                              lsp[:, 0, :], ALU.subtract).then_inc(sem["l_rest"], 1)
            dve.tensor_tensor(gbias[:, :], v("bih", 0, 4), v("bhh", 0, 4), ALU.add).then_inc(sem["l_gbias"], 1)
            zeroed = (hsp[:, :, :], asp[:, :, :], negmax[:, :], c2[:, :])
            for t in zeroed:
                dve.memset(t, 0.0).then_inc(sem["l_zero"], 1)
            dve.memset(ones[:, :], 1.0).then_inc(sem["l_zero"], 1)
            dve.wait_ge(sem["x_res"], 3)
            layernorm(3, xres)
            dve.wait_ge(sem["l_zero"], 2 + len(zeroed))

            def parts(t, n):
                return pat(t, [[1, n], [n, 3]])

            base = step.n
            with dve.Fori(0, S) as t:
                step.n, step.base = 0, base + t * LSTM_STEPS
                dve.wait_ge(sem["g_ps"], t + 1)
                dve.tensor_reduce(gsum[:, :], parts(bank[0][:, 0:1], 4 * B), AX, ALU.add).then_inc(sem["g_sum"], 1)
                dve.wait_ge(sem["g_act"], t + 1)
                step.mark(dve.scalar_tensor_tensor(out=fc2[:, :], in0=gact[:, B:2 * B], scalar=1.0, in1=c2[:, :],
                                                   op0=ALU.add, op1=ALU.mult))
                step.mark(dve.scalar_tensor_tensor(out=ig[:, :], in0=gact[:, 0:B], scalar=1.0,
                                                   in1=gact[:, 3 * B:4 * B], op0=ALU.add, op1=ALU.mult))
                step.sync()
                dve.scalar_tensor_tensor(out=c2[:, :], in0=fc2[:, :], scalar=0.5, in1=ig[:, :],
                                         op0=ALU.mult, op1=ALU.add).then_inc(sem["c_new"], 1)
                dve.wait_ge(sem["c_tanh"], t + 1)
                o = gact[:, 2 * B:3 * B]
                dve.scalar_tensor_tensor(out=hsp[:, 0, :], in0=o, scalar=1.0, in1=tanhc[:, :],
                                         op0=ALU.add, op1=ALU.mult).then_inc(sem["h_hi"], 1)
                step.mark(dve.scalar_tensor_tensor(out=h32[:, :], in0=o, scalar=1.0, in1=tanhc[:, :],
                                                   op0=ALU.add, op1=ALU.mult))
                step.sync()
                dve.wait_ge(sem["h_hi"], t + 1)
                dve.tensor_tensor(hsp[:, 1, :], h32[:, :], hsp[:, 0, :], ALU.subtract).then_inc(sem["h_mid"], 1)
                step.mark(dve.tensor_tensor(hrest[:, :], h32[:, :], hsp[:, 0, :], ALU.subtract))
                step.sync()
                dve.wait_ge(sem["h_mid"], t + 1)
                dve.tensor_tensor(hsp[:, 2, :], hrest[:, :], hsp[:, 1, :], ALU.subtract).then_inc(sem["h_lo"], 1)
                dve.wait_ge(sem["s_hi"], t + 1)
                dve.tensor_reduce(mc[:, :], bank[1][:, 0:B * KC].rearrange("p (b c) -> p b c", c=KC), AX, ALU.max) \
                   .then_inc(sem["m_c"], 1)
                dve.wait_ge(sem["m_t"], t + 1)
                step(dve.tensor_reduce(m1[:, :], bank[3][0:B, 0:P], AX, ALU.max))
                dve.tensor_scalar(negmax[0:B, :], cst[0:B, C_NEG:C_NEG + B * KC], m1[:, :], None, ALU.mult) \
                   .then_inc(sem["m_d"], 1)
                dve.wait_ge(sem["s_ps"], t + 1)
                dve.tensor_reduce(ssum[:, :], parts(bank[2][:, 0:1], B * KC), AX, ALU.add).then_inc(sem["s_sum"], 1)
                dve.wait_ge(sem["e_32"], t + 1)
                dve.tensor_tensor(esp[:, 1, :], e32[:, :], esp[:, 0, :], ALU.subtract).then_inc(sem["e_mid"], 1)
                step.mark(dve.tensor_tensor(erest[:, :], e32[:, :], esp[:, 0, :], ALU.subtract))
                step.sync()
                dve.wait_ge(sem["e_mid"], t + 1)
                dve.tensor_tensor(esp[:, 2, :], erest[:, :], esp[:, 1, :], ALU.subtract).then_inc(sem["e_lo"], 1)
                dve.wait_ge(sem["oh_ps"], t + 1)
                step.mark(dve.tensor_reduce(oh[:, :], parts(bank[5][:, 0:1], B), AX, ALU.add))
                dve.wait_ge(sem["z_ps"], t + 1)
                step(dve.tensor_reduce(zs[:, :], pat(bank[4][:, 0:1], [[KC, B], [B * KC, 3], [1, KC]]),
                                       mybir.AxisListType.XY, ALU.add))
                step(dve.reciprocal(rz[:, :], zs[:, :]))
                dve.wait_ge(sem["v_ps"], t + 1)
                step(dve.tensor_reduce(opre[:, :], parts(bank[6][:, 0:1], B), AX, ALU.add))
                step(dve.tensor_tensor(opre[:, :], opre[:, :], rz[:, :], ALU.mult))
                dve.tensor_tensor(opre[:, :], opre[:, :], oh[:, :], ALU.add).then_inc(sem["o_pre"], 1)
                dve.wait_ge(sem["at_32"], t + 1)
                dve.tensor_tensor(asp[:, 1, :], a32[:, :], asp[:, 0, :], ALU.subtract).then_inc(sem["at_mid"], 1)
                step.mark(dve.tensor_tensor(arest[:, :], a32[:, :], asp[:, 0, :], ALU.subtract))
                step.sync()
                dve.wait_ge(sem["at_mid"], t + 1)
                dve.tensor_tensor(asp[:, 2, :], arest[:, :], asp[:, 1, :], ALU.subtract).then_inc(sem["at_lo"], 1)
                dve.wait_ge(sem["y_st"], t + 1)
                assert step.n == LSTM_STEPS, step.n
            step.n, step.base = base + S * LSTM_STEPS, 0
            dve.wait_ge(sem["y_tr"], 1)
            dve.tensor_tensor(xres[:, :, :], xres[:, :, :], bank[7][:, 0:TOK].rearrange("p (j d) -> p j d", j=NJ),
                              ALU.add).then_inc(sem["x_res"], 1)

            for t, x in ((up[:, :, :, :], 0.0), (two[:, :], 2.0)):
                dve.memset(t, x).then_inc(sem["m_const"], 1)
            dve.tensor_copy(sel[:, :], cst[0:6 * MN, C_SEL:C_SEL + 2 * MN]).then_inc(sem["m_const"], 1)
            dve.wait_ge(sem["x_res"], 4)
            layernorm(4, xres)
            z, z2, poly, delta, du = (T[:, i, :] for i in (3, 13, 14, 6, 7))
            for l in range(ML):
                conv(dve, step, l, 0).then_inc(sem["m_conv"], 1)
                dve.wait_ge(sem["m_bc"], l + 1)
                dve.tensor_copy(dts[:, :], bank[3][0:MR, 0:TOK]).then_inc(sem["m_dts"], 1)
                bc, rest = bank[2][0:6 * MN, 0:TOK], T[0:6 * MN, 15, 0:TOK]
                step(dve.tensor_copy(bcs[:, :], bc))
                for k in (1, 2):
                    for q in range(k, 3):
                        part = slice(q * 2 * MN, (q + 1) * 2 * MN)
                        step.mark(dve.tensor_tensor(rest[part, :], (bc if k == 1 else rest)[part, :], bcs[part, :],
                                                    ALU.subtract))
                    step.sync()
                    for q in range(k, 3):
                        part = slice(q * 2 * MN, (q + 1) * 2 * MN)
                        ins = dve.tensor_copy(bcs[part, :], rest[part, :])
                        if k == 1:
                            step.mark(ins)
                    step.sync()
                ins.then_inc(sem["m_bcs"], 1)
                dve.wait_ge(sem["m_e"], l + 1)
                step(dve.tensor_tensor(z, T[:, 4, :], T[:, 5, :], ALU.mult))
                step(dve.tensor_tensor(z2, z, z, ALU.mult))
                step(dve.tensor_scalar(poly, z2, LOG1P[4], LOG1P[3], ALU.mult, ALU.add))
                step(dve.tensor_tensor(poly, poly, z2, ALU.mult))
                for c in (LOG1P[2], LOG1P[1]):
                    step(dve.scalar_tensor_tensor(out=poly, in0=poly, scalar=c, in1=z2, op0=ALU.add, op1=ALU.mult))
                step(dve.scalar_tensor_tensor(out=poly, in0=poly, scalar=LOG1P[0], in1=z, op0=ALU.add, op1=ALU.mult))
                step(dve.tensor_tensor(delta, poly, T[:, 12, :], ALU.add))
                dve.tensor_tensor(du, delta, T[:, 1, :], ALU.mult).then_inc(sem["m_delta"], 1)
                dve.wait_ge(sem["m_delta"], l + 1)
                if l:
                    dve.wait_ge(sem["m_y"], l)
                for i in range(MNP):
                    n = l * MNP + i
                    dve.wait_ge(sem["m_bsb"], n + 1)
                    dve.tensor_tensor(pairs(state[0], i), over_pair(du[:, 0:TOK]), both(T[:, 8 + i % 2, :]), ALU.mult) \
                       .then_inc(sem["m_dbu0"], 1)
                    at = slice(i * 2 * TOK, (i + 1) * 2 * TOK)
                    for ch in range(MC):
                        dve.wait_ge(sem["m_dbu0" if ch == 0 else "m_dbu1"], n + 1)
                        dve.wait_ge(sem["m_dA"], 2 * n + ch + 1)
                        dve.tensor_tensor_scan(out=state[ch][:, at], data0=decay[ch][:, at], data1=state[ch][:, at],
                                               initial=0.0, op0=ALU.mult, op1=ALU.add) \
                           .then_inc(sem["m_scan0" if ch == 0 else "m_scan1"], 1)
                    dve.wait_ge(sem["m_csb"], n + 1)
                    dve.wait_ge(sem["m_scan0"], n + 1)
                    dve.tensor_tensor(pairs(state[0], i), pairs(state[0], i), both(T[:, 10 + i % 2, :]), ALU.mult) \
                       .then_inc(sem["m_hc0"], 1)
                dve.wait_ge(sem["m_y"], l + 1)
                for ch in range(MC):
                    half = slice(ch * TOK, (ch + 1) * TOK)
                    step.mark(dve.scalar_tensor_tensor(out=T[:, 3, half], in0=T[:, 1, half], scalar=v("mD", l * MC + ch),
                                                       in1=bank[0][:, half], op0=ALU.mult, op1=ALU.add))
                step.sync()
                dve.wait_ge(sem["m_zs"], l + 1)
                dve.tensor_tensor(T[:, 13, :], T[:, 3, :], T[:, 2, :], ALU.mult).then_inc(sem["m_ys"], 1)
                dve.wait_ge(sem["m_o"], l + 1)
                res = T[:, 3, 0:TOK].rearrange("p (j d) -> p j d", j=NJ)
                step(dve.tensor_tensor(res, xn[:, :, :], bank[4][:, 0:TOK].rearrange("p (j d) -> p j d", j=NJ), ALU.add))
                layernorm(5 + l, res, l)
            step(dve.tensor_tensor(xres[:, :, :], xres[:, :, :], xn[:, :, :], ALU.add))
            layernorm(5 + ML, xres)
            step(dve.tensor_tensor(facc[:, :, :], xres[:, :, :], pat(r("wob"), [[0, NJ], [1, D]]), ALU.add))
            dve.wait_ge(sem["r_gate"], 1)
            step(dve.tensor_tensor(lg[:, :, :], bank[6][:, 0:NJ * E].rearrange("p (j e) -> p j e", j=NJ),
                                   pat(r("gateb", 0, E), [[0, NJ], [1, E]]), ALU.add))
            gate_softmax()
            for j in range(NJ):
                step.mark(dve.tensor_scalar(oneh[:, j, :], iota, i8f[:, j, 0:1], None, ALU.is_equal))
            step.sync()
            dve.wait_ge(sem["r_a"], 1)
            dve.tensor_tensor(loraa[:, :, :].rearrange("p j (e k) -> p (j e) k", k=LR),
                              bank[7][:, 0:NJ * E * LR].rearrange("p (n k) -> p n k", k=LR),
                              pat(oneh[:, :, :], [[1, NJ * E], [0, LR]]), ALU.mult).then_inc(sem["r_am"], 1)
            dve.wait_ge(sem["r_amps"], 1)
            dve.tensor_copy(cwT[:, :], bank[5][0:E * LR, 0:TOK]).then_inc(sem["r_amT"], 1)
            dve.wait_ge(sem["r_o"], 1)
            dve.tensor_tensor(xres[:, :, :], facc[:, :, :], bank[4][:, 0:TOK].rearrange("p (j d) -> p j d", j=NJ),
                              ALU.add).then_inc(sem["x_res"], 2)

        @block.tensor
        def _(pe):
            def ln_transpose(n):
                pe.wait_ge(sem["ln_xn"], n + 1)
                for j in range(NJ):
                    ins = pe.transpose(bank[7][:, j * P:(j + 1) * P], xn[:, j, :], ident)
                ins.then_inc(sem["ln_tr"], 1)

            pe.wait_ge(sem["d_par"], 48)
            cb8 = cst[:, C_CB8:C_CB8 + P]
            pe.matmul(bank[6][:, 0:D], wx[:, 0:D], cb8, start=True, stop=True)
            pe.matmul(bank[6][:, D:2 * D], wx[:, D:2 * D], cb8, start=True, stop=True)
            pe.matmul(bank[6][:, 2 * D:2 * D + 2], cb8, v("bq", 0, 2), start=True, stop=True).then_inc(sem["xw_ps"], 1)
            ln_transpose(0)
            pe.wait_ge(sem["xw_sb"], 1)

            def k_proj(s):
                if s >= 2:
                    pe.wait_ge(sem["k_sq"], s - 1)
                if s == 0:
                    pe.wait_ge(sem["ln_xT"], 1)
                    pe.matmul(bank[0][:, 0:TOK], xw[:, D:2 * D], xnT[:, :], start=True, stop=True) \
                      .then_inc(sem["k_proj"], 1)
                    return
                b = s - 1
                pe.wait_ge(d_ctx[b], 16)
                pe.matmul(bank[s % 2][:, :], xw[:, 0:D], ctxT[:, b * SK:(b + 1) * SK], start=True, stop=True) \
                  .then_inc(sem["k_proj"], 1)
                if b >= 2:
                    pe.wait_ge(sem["v_evac"], b - 1)
                for c in range(KC):
                    at = b * SK + c * P
                    ins = pe.matmul(bank[4 + b % 2][:, c * P:(c + 1) * P], ctxT[:, at:at + P], wx[:, 2 * D:3 * D],
                                    start=True, stop=True)
                ins.then_inc(sem["v_proj"], 1)

            def k_var(s):
                w, p = (TOK if s == 0 else SK), s % 2
                pe.wait_ge(sem["k_sq"], s + 1)
                if s >= 2:
                    pe.wait_ge(sem["k_rstd"], s - 1)
                pe.matmul(bank[2 + p][:, 0:w], cst[:, C_BLK8:C_BLK8 + P], T[:, 2 + p, 0:w], start=True, stop=True) \
                  .then_inc(sem["k_var"], 1)

            for s in range(2 + B):
                if s <= B:
                    k_proj(s)
                if s >= 1:
                    k_var(s - 1)

            def x_scores(i):
                b, g = divmod(i, XG)
                if i == 0:
                    pe.wait_ge(sem["qblk_ready"], 1)
                    pe.wait_ge(sem["k_done"], 1 + B)
                    pe.wait_ge(sem["v_evac"], B)
                    pe.wait_ge(sem["k_rstd"], 1 + B)
                if i >= 2:
                    pe.wait_ge(sem["x_max"], i - 1)
                pe.matmul(bank[i % 2][:, :], qblk[:, g, b, :, :], kT[:, b * SK:(b + 1) * SK],
                          start=True, stop=True).then_inc(sem["x_score"], 1)

            def x_transpose(i):
                pe.wait_ge(sem["x_norm"], i + 1)
                if i >= 2:
                    pe.wait_ge(sem["x_pt"], i - 1)
                for c in range(KC):
                    ins = pe.transpose(bank[2 + i % 2][:, c * P:(c + 1) * P], T[:, 4 + i % 2, c * P:(c + 1) * P], ident)
                ins.then_inc(sem["x_tr"], 1)

            def x_pv(i):
                b, g = divmod(i, XG)
                pe.wait_ge(sem["x_pt"], i + 1)
                if g == 0 and b >= 2:
                    pe.wait_ge(sem["x_oT"], b - 1)
                for c in range(KC):
                    ins = pe.matmul(bank[4 + b % 2][32 * g:32 * g + 32, 0:P], vx[:, b * KC + c, 32 * g:32 * g + 32],
                                    T[:, 6 + i % 2, c * P:(c + 1) * P], start=(c == 0), stop=(c == KC - 1))
                ins.then_inc(sem["x_pv"], 1)

            for i in range(B * XG + 3):
                if i < B * XG:
                    x_scores(i)
                if 2 <= i < B * XG + 2:
                    x_transpose(i - 2)
                if i >= 3:
                    x_pv(i - 3)
            pe.wait_ge(sem["x_oT"], B + 1)
            for j in range(NJ):
                ins = pe.matmul(bank[6][:, j * D:(j + 1) * D], oT[:, j * P:(j + 1) * P], wx[:, 3 * D:4 * D],
                                start=True, stop=True)
            ins.then_inc(sem["x_o"], 1)

            ln_transpose(1)

            def a_proj(m):
                if m == 0:
                    pe.wait_ge(sem["a_wc"], 1)
                    pe.wait_ge(sem["ln_xT"], 2)
                if m >= 2:
                    pe.wait_ge(sem["a_z0"], m - 1)
                for h in range(2):
                    ins = pe.matmul(bank[m % 2][:, h * TOK:(h + 1) * TOK], wqkv[:, (2 * m + h) * P:(2 * m + h + 1) * P],
                                    xnT[:, :], start=True, stop=True)
                ins.then_inc(sem["a_proj"], 1)

            def a_var(m):
                pe.wait_ge(sem["a_sq"], m + 1)
                if m >= 2:
                    pe.wait_ge(sem["a_rstd"], m - 1)
                pe.matmul(bank[2 + m % 2][:, :], cst[:, C_BLK64:C_BLK64 + P], T[:, m % 2, :], start=True, stop=True) \
                  .then_inc(sem["a_var"], 1)

            def a_rot(m):
                pe.wait_ge(sem["a_z"], m + 1)
                if m >= 2:
                    pe.wait_ge(sem["a_t2"], m - 1)
                pe.matmul(bank[4 + m % 2][:, :], cst[:, C_ROT:C_ROT + P], T[:, 8 + m % 2, :], start=True, stop=True) \
                  .then_inc(sem["a_rot"], 1)

            def a_vproj(n):
                if n >= 1:
                    pe.wait_ge(sem["a_vev"], n)
                at = 2 * AH * AD + (n % 2) * 512
                pe.matmul(bank[6][:, :], xnT[:, (n // 2) * P:(n // 2 + 1) * P], wqkv[:, at:at + 512],
                          start=True, stop=True).then_inc(sem["a_vproj"], 1)

            for m in range(10):
                if m < 8:
                    a_proj(m)
                if 1 <= m <= 8:
                    a_var(m - 1)
                if m >= 2:
                    a_rot(m - 2)
                if 4 <= m < 8:
                    a_vproj(m - 4)
            pe.wait_ge(sem["a_rope"], 8)
            for j in range(NJ):
                for h in range(AH):
                    rowsh = slice(AD * (h % 2), AD * (h % 2) + AD)
                    for b in range(BT):
                        at = (h // 2) * TOK + (j * BT + b) * S
                        ins = pe.matmul(bank[j + 2 * (h % 2)][b * S:(b + 1) * S, h // 2 * S:(h // 2 + 1) * S], kT[rowsh, at:at + S],
                                        kT[rowsh, 4 * 512 + at:4 * 512 + at + S], start=True, stop=True)
                ins.then_inc(sem["a_score"], 1)
            pe.wait_ge(sem["a_vev"], 4)
            pe.wait_ge(sem["d_attn"], 32)
            for j in range(NJ):
                pe.wait_ge(sem["a_pt"], j + 1)
                for h in range(AH):
                    o = bank[2 + 2 * j + h // 8]
                    ins = pe.matmul(o[AD * (h % 2):AD * (h % 2) + AD, (h // 2 % 4) * P:(h // 2 % 4 + 1) * P],
                                    avals[:, j, h * AD:(h + 1) * AD], aprobT[:, j, h, :], start=True, stop=True)
                ins.then_inc(sem["a_pv"], 1)
            for j in range(NJ):
                pe.wait_ge(sem["a_oT"], j + 1)
                pe.wait_ge(sem["a_oTd"], j + 1)
                for n in range(AH // 2):
                    ins = pe.matmul(bank[6][:, j * D:(j + 1) * D], T[:, 8 + 2 * j + n // 4, (n % 4) * P:(n % 4 + 1) * P],
                                    projT[:, n * D:(n + 1) * D], start=(n == 0), stop=(n == AH // 2 - 1))
            ins.then_inc(sem["a_o"], 1)

            ln_transpose(2)
            pe.wait_ge(sem["ln_xT"], 3)
            pe.wait_ge(sem["d_ffn"], 80)
            for j in range(NJ):
                ins = pe.matmul(bank[6][:, j * E:(j + 1) * E], xnT[:, j * P:(j + 1) * P], wg[:, :], start=True, stop=True)
            ins.then_inc(sem["f_gate"], 1)
            pe.wait_ge(sem["d_ffn"], 80)

            def f_hidden(e):
                if e >= 2:
                    pe.wait_ge(sem["f_act"], 2 * (e - 1))
                w = w1[:, e * F:(e + 1) * F] if e < E else ws[:, 0:F]
                for fc in range(FC):
                    half = slice((fc % 2) * TOK, (fc % 2) * TOK + TOK)
                    ins = pe.matmul(bank[2 * (e % 2) + fc // 2][:, half], w[:, fc * P:(fc + 1) * P], xnT[:, :],
                                    start=True, stop=True)
                    if fc % 2:
                        ins.then_inc(sem["f_h"], 1)

            def f_out(e):
                pe.wait_ge(sem["f_act"], 2 * (e + 1))
                if e >= 2:
                    pe.wait_ge(sem["f_acc"], NJ * (e - 1))
                w = w2[:, e * F:(e + 1) * F] if e < E else ws[:, F:2 * F]
                for j in range(NJ):
                    for fc in range(FC):
                        at = (fc % 2) * TOK + j * P
                        ins = pe.matmul(bank[4 + e % 2][:, j * D:(j + 1) * D], T[:, 2 * (e % 2) + fc // 2, at:at + P],
                                        w[:, fc * D:(fc + 1) * D], start=(fc == 0), stop=(fc == FC - 1))
                ins.then_inc(sem["f_y"], 1)

            def l_keys_values(b):
                if b == 0:
                    pe.wait_ge(sem["d_lw"], 16)
                    pe.wait_ge(sem["f_cwT"], 1)
                else:
                    pe.wait_ge(sem["l_rest"], 2 * b - 1)
                pe.matmul(bank[6][:, :], lw[:, 14 * D:15 * D], ctxT[:, b * SK:(b + 1) * SK], start=True, stop=True) \
                  .then_inc(sem["l_kv"], 1)
                if b:
                    pe.wait_ge(sem["l_rest"], 2 * b)
                for c in range(KC):
                    at = b * SK + c * P
                    ins = pe.matmul(bank[7][:, c * P:(c + 1) * P], ctxT[:, at:at + P], lw[:, 13 * D:14 * D],
                                    start=True, stop=True)
                ins.then_inc(sem["l_kv"], 1)

            for e in range(E + 2):
                if e <= E:
                    f_hidden(e)
                if e == 1:
                    pe.wait_ge(sem["f_cw"], 1)
                    for j in range(NJ):
                        ins = pe.transpose(bank[7][0:E, j * P:(j + 1) * P], cw[:, 2, j, :], ident)
                    ins.then_inc(sem["f_cwps"], 1)
                if e >= 1:
                    f_out(e - 1)
                if e >= 2:
                    l_keys_values(e - 2)
            pe.wait_ge(sem["l_rest"], 2 * B)
            pe.wait_ge(sem["f_cwT"], 1)
            pe.wait_ge(sem["d_ffn"], 80)
            for j in range(NJ):
                ins = pe.matmul(bank[6][:, j * D:(j + 1) * D], cwT[0:E, j * P:(j + 1) * P], b2[:, :], start=True, stop=True)
            ins.then_inc(sem["f_b2"], 1)

            ln_transpose(3)
            pe.wait_ge(sem["ln_xT"], 4)
            for g in range(4):
                ins = pe.matmul(bank[g // 2][:, (g % 2) * TOK:(g % 2 + 1) * TOK], lw[:, g * D:(g + 1) * D], xnT[:, :],
                                start=True, stop=True)
            ins.then_inc(sem["l_gxps"], 1)

            def mm(out, lhsT, rhs, start=False, stop=False):
                return pe.matmul(out, lhsT, rhs, start=start, stop=stop, skip_group_check=True)

            def weight(k, m):
                return lsp[:, k, m * D:(m + 1) * D]

            MEETS = ((2, 1), (1, 2), (0, 3))

            def x_gates(t):
                mm(bank[0][:, 0:4 * B], ident, gx[:, bass.ds(t, 1), :, :], start=True)

            def h_gates():
                for k, n in MEETS:
                    for g in range(4):
                        mm(pat(bank[0][:, 0:1], [[4 * B, n], [1, B]], g * B), weight(k, 4 + g), hsp[:, 0:n, :])

            pe.wait_ge(sem["l_gx"], 1)
            pe.wait_ge(sem["l_split"], 2 * B + 1)
            pe.wait_ge(sem["l_zero"], 2 + 4)
            x_gates(0)
            h_gates()
            with pe.Fori(0, S) as t:
                for (k, n), ready in zip(MEETS, ("at_hi", "at_mid", "at_lo")):
                    pe.wait_ge(sem[ready], t)
                    for g in range(4):
                        ins = mm(pat(bank[0][:, 0:1], [[4 * B, n], [1, B]], g * B), weight(k, g), asp[:, 0:n, :],
                                 stop=(k == 0))
                ins.then_inc(sem["g_ps"], 1)
                pe.wait_ge(sem["h_hi"], t + 1)
                for i in range(B * KC):
                    ins = mm(bank[1][:, i:i + 1], ks[0][:, i * P:(i + 1) * P], hsp[:, 0, i // KC:i // KC + 1],
                             start=(i == 0), stop=True)
                ins.then_inc(sem["s_hi"], 1)

                def scores(k, n, start=False):
                    for i in range(B * KC):
                        mm(pat(bank[2][:, 0:1], [[B * KC, n]], i), ks[k][:, i * P:(i + 1) * P],
                           pat(hsp[:, 0, 0:1], [[B, n]], i // KC), start=(start and i == 0))

                pe.wait_ge(sem["h_mid"], t + 1)
                scores(1, 2, True)
                pe.wait_ge(sem["m_c"], t + 1)
                pe.transpose(bank[3][0:B, 0:P], mc[:, :], ident).then_inc(sem["m_t"], 1)
                scores(2, 1)
                pe.wait_ge(sem["h_lo"], t + 1)
                scores(0, 3)
                pe.wait_ge(sem["m_d"], t + 1)
                mm(bank[2][:, 0:B * KC], ones[:, :], negmax[:, :], stop=True).then_inc(sem["s_ps"], 1)
                x_gates(t + 1)
                h_gates()
                for k, n in MEETS:
                    ins = mm(bank[5][:, 0:n * B], weight(k, 8), hsp[:, 0:n, :].rearrange("p k b -> p (k b)"),
                             start=(k == 2), stop=(k == 0))
                ins.then_inc(sem["oh_ps"], 1)

                def values(k, n):
                    for i in range(B * KC):
                        ins = mm(pat(bank[6][:, 0:1], [[B, n]], i // KC), vs[k][:, i * P:(i + 1) * P],
                                 pat(esp[:, 0, 0:1], [[B * KC, n]], i), start=(k == 2 and i == 0), stop=(k == 0))
                    return ins

                pe.wait_ge(sem["e_hi"], t + 1)
                values(2, 1)
                pe.wait_ge(sem["e_mid"], t + 1)
                values(1, 2)
                pe.wait_ge(sem["e_lo"], t + 1)
                mm(bank[4][:, 0:3 * B * KC], ones[:, :], esp[:, :, :].rearrange("p k i -> p (k i)"),
                   start=True, stop=True).then_inc(sem["z_ps"], 1)
                values(0, 3).then_inc(sem["v_ps"], 1)
            pe.wait_ge(sem["y_st"], S)
            for j in range(NJ):
                ins = pe.transpose(bank[7][:, j * P:(j + 1) * P], yT[:, j * BT:(j + 1) * BT, :].rearrange("p b t -> p (b t)"), ident)
            ins.then_inc(sem["y_tr"], 1)

            ln_transpose(4)
            pe.wait_ge(sem["d_late"], 64)
            pe.wait_ge(sem["m_const"], MC + 3)
            for l in range(ML):
                pe.wait_ge(sem["ln_xT"], 5 + l)
                if l:
                    pe.wait_ge(sem["m_ys"], l)
                for n in range(2 * MC):
                    ins = pe.matmul(bank[n // 2][:, (n % 2) * TOK:(n % 2 + 1) * TOK],
                                    m_in[:, (4 * l + n) * P:(4 * l + n + 1) * P], xnT[:, :], start=True, stop=True)
                ins.then_inc(sem["m_uz"], 1)
                pe.wait_ge(sem["m_us"], l + 1)
                if l:
                    pe.wait_ge(sem["m_csb"], l * MNP)
                for out, a, z in ((bank[2][0:6 * MN, 0:TOK], 0, 6 * MN), (bank[3][0:MR, 0:TOK], 6 * MN, 6 * MN + MR)):
                    for ch in range(MC):
                        at = (l * MC + ch) * (6 * MN + MR)
                        ins = pe.matmul(out, m_x[:, at + a:at + z], T[:, 1, ch * TOK:(ch + 1) * TOK],
                                        start=(ch == 0), stop=(ch == MC - 1))
                ins.then_inc(sem["m_bc"], 1)
                pe.wait_ge(sem["m_dts"], l + 1)
                for ch in range(MC):
                    at = l * MI + ch * P
                    ins = pe.matmul(bank[4][:, ch * TOK:(ch + 1) * TOK], dtw[:, at:at + P], dts[:, :], start=True, stop=True)
                ins.then_inc(sem["m_dps"], 1)
                pe.wait_ge(sem["m_bcs"], l + 1)

                def spread(b, n):
                    for k in range(2):
                        ins = pe.matmul(bank[b][:, k * TOK:(k + 1) * TOK], pat(sel[:, n + k:n + k + 1], [[0, P]]),
                                        bcs[:, :], start=True, stop=True)
                    return ins

                for i in range(MNP + 2):
                    if i < MNP:
                        n = l * MNP + i
                        if i >= 2:
                            pe.wait_ge(sem["m_bsb"], n - 1)
                            pe.wait_ge(sem["m_csb"], n - 1)
                        spread(2 + i % 2, 2 * i).then_inc(sem["m_bps"], 1)
                        spread(5 + i % 2, MN + 2 * i).then_inc(sem["m_cps"], 1)
                    if i >= 2:
                        n = l * MNP + i - 2
                        for ch in range(MC):
                            pe.wait_ge(sem["m_hc0" if ch == 0 else "m_hc1"], n + 1)
                            for k in range(2):
                                at = (2 * (i - 2) + k) * TOK
                                ins = pe.matmul(bank[0][:, ch * TOK:(ch + 1) * TOK], ident, state[ch][:, at:at + TOK],
                                                start=(i == 2 and ch == 0 and k == 0), stop=(i == MNP + 1),
                                                skip_group_check=True)
                ins.then_inc(sem["m_y"], 1)
                pe.wait_ge(sem["m_ys"], l + 1)
                for j in range(NJ):
                    for ch in range(MC):
                        at = (l * MC + ch) * D
                        ins = pe.matmul(bank[4][:, j * D:(j + 1) * D], T[:, 13, ch * TOK + j * P:ch * TOK + (j + 1) * P],
                                        m_out[:, at:at + D], start=(ch == 0), stop=(ch == MC - 1))
                ins.then_inc(sem["m_o"], 1)
                ln_transpose(5 + l)

            ln_transpose(5 + ML)
            pe.wait_ge(sem["ln_xT"], 6 + ML)
            pe.wait_ge(sem["d_late"], 64)
            lora, wi, wo = fw[:, E:E + E * LR], fw[:, E + E * LR:E + E * LR + F], fw[:, E + E * LR + F:]
            for j in range(NJ):
                ins = pe.matmul(bank[6][:, j * E:(j + 1) * E], xnT[:, j * P:(j + 1) * P], fw[:, 0:E], start=True, stop=True)
            ins.then_inc(sem["r_gate"], 1)
            for j in range(NJ):
                ins = pe.matmul(bank[7][:, j * E * LR:(j + 1) * E * LR], xnT[:, j * P:(j + 1) * P], lora,
                                start=True, stop=True)
            ins.then_inc(sem["r_a"], 1)
            for fc in range(FC):
                pe.matmul(bank[fc][:, 0:TOK], wi[:, fc * P:(fc + 1) * P], xnT[:, :], start=True, stop=False)
            pe.wait_ge(sem["r_am"], 1)
            for j in range(NJ):
                ins = pe.transpose(bank[5][0:E * LR, j * P:(j + 1) * P], loraa[:, j, :], ident)
            ins.then_inc(sem["r_amps"], 1)
            pe.wait_ge(sem["r_amT"], 1)
            for fc in range(FC):
                pe.matmul(bank[fc][:, 0:TOK], lb[:, fc * P:(fc + 1) * P], cwT[:, :], start=False, stop=True) \
                  .then_inc(sem["r_h"], 1)
            pe.wait_ge(sem["r_act"], FC)
            for j in range(NJ):
                for fc in range(FC):
                    at = (fc % 2) * TOK + j * P
                    ins = pe.matmul(bank[4][:, j * D:(j + 1) * D], T[:, fc // 2, at:at + P], wo[:, fc * D:(fc + 1) * D],
                                    start=(fc == 0), stop=(fc == FC - 1))
            ins.then_inc(sem["r_o"], 1)


def lay_out(i):
    a = {k: np.asarray(x) for k, x in i.items()}

    def wide(m):
        return m.reshape(-1, P, m.shape[-1]).transpose(1, 0, 2).reshape(P, -1)

    ctxT = a["ctx_1024"].reshape(B * SK, D).T
    kv = a["L0_xattn_Wkv"]
    wx = np.concatenate([kv[:D], a["L0_xattn_Wq"], kv[D:].T, a["L0_xattn_Wo"].T], 1)

    def col(x, times=1):
        return np.tile(x, times).reshape(-1, P).T

    n = "L1_attn_"
    parts = {
        "bq": col(a["L0_xattn_bq"]), "bk": col(a["L0_xattn_bkv"][:D]), "bv": col(a["L0_xattn_bkv"][D:]),
        "qw": col(a["L0_xattn_qn_w"], XH), "qb": col(a["L0_xattn_qn_b"], XH),
        "kw": col(a["L0_xattn_kn_w"], XH), "kb": col(a["L0_xattn_kn_b"], XH),
        "aqw": col(a["L0_attn_qn_w"], 2), "aqb": col(a["L0_attn_qn_b"], 2),
        "akw": col(a["L0_attn_kn_w"], 2), "akb": col(a["L0_attn_kn_b"], 2),
        "sink": np.broadcast_to(a["L0_attn_sinks"], (P, AH)),
        "b1": a["L0_ffn_b1"].reshape(E * FC, P).T, "bs1": col(a["L0_ffn_bs1"]),
        "bih": lstm_order(a["L1_xattn_b_ih"]).reshape(4, P).T, "bhh": lstm_order(a["L1_xattn_b_hh"]).reshape(4, P).T,
        "bout": col(a["L1_xattn_b_out"]),
        "convw": a[n + "conv_w"].reshape(ML * MC, P, MK).transpose(1, 0, 2).reshape(P, -1),
        "convb": a[n + "conv_b"].reshape(ML * MC, P).T, "dtb": a[n + "dt_proj_b"].reshape(ML * MC, P).T,
        "mD": a[n + "D"].reshape(ML * MC, P).T,
        "alog": a[n + "A_log"].reshape(ML * MC, P, MN).transpose(1, 0, 2).reshape(P, -1),
        "wib": col(a["L1_ffn_wi_b"]),
    }
    vec = np.concatenate([parts[k].reshape(P, w) for k, w in V_NAMES], 1)
    lines = {"bo": a["L0_xattn_bo"], "projb": a["L0_attn_proj_b"], "bs2": a["L0_ffn_bs2"], "wob": a["L1_ffn_wo_b"],
             "gateb": a["L1_ffn_gate_b"], "lnw": a[n + "ln_w"].reshape(-1), "lnb": a[n + "ln_b"].reshape(-1)}
    rows = np.broadcast_to(np.concatenate([lines[k] for k, _ in R_NAMES]), (P, R_END))
    w_ih = lstm_order(a["L1_xattn_W_ih"])
    xp = a[n + "x_proj_w"].reshape(ML, MC, P, MR + 2 * MN)
    xp = np.concatenate([xp[..., MR:]] * 3 + [xp[..., :MR]], -1).transpose(2, 0, 1, 3).reshape(P, -1)
    outs = {
        "x": a["x"].reshape(TOK, D), "cst": shape_constants(), "vec": vec, "rows": rows, "wx": wx, "ctxT": ctxT,
        "mask": a["mask_BxS2_bk0"].reshape(1, B * SK),
        "qkvT": a["L0_attn_qkv_w"].T, "projT": wide(a["L0_attn_proj_w"].T),
        "wg": a["L0_ffn_Wg"], "w1": a["L0_ffn_W1"].transpose(1, 0, 2).reshape(P, E * F),
        "w2": wide(a["L0_ffn_W2"].reshape(E * F, D)), "b2": a["L0_ffn_b2"],
        "ws": np.concatenate([a["L0_ffn_Ws1"], wide(a["L0_ffn_Ws2"])], 1),
        "lw": np.concatenate([w_ih[:, :D].T, w_ih[:, D:].T, lstm_order(a["L1_xattn_W_hh"]).T,
                              a["L1_xattn_Wout"][:, D:].T, a["L1_xattn_Wout"][:, :D].T, a["L1_xattn_Wq"]], 1),
        "mw": np.concatenate([a[n + "in_proj_w"].transpose(1, 0, 2).reshape(P, -1), xp,
                              a[n + "out_proj_w"].reshape(ML * MC, P, D).transpose(1, 0, 2).reshape(P, -1)], 1),
        "dtw": a[n + "dt_proj_w"].transpose(1, 0, 2).reshape(MR, -1),
        "fw": np.concatenate([a["L1_ffn_gate_W"].T, a["L1_ffn_lora_A"].reshape(E * LR, D).T,
                              a["L1_ffn_wi_W"].T, wide(a["L1_ffn_wo_W"].T)], 1),
        "lb": a["L1_ffn_lora_B"].transpose(0, 2, 1).reshape(E * LR, F),
    }
    return {k: np.ascontiguousarray(x) for k, x in outs.items()}


def lstm_order(w):
    i, f, g, o = np.split(w, 4, 0)
    return np.concatenate([i, f, o, g], 0)


def kernel(**inputs):
    import concourse.bacc as _bacc
    from concourse.bass_utils import run_bass_kernel_spmd as _run

    nc = _bacc.Bacc("TRN2", target_bir_lowering=False, num_devices=1)
    arrays = {f"in_{k}_dram": x for k, x in lay_out(inputs).items()}
    arr = {k[3:-5]: nc.dram_tensor(k, x.shape, mybir.dt.from_np(x.dtype), kind="ExternalInput").ap()
           for k, x in arrays.items()}
    out = nc.dram_tensor("out_0_dram", (TOK, D), F32, kind="ExternalOutput").ap()
    build(nc, arr, out)
    got = _run(nc, [arrays], core_ids=[0])
    return got.results[0]["out_0_dram"].reshape(B, S, D)
```

```python
from contextlib import ExitStack

import concourse.bass as bass
import numpy as np
from concourse import mybir

ALU = mybir.AluOpType
ACT = mybir.ActivationFunctionType
AX = mybir.AxisListType.X
F32 = mybir.dt.float32
BF16 = mybir.dt.bfloat16
U32 = mybir.dt.uint32
U8 = mybir.dt.uint8

P = 128
B, S, D = 8, 32, 128
SK = 512
TOK = B * S
NJ = TOK // P
BT = B // NJ
BH = B // 2
GATES = (0, 7)
XH, XD = 16, 8
XG = 4
AH, AD = 16, 64
E, F = 8, 512
FC = F // P
ML, MI, MN, MR, MK = 4, 256, 16, 8, 4
MC = MI // P
LR = 4
KC = SK // P
MASKED = -1e30
FLOOR = -1e29

C_ID, C_CB8, C_BLK8, C_CB64, C_BLK64, C_ROT, C_COS, C_SIN, C_CAUSAL, C_HM, C_HM16, C_IOTA, C_NEG, C_SEL = np.cumsum(
    [0, P, P, P, P, P, P, S, S, S, 4, 16, 8, B * KC]).tolist()
C_END = C_SEL + 2 * MN

V_NAMES = [("bq", 1), ("bk", 1), ("bv", 1), ("qw", 1), ("qb", 1), ("kw", 1), ("kb", 1), ("aqw", 1), ("aqb", 1),
           ("akw", 1), ("akb", 1), ("sink", AH), ("b1", E * FC), ("bs1", FC), ("bih", 4), ("bhh", 4),
           ("bout", 1), ("convw", ML * MC * MK), ("convb", ML * MC), ("dtb", ML * MC), ("mD", ML * MC),
           ("alog", ML * MC * MN), ("wib", FC)]
V_AT = dict(zip([n for n, _ in V_NAMES], np.cumsum([0] + [w for _, w in V_NAMES]).tolist()))
V_END = sum(w for _, w in V_NAMES)

R_NAMES = [("bo", D), ("projb", D), ("bs2", D), ("wob", D), ("gateb", E), ("lnw", ML * D), ("lnb", ML * D)]
R_AT = dict(zip([n for n, _ in R_NAMES], np.cumsum([0] + [w for _, w in R_NAMES]).tolist()))
R_END = sum(w for _, w in R_NAMES)


def shape_constants():
    p = np.arange(P)
    c = np.zeros((P, C_END), np.float32)
    c[:, C_ID:C_ID + P] = np.eye(P)
    for size, centre, mean in ((XD, C_CB8, C_BLK8), (AD, C_CB64, C_BLK64)):
        same = (p[:, None] // size == p[None, :] // size) / size
        c[:, mean:mean + P] = same
        c[:, centre:centre + P] = np.eye(P) - same
    half = AD // 2
    for m in range(P):
        k = m + half if m % AD < half else m - half
        c[k, C_ROT + m] = -1.0 if m % AD < half else 1.0
    freq = (1.0 / np.float32(10000.0) ** (np.arange(0, AD, 2, dtype=np.float32) / AD)).astype(np.float32)
    angle = np.arange(S, dtype=np.float32)[None, :] * freq[(p % half)][:, None]
    c[:, C_COS:C_COS + S] = np.cos(angle)
    c[:, C_SIN:C_SIN + S] = np.sin(angle)
    c[:, C_CAUSAL:C_CAUSAL + S] = np.where(np.arange(S)[None, :] <= (p % S)[:, None], 0.0, MASKED)
    c[:, C_HM:C_HM + 4] = (p[:, None] % 32) // XD == np.arange(4)[None, :]
    c[:, C_HM16:C_HM16 + 16] = (p[:, None] // XD == np.arange(16)[None, :]) * np.float32(XD ** -0.5)
    c[:, C_IOTA:C_IOTA + 8] = np.arange(8)[None, :]
    c[:, C_NEG:C_NEG + B * KC] = -1.0 * (p[:, None] == np.arange(B * KC)[None, :] // KC)
    c[:, C_SEL:C_SEL + 2 * MN] = (p[:, None] % 32 == np.arange(32)[None, :]) * (p[:, None] < 96)
    return c


LOG1P = [2.000000007681758, 0.6666632164140144, 0.40024595229818943, 0.2796515775679465, 0.28157778313522575]

def pat(t, dims, off=0):
    return bass.AP(tensor=t.tensor, offset=t.offset + off, ap=[list(t.ap[0])] + [list(d) for d in dims])


class Steps:

    def __init__(self, eng, sem):
        self.eng, self.sem, self.n, self.base = eng, sem, 0, 0

    def __call__(self, ins):
        self.mark(ins)
        self.sync()

    def mark(self, ins):
        ins.then_inc(self.sem, 1)
        self.n += 1

    def sync(self):
        self.eng.wait_ge(self.sem, self.base + self.n)


def build(nc, arr, out, upto=99):
    with ExitStack() as ctx:
        def sb(name, shape, dt=F32):
            return ctx.enter_context(nc.sbuf_tensor(name, shape, dt))

        sem = {}

        def sems(*names):
            for n in names:
                sem[n] = ctx.enter_context(nc.semaphore(n))

        cst = sb("cst", [P, C_END])
        vec = sb("vec", [P, V_END])
        rows = sb("rows", [P, R_END])
        wx = sb("wx", [P, 4 * D])
        ident = cst[:, C_ID:C_ID + P]

        def v(name, i=0, n=1):
            return vec[:, V_AT[name] + i:V_AT[name] + i + n]

        def r(name, i=0, n=D):
            return rows[:, R_AT[name] + i:R_AT[name] + i + n]

        wqkv = sb("wqkv", [P, 3 * AH * AD])
        projT = sb("projT", [P, AH * AD])
        w1 = sb("w1", [P, E * F])
        w2 = sb("w2", [P, E * F])
        ws = sb("ws", [P, 2 * F])
        wg = sb("wg", [P, E])
        b2 = sb("b2", [E, D])
        x_in = sb("x_in", [P, NJ, D])
        xres = sb("xres", [P, NJ, D])
        xbias = sb("xbias", [P, NJ, D])
        xn = sb("xn", [P, NJ, D])
        xnT = sb("xnT", [P, TOK])
        bn = sb("bn", [P, NJ, 6])
        mv = sb("mv", [P, NJ, 2])
        lnv = sb("lnv", [P, NJ])
        rs = sb("rs", [P, NJ])

        ctxT = sb("ctxT", [P, B * SK])
        kT = sb("kT", [P, B * SK])
        vx = sb("vx", [P, B * KC, D])
        qblk = sb("qblk", [P, XG, B, 4, S])
        T = sb("T", [P, 16, 512])
        maskb = sb("maskb", [P, B * SK], BF16)
        mask8 = T[:, 12:14, :].rearrange("p n k -> p (n k)").bitcast(U8)
        xw = sb("xw", [P, 2 * D + 2])
        oT = sb("oT", [P, TOK])
        xmax = sb("xmax", [P, B * XG])
        xneg = sb("xneg", [P, B * XG])
        xz = sb("xz", [P, B * XG])
        xrz = sb("xrz", [P, B * XG])

        eps5 = sb("eps5", [P, 1])
        eps6 = sb("eps6", [P, 1])
        wmean = sb("wmean", [P, 2 * AH])
        am = sb("am", [P, NJ, AH])
        asink = sb("asink", [P, NJ, AH])
        az = sb("az", [P, NJ, AH])
        lg = sb("lg", [P, NJ, E])
        gm = sb("gm", [P, NJ])
        gz = sb("gz", [P, NJ])
        m8 = sb("m8", [P, NJ, E])
        i8 = sb("i8", [P, NJ, E], U32)
        i8f = sb("i8f", [P, NJ, E])
        gw = sb("gw", [P, NJ, 2])
        cw = sb("cw", [P, 3, NJ, E])
        cwT = sb("cwT", [E * LR, TOK])
        facc = sb("facc", [P, NJ, D])
        avals = vx[:, :, :].rearrange("p n d -> p (n d)")[:, 0:NJ * AH * AD].rearrange("p (j n) -> p j n", j=NJ)
        aprobT = bass.AP(tensor=qblk[:, 0, 0, 0, 0:1].tensor, offset=0, ap=[[XG * B * 4 * S, P], [AH * P, NJ], [P, AH], [1, P]])
        lw = sb("lw", [P, 3 * 4 * D + 3 * D])
        bf = [t.bitcast(BF16) for t in (kT[:, :], qblk[:, :, :, :, :].rearrange("p a b c d -> p (a b c d)"),
                                        vx[:, :, :].rearrange("p n d -> p (n d)"))]
        half_b = B * SK
        ks = [bf[0][:, 0:half_b], bf[0][:, half_b:2 * half_b], maskb[:, :]]
        vs = [bf[1][:, 0:half_b], bf[1][:, half_b:2 * half_b], bf[2][:, 0:half_b]]
        lsp = sb("lsp", [P, 3, 9 * D], BF16)
        gbias = sb("gbias", [P, 4])
        gx = sb("gx", [P, S + 1, 3, 4, B], BF16)
        gx32, gxrest = (T[:, i:i + 2, :].rearrange("p a (t g b) -> p (a t) (g b)", g=4, b=B) for i in (0, 2))
        identb = T[:, 14, :].bitcast(BF16)[:, 0:P]
        yT = sb("yT", [P, B, S])
        ones = sb("ones", [P, P], BF16)
        hsp = sb("hsp", [P, 2, 3, BH], BF16)
        asp = sb("asp", [P, 2, 3, BH], BF16)
        esp = sb("esp", [P, 2, 3, BH * KC], BF16)
        negmax = sb("negmax", [P, 2, BH * KC], BF16)
        (h32, a32, c2, tanhc, fc2, ig, hrest, arest, mc, zs, rz, oh, opre) = [
            sb(n, [P, 2, BH]) for n in ("h32", "a32", "c2", "tanhc", "fc2", "ig", "hrest", "arest", "mc", "zs", "rz",
                                        "oh", "opre")]
        m1 = sb("m1", [BH, 2])
        (gsum, gact, ssum, e32, erest) = [sb(n, [P, 2, BH * KC]) for n in ("gsum", "gact", "ssum", "e32", "erest")]
        MNP = MN // 2
        mw = w1[:, 0:ML * (2 * MI + MC * (6 * MN + MR) + MC * D)]
        m_in = mw[:, 0:ML * 2 * MI]
        m_x = mw[:, ML * 2 * MI:ML * 2 * MI + ML * MC * (6 * MN + MR)]
        m_out = mw[:, ML * 2 * MI + ML * MC * (6 * MN + MR):]
        dtw = projT[0:MR, 0:ML * MI]
        decay = [ctxT[:, :], kT[:, :]]
        state = [qblk[:, :, :, :, :].rearrange("p a b c d -> p (a b c d)"), vx[:, :, :].rearrange("p n d -> p (n d)")]
        up = sb("up", [P, MC, B, S + MK - 1])
        aneg = sb("aneg", [P, ML * MC * MN])
        bcs = sb("bcs", [6 * MN, TOK], BF16)
        sel = sb("sel", [6 * MN, 2 * MN], BF16)
        dts = sb("dts", [MR, TOK])
        two = sb("two", [P, 1])
        fw = wqkv[:, 0:E + E * LR + F + FC * D]
        lb = wqkv[0:E * LR, 2048:2048 + F]
        oneh = sb("oneh", [P, NJ, E])
        loraa = T[:, 14, 0:NJ * E * LR].rearrange("p (j n) -> p j n", j=NJ)
        bank = [ctx.enter_context(nc.psum_tensor(f"bank{i}", [P, 512], F32)) for i in range(8)]

        sems("d_par", "d_rows", "d_x", "d_mask", "d_out",
             "pe_step", "act_step", "dve_step", "pool_step",
             "ln_var", "ln_rstd", "ln_xn", "ln_tr", "ln_xT",
             "xw_ps", "xw_sb", "k_proj", "k_sq", "k_var", "k_rstd", "k_hat", "k_done", "v_proj", "v_evac",
             "eps_ready", "mask_ready", "qblk_ready", "x_score", "x_max", "x_exp", "x_norm", "x_tr", "x_pt", "x_pv",
             "x_oT", "x_o", "xb_ready", "x_res")
        d_ctx = [ctx.enter_context(nc.semaphore(f"d_ctx{b}")) for b in range(B)]

        sems("d_attn", "d_ffn",
             "a_wmean", "a_wc", "a_proj", "a_sq", "a_var", "a_rstd", "a_z0", "a_z", "a_rot", "a_t2", "a_rope",
             "a_vproj", "a_vev", "a_score", "a_sub", "a_exp", "a_zero", "a_pt", "a_pv", "a_oT", "a_oTd", "a_o",
             "f_gate", "f_sub", "f_exp", "f_cw", "f_cwps", "f_cwT", "f_h", "f_act", "f_y", "f_acc", "f_b2")
        sems("d_lw", "l_w", "l_kv", "l_hi", "l_rest", "l_split", "l_gbias", "l_gxps", "l_gx", "l_gxlow", "l_zero",
             "g_ps", "g_sum", "g_act", "c_new", "c_tanh", "h_hi", "h_mid", "h_lo", "s_hi", "m_c", "m_t", "m_d", "s_ps",
             "s_sum", "e_hi", "e_32", "e_mid", "e_lo", "oh_ps", "z_ps", "v_ps", "o_pre", "at_hi", "at_32", "at_mid",
             "at_lo", "y_st", "y_tr")
        sems("d_late", "m_const", "m_uz", "m_up", "m_zs", "m_conv", "m_convp", "m_us", "m_bc",
             "m_dts", "m_bcs", "m_dps", "m_e", "m_delta", "m_bps", "m_cps", "m_bsb", "m_csb", "m_dA", "m_dbu0",
             "m_dbu1", "m_scan0", "m_scan1", "m_hc0", "m_hc1", "m_y", "m_ys", "m_o",
             "r_gate", "r_a", "r_am", "r_amps", "r_amT", "r_h", "r_act", "r_o")
        N_OUT = 6
        LSTM_STEPS = 26
        block = ctx.enter_context(nc.Block())

        def lstm_loop(engine, half, steps=None):
            def turn(t):
                half(main=(1, t), out=(0, t), gates=(0, t + 1))
                half(main=(0, t + 1), out=(1, t), gates=(1, t + 1))

            half(gates=(0, 0))
            half(main=(0, 0), gates=(1, 0))
            turn(0)
            before = steps.n if steps else 0
            with engine.Fori(0, (S - 2) // 2) as i:
                if steps:
                    steps.n, steps.base = 0, before + i * (2 * LSTM_STEPS)
                turn(i * 2 + 1)
                turn(i * 2 + 2)
            if steps:
                assert steps.n == 2 * LSTM_STEPS
                steps.n, steps.base = before + (S - 2) * LSTM_STEPS, 0
            half(main=(1, S - 1), out=(0, S - 1))
            half(out=(1, S - 1))

        def nth(stream, t):
            return t * 2 + (stream + 1)

        def both(t):
            return t.rearrange("p (n k) -> p n k", n=2)

        def pairs(t, i):
            return both(t[:, i * 2 * TOK:(i + 1) * 2 * TOK])

        def over_pair(t):
            return pat(t, [[0, 2], [1, TOK]])

        def conv(eng, step, l, ch):
            acc = T[:, 0, ch * TOK:(ch + 1) * TOK].rearrange("p (b t) -> p b t", b=B)
            at = (l * MC + ch) * MK
            eng.wait_ge(sem["m_up"], l + 1)
            step(eng.tensor_scalar(acc, up[:, ch, :, 0:S], v("convw", at), v("convb", l * MC + ch), ALU.mult, ALU.add))
            for k in range(1, MK):
                if ch == 0:
                    ins = eng.scalar_tensor_tensor(out=acc, in0=up[:, ch, :, k:k + S], scalar=v("convw", at + k), in1=acc,
                                                   op0=ALU.mult, op1=ALU.add)
                else:
                    tap = T[:, 14, TOK:2 * TOK].rearrange("p (b t) -> p b t", b=B)
                    step(eng.tensor_scalar(tap, up[:, ch, :, k:k + S], v("convw", at + k), 0.0, ALU.mult, ALU.add))
                    ins = eng.tensor_tensor(acc, acc, tap, ALU.add)
                if k < MK - 1:
                    step(ins)
            return ins

        @block.sync
        def _(sp):
            sp.dma_start(x_in[:, :, :], arr["x"].rearrange("(j p) d -> p j d", p=P)).then_inc(sem["d_x"], 16)
            sp.dma_start(cst[:, :], arr["cst"]).then_inc(sem["d_par"], 16)
            sp.dma_start(wx[:, :], arr["wx"]).then_inc(sem["d_par"], 16)
            for b in range(B):
                sp.dma_start(ctxT[:, b * SK:(b + 1) * SK], arr["ctxT"][:, b * SK:(b + 1) * SK]) \
                  .then_inc(d_ctx[b], 16)
            sp.dma_start(wg[:, :], arr["wg"]).then_inc(sem["d_ffn"], 16)
            sp.dma_start(b2[:, :], arr["b2"]).then_inc(sem["d_ffn"], 16)
            sp.dma_start(ws[:, :], arr["ws"]).then_inc(sem["d_ffn"], 16)
            sp.dma_start(w1[:, :], arr["w1"]).then_inc(sem["d_ffn"], 16)
            sp.dma_start(w2[:, :], arr["w2"]).then_inc(sem["d_ffn"], 16)
            sp.dma_start(lw[:, :], arr["lw"]).then_inc(sem["d_lw"], 16)
            sp.wait_ge(sem["a_o"], 1)
            sp.dma_start(dtw, arr["dtw"]).then_inc(sem["d_late"], 16)
            sp.dma_start(fw, arr["fw"]).then_inc(sem["d_late"], 16)
            sp.dma_start(lb, arr["lb"]).then_inc(sem["d_late"], 16)
            sp.wait_ge(sem["f_y"], E + 1)
            sp.dma_start(mw, arr["mw"]).then_inc(sem["d_late"], 16)
            sp.wait_ge(sem["x_res"], N_OUT)
            sp.dma_start(out.rearrange("(j p) d -> p j d", p=P), xres[:, :, :]).then_inc(sem["d_out"], 16)
            sp.wait_ge(sem["d_out"], 16)

        @block.gpsimd
        def _(pool):
            step = Steps(pool, sem["pool_step"])
            pool.wait_ge(sem["d_mask"], 16)
            pool.tensor_scalar(maskb[:, :], mask8[:, :], -MASKED, MASKED, ALU.mult, ALU.add) \
                .then_inc(sem["mask_ready"], 1)
            pool.wait_ge(sem["d_par"], 48)
            for s in range(1 + B):
                pool.wait_ge(sem["k_hat"], s + 1)
                if s == 0:
                    ins = pool.tensor_scalar(T[:, 10, 0:TOK], T[:, 8, 0:TOK], 1.0, v("qb"), ALU.mult, ALU.add)
                else:
                    ins = pool.tensor_scalar(kT[:, (s - 1) * SK:s * SK], T[:, 8 + s % 2, :], 1.0, v("kb"),
                                             ALU.mult, ALU.add)
                ins.then_inc(sem["k_done"], 1)
            pool.wait_ge(sem["d_rows"], 16)
            pool.wait_ge(sem["d_x"], 16)
            pool.tensor_tensor(xbias[:, :, :], x_in[:, :, :], pat(r("bo"), [[0, NJ], [1, D]]), ALU.add) \
                .then_inc(sem["xb_ready"], 1)

            pool.wait_ge(sem["x_res"], 1)
            pool.tensor_tensor(xbias[:, :, :], xres[:, :, :], pat(r("projb"), [[0, NJ], [1, D]]), ALU.add) \
                .then_inc(sem["xb_ready"], 1)
            pool.wait_ge(sem["a_wmean"], 1)
            wqk = wqkv[:, 0:2 * AH * AD].rearrange("p (h d) -> p h d", d=AD)
            pool.tensor_tensor(wqk, wqk, pat(wmean[:, :], [[1, 2 * AH], [0, AD]]), ALU.subtract) \
                .then_inc(sem["a_wc"], 1)
            pool.memset(qblk[:, :, :, :, :], 0.0).then_inc(sem["a_zero"], 1)
            for m in range(8):
                pool.wait_ge(sem["a_z0"], m + 1)
                if m >= 2:
                    pool.wait_ge(sem["a_t2"], m - 1)
                pool.tensor_scalar(T[:, 8 + m % 2, :], T[:, 6 + m % 2, :], 1.0, v("aqb" if m < 4 else "akb"),
                                   ALU.mult, ALU.add).then_inc(sem["a_z"], 1)

            pool.wait_ge(sem["x_res"], 2)
            step(pool.tensor_scalar(T[:, 15, 0:D], r("bs2"), 0.1, 0.0, ALU.mult, ALU.add))
            pool.tensor_tensor(facc[:, :, :], xres[:, :, :], pat(T[:, 15, :], [[0, NJ], [1, D]]), ALU.add) \
                .then_inc(sem["xb_ready"], 1)

            pool.wait_ge(sem["d_lw"], 16)
            for at, end, by in ((7, 8, 2.0), (8, 11, 0.5), (12, 13, 0.5)):
                pool.tensor_scalar(lw[:, at * D:end * D], lw[:, at * D:end * D], by, 0.0, ALU.mult, ALU.add) \
                    .then_inc(sem["l_w"], 1)
            pool.memset(gx[:, S, :, :, :], 0.0).then_inc(sem["l_zero"], 1)
            pool.tensor_scalar(identb, ident, 1.0, 0.0, ALU.mult, ALU.add).then_inc(sem["l_zero"], 1)
            for i in range(2 * B + 1):
                if i < 2 * B:
                    b = i // 2
                    parts = [t[:, b * SK:(b + 1) * SK] for t in (vs if i % 2 else ks)]
                    rest = T[:, 8 + i % 2, :]
                else:
                    parts = [lsp[:, k, :] for k in range(3)]
                    rest = T[:, 10:13, :].rearrange("p n d -> p (n d)")[:, 0:9 * D]
                pool.wait_ge(sem["l_rest"], i + 1)
                step(pool.tensor_scalar(parts[1], rest, 1.0, 0.0, ALU.mult, ALU.add))
                pool.tensor_tensor(parts[2], rest, parts[1], ALU.subtract).then_inc(sem["l_split"], 1)

            pool.wait_ge(sem["x_res"], 4)
            for ch in range(MC):
                pool.memset(decay[ch].rearrange("p (n s) -> p n s", s=S)[:, :, 0], 0.0).then_inc(sem["m_const"], 1)
            for l in range(ML):
                conv(pool, step, l, 1).then_inc(sem["m_convp"], 1)
                pool.wait_ge(sem["m_delta"], l + 1)
                for i in range(MNP + 1):
                    if i < MNP:
                        if l:
                            pool.wait_ge(sem["m_y"], l)
                        pool.wait_ge(sem["m_bsb"], l * MNP + i + 1)
                        pool.tensor_tensor(pairs(state[1], i), over_pair(T[:, 7, TOK:2 * TOK]), both(T[:, 8 + i % 2, :]),
                                           ALU.mult).then_inc(sem["m_dbu1"], 1)
                    if i >= 1:
                        pool.wait_ge(sem["m_csb"], l * MNP + i)
                        pool.wait_ge(sem["m_scan1"], l * MNP + i)
                        pool.tensor_tensor(pairs(state[1], i - 1), pairs(state[1], i - 1), both(T[:, 10 + (i - 1) % 2, :]),
                                           ALU.mult).then_inc(sem["m_hc1"], 1)

        @block.scalar
        def _(act):
            step = Steps(act, sem["act_step"])
            act.dma_start(vec[:, :], arr["vec"]).then_inc(sem["d_par"], 16)
            act.dma_start(mask8[:, :], bass.AP(tensor=arr["mask"].tensor, offset=0, ap=[[0, P], [1, B * SK]])) \
               .then_inc(sem["d_mask"], 16)
            act.dma_start(rows[:, :], arr["rows"]).then_inc(sem["d_rows"], 16)
            act.dma_start(wqkv[:, :], arr["qkvT"]).then_inc(sem["d_attn"], 16)
            act.dma_start(projT[:, :], arr["projT"]).then_inc(sem["d_attn"], 16)

            def ln_rstd(n):
                act.wait_ge(sem["ln_var"], n + 1)
                step(act.activation(lnv[:, :], mv[:, :, 1], ACT.Ln, bias=eps5[:, :]))
                act.activation(rs[:, :], lnv[:, :], ACT.Exp, scale=-0.5).then_inc(sem["ln_rstd"], 1)

            act.preload_act_table_set("natural_log_exp_and_others")
            act.wait_ge(sem["eps_ready"], 2)
            act.wait_ge(sem["d_par"], 48)
            ln_rstd(0)

            def k_square(s):
                w, p = (TOK if s == 0 else SK), s % 2
                act.wait_ge(sem["k_proj"], s + 1)
                if s == 0:
                    act.wait_ge(sem["xw_sb"], 1)
                if s >= 2:
                    act.wait_ge(sem["k_hat"], s - 1)
                bias = xw[:, 2 * D:2 * D + 1] if s == 0 else xw[:, 2 * D + 1:2 * D + 2]
                act.activation(T[:, p, 0:w], bank[p][:, 0:w], ACT.Identity, bias=bias)
                act.activation(T[:, 2 + p, 0:w], bank[p][:, 0:w], ACT.Square, bias=bias).then_inc(sem["k_sq"], 1)

            def k_rstd(s):
                w, p = (TOK if s == 0 else SK), s % 2
                act.wait_ge(sem["k_var"], s + 1)
                step(act.activation(T[:, 4 + p, 0:w], bank[2 + p][:, 0:w], ACT.Ln, bias=eps6[:, :]))
                act.activation(T[:, 6 + p, 0:w], T[:, 4 + p, 0:w], ACT.Exp, scale=-0.5).then_inc(sem["k_rstd"], 1)

            for s in range(2 + B):
                if s <= B:
                    k_square(s)
                if s >= 1:
                    k_rstd(s - 1)

            def x_exp(i):
                act.wait_ge(sem["x_max"], i + 1)
                if i >= 2:
                    act.wait_ge(sem["x_norm"], i - 1)
                act.activation(T[:, 2 + i % 2, :], T[:, i % 2, :], ACT.Exp, bias=xneg[:, i:i + 1],
                               accum_out=xz[:, i:i + 1]).then_inc(sem["x_exp"], 1)

            def x_copy_pt(i):
                act.wait_ge(sem["x_tr"], i + 1)
                if i >= 2:
                    act.wait_ge(sem["x_pv"], i - 1)
                act.activation(T[:, 6 + i % 2, :], bank[2 + i % 2][:, :], ACT.Copy).then_inc(sem["x_pt"], 1)

            for i in range(B * XG + 2):
                if i < B * XG:
                    x_exp(i)
                if i >= 2:
                    x_copy_pt(i - 2)

            ln_rstd(1)

            def a_square(m):
                act.wait_ge(sem["a_proj"], m + 1)
                if m >= 2:
                    act.wait_ge(sem["a_var"], m - 1)
                act.activation(T[:, m % 2, :], bank[m % 2][:, :], ACT.Square).then_inc(sem["a_sq"], 1)

            def a_rstd(m):
                act.wait_ge(sem["a_var"], m + 1)
                step(act.activation(T[:, 2 + m % 2, :], bank[2 + m % 2][:, :], ACT.Ln, bias=eps5[:, :]))
                if m >= 2:
                    act.wait_ge(sem["a_z0"], m - 1)
                act.activation(T[:, 4 + m % 2, :], T[:, 2 + m % 2, :], ACT.Exp, scale=-0.5).then_inc(sem["a_rstd"], 1)

            def a_vev(n):
                act.wait_ge(sem["a_vproj"], n + 1)
                act.activation(avals[:, n // 2, (n % 2) * 512:(n % 2) * 512 + 512], bank[6][:, :], ACT.Copy) \
                   .then_inc(sem["a_vev"], 1)

            for m in range(9):
                if m < 8:
                    a_square(m)
                if m >= 1:
                    a_rstd(m - 1)
                if m >= 5:
                    a_vev(m - 5)
            for j in range(NJ):
                act.wait_ge(sem["a_sub"], j + 1)
                act.activation(T[:, 4 + j, :], T[:, 2 + j, :], ACT.Exp)
                act.activation(asink[:, j, :], asink[:, j, :], ACT.Exp).then_inc(sem["a_exp"], 1)
            for j in range(NJ):
                act.wait_ge(sem["a_pv"], j + 1)
                act.activation(T[:, 8 + 2 * j, :], bank[2 + 2 * j][:, :], ACT.Copy).then_inc(sem["a_oT"], 1)

            def l_high(i):
                act.wait_ge(sem["l_kv"], i + 1)
                at = i // 2 * SK
                act.activation((vs if i % 2 else ks)[0][:, at:at + SK], bank[6 + i % 2][:, :], ACT.Copy) \
                   .then_inc(sem["l_hi"], 1)

            ln_rstd(2)
            act.wait_ge(sem["f_sub"], 1)
            act.activation(lg[:, :, :], lg[:, :, :], ACT.Exp).then_inc(sem["f_exp"], 1)
            act.preload_act_table_set("silu_and_others")
            for e in range(E + 1):
                for q in range(2):
                    act.wait_ge(sem["f_h"], 2 * e + q + 1)
                    if e >= 2:
                        act.wait_ge(sem["f_y"], e - 1)
                    for fc in (2 * q, 2 * q + 1):
                        half = slice((fc % 2) * TOK, (fc % 2) * TOK + TOK)
                        bias = v("b1", e * FC + fc) if e < E else v("bs1", fc)
                        ins = act.activation(T[:, 2 * (e % 2) + q, half], bank[2 * (e % 2) + q][:, half], ACT.Silu,
                                             bias=bias)
                    ins.then_inc(sem["f_act"], 1)
                if e >= 2:
                    l_high(2 * (e - 2))
                    l_high(2 * (e - 2) + 1)
            l_high(2 * B - 2)
            l_high(2 * B - 1)
            act.wait_ge(sem["l_w"], 3)
            act.activation(lsp[:, 0, :], lw[:, 4 * D:13 * D], ACT.Copy).then_inc(sem["l_hi"], 1)
            act.preload_act_table_set("natural_log_exp_and_others")

            ln_rstd(3)
            act.wait_ge(sem["l_gbias"], 1)
            act.wait_ge(sem["l_gxps"], 1)

            def to_time(first):
                at = first.ap[1][0]
                return pat(first, [[1, B], [at, S]])

            for g in range(4):
                share = bank[g // 2][:, (g % 2) * TOK:(g % 2 + 1) * TOK].rearrange("p (b t) -> p b t", b=B)
                for to in (gx32[:, 0:1, g * B:(g + 1) * B], gx[:, 0:1, 0, g, :]):
                    ins = act.activation(to_time(to), share, ACT.Identity, bias=gbias[:, g:g + 1],
                                         scale=2.0 if g == 3 else 1.0)
                if g % 2:
                    ins.then_inc(sem["l_gx"], 1)
            act.preload_act_table_set("exp_and_others")

            def half(main=None, out=None, gates=None):
                if out:
                    g, t = out
                    act.wait_ge(sem["o_pre"], nth(g, t))
                    act.activation(asp[:, g, 0, :], opre[:, g, :], ACT.Tanh).then_inc(sem["at_hi"], 1)
                    act.activation(a32[:, g, :], opre[:, g, :], ACT.Tanh).then_inc(sem["at_32"], 1)
                    t = bass.ds(t, 1)
                    act.activation(yT[:, g * BH:(g + 1) * BH, t].rearrange("p b t -> p (b t)"), opre[:, g, :], ACT.Tanh) \
                       .then_inc(sem["y_st"], 1)
                if gates:
                    g, t = gates
                    act.wait_ge(sem["g_sum"], nth(g, t))
                    act.activation(gact[:, g, :], gsum[:, g, :], ACT.Tanh, scale=0.5).then_inc(sem["g_act"], 1)
                if main:
                    g, t = main
                    act.wait_ge(sem["s_sum"], nth(g, t))
                    act.activation(esp[:, g, 0, :], ssum[:, g, :], ACT.Exp, scale=0.5).then_inc(sem["e_hi"], 1)
                    act.activation(e32[:, g, :], ssum[:, g, :], ACT.Exp, scale=0.5).then_inc(sem["e_32"], 1)
                if gates:
                    g, t = gates
                    act.wait_ge(sem["c_new"], nth(g, t))
                    act.activation(tanhc[:, g, :], c2[:, g, :], ACT.Tanh, scale=0.5).then_inc(sem["c_tanh"], 1)

            lstm_loop(act, half)

            act.preload_act_table_set("natural_log_exp_and_others")
            ln_rstd(4)
            step(act.activation(aneg[:, :], v("alog", 0, ML * MC * MN), ACT.Exp))
            step(act.activation(aneg[:, :], aneg[:, :], ACT.Copy, scale=-1.0))
            for l in range(ML):
                act.preload_act_table_set("silu_and_others")
                act.wait_ge(sem["m_uz"], l + 1)
                act.wait_ge(sem["m_const"], MC + 3)
                act.activation(up[:, :, :, MK - 1:], bank[0][:, :].rearrange("p (c b t) -> p c b t", c=MC, b=B), ACT.Copy) \
                   .then_inc(sem["m_up"], 1)
                act.activation(T[:, 2, :], bank[1][:, :], ACT.Silu).then_inc(sem["m_zs"], 1)
                act.wait_ge(sem["m_conv"], l + 1)
                act.wait_ge(sem["m_convp"], l + 1)
                act.activation(T[:, 1, :], T[:, 0, :], ACT.Silu).then_inc(sem["m_us"], 1)
                act.preload_act_table_set("natural_log_exp_and_others")
                act.wait_ge(sem["m_dps"], l + 1)
                for ch in range(MC):
                    half = slice(ch * TOK, (ch + 1) * TOK)
                    step.mark(act.activation(T[:, 3, half], bank[4][:, half], ACT.Abs, bias=v("dtb", l * MC + ch)))
                    step.mark(act.activation(T[:, 12, half], bank[4][:, half], ACT.Relu, bias=v("dtb", l * MC + ch)))
                step.sync()
                step(act.activation(T[:, 4, :], T[:, 3, :], ACT.Exp, scale=-1.0))
                step(act.activation(T[:, 5, :], T[:, 4, :], ACT.Ln, bias=two[:, :]))
                act.activation(T[:, 5, :], T[:, 5, :], ACT.Exp, scale=-1.0).then_inc(sem["m_e"], 1)
                act.wait_ge(sem["m_delta"], l + 1)
                for i in range(MNP):
                    n = l * MNP + i
                    act.wait_ge(sem["m_bps"], n + 1)
                    if n >= 2:
                        act.wait_ge(sem["m_dbu0"], n - 1)
                        act.wait_ge(sem["m_dbu1"], n - 1)
                    act.activation(T[:, 8 + i % 2, :], bank[2 + i % 2][:, :], ACT.Copy).then_inc(sem["m_bsb"], 1)
                    for ch in range(MC):
                        for k in range(2):
                            at = (l * MC + ch) * MN + 2 * i + k
                            seqs = decay[ch][:, (2 * i + k) * TOK:(2 * i + k + 1) * TOK].rearrange("p (b t) -> p b t", b=B)
                            ins = act.activation(seqs[:, :, 1:], T[:, 6, ch * TOK:(ch + 1) * TOK]
                                                 .rearrange("p (b t) -> p b t", b=B)[:, :, 1:],
                                                 ACT.Exp, scale=aneg[:, at:at + 1])
                        ins.then_inc(sem["m_dA"], 1)
                    act.wait_ge(sem["m_cps"], n + 1)
                    if n >= 2:
                        act.wait_ge(sem["m_hc0"], n - 1)
                        act.wait_ge(sem["m_hc1"], n - 1)
                    act.activation(T[:, 10 + i % 2, :], bank[5 + i % 2][:, :], ACT.Copy).then_inc(sem["m_csb"], 1)
                ln_rstd(5 + l)

            ln_rstd(5 + ML)
            act.wait_ge(sem["f_sub"], 2)
            act.activation(lg[:, :, :], lg[:, :, :], ACT.Exp).then_inc(sem["f_exp"], 1)
            for fc in range(FC):
                half = slice((fc % 2) * TOK, (fc % 2) * TOK + TOK)
                act.wait_ge(sem["r_h"], fc + 1)
                act.activation(T[:, fc // 2, half], bank[fc][:, 0:TOK], ACT.Relu, bias=v("wib", fc)) \
                   .then_inc(sem["r_act"], 1)

        @block.vector
        def _(dve):
            step = Steps(dve, sem["dve_step"])
            dve.memset(eps5[:, :], 1e-5).then_inc(sem["eps_ready"], 1)
            dve.memset(eps6[:, :], 1e-6).then_inc(sem["eps_ready"], 1)

            def layernorm(n, src, affine=None):
                for j in range(NJ):
                    step.mark(dve.bn_stats(bn[:, j, :], src[:, j, :]))
                step.sync()
                for j in range(NJ):
                    ins = dve.bn_aggr(mv[:, j, :], bn[:, j, :])
                    if j < NJ - 1:
                        step.mark(ins)
                ins.then_inc(sem["ln_var"], 1)
                dve.wait_ge(sem["ln_rstd"], n + 1)
                step.sync()
                for j in range(NJ):
                    ins = dve.tensor_scalar(xn[:, j, :], src[:, j, :], mv[:, j, 0:1], rs[:, j:j + 1],
                                            ALU.subtract, ALU.mult)
                    if affine is not None:
                        step.mark(ins)
                if affine is not None:
                    step.sync()
                    step(dve.tensor_tensor(xn[:, :, :], xn[:, :, :], pat(r("lnw", affine * D), [[0, NJ], [1, D]]), ALU.mult))
                    ins = dve.tensor_tensor(xn[:, :, :], xn[:, :, :], pat(r("lnb", affine * D), [[0, NJ], [1, D]]), ALU.add)
                ins.then_inc(sem["ln_xn"], 1)
                dve.wait_ge(sem["ln_tr"], n + 1)
                dve.tensor_copy(xnT[:, :], bank[7][:, 0:TOK]).then_inc(sem["ln_xT"], 1)

            step(dve.memset(qblk[:, :, :, :, :], 0.0))
            dve.wait_ge(sem["d_x"], 16)
            layernorm(0, x_in)
            dve.wait_ge(sem["xw_ps"], 1)
            dve.tensor_copy(xw[:, :], bank[6][:, 0:2 * D + 2]).then_inc(sem["xw_sb"], 1)
            dve.wait_ge(sem["d_par"], 48)

            def k_hat(s):
                w, p = (TOK if s == 0 else SK), s % 2
                dve.wait_ge(sem["k_rstd"], s + 1)
                if s >= 2:
                    dve.wait_ge(sem["k_done"], s - 1)
                dve.scalar_tensor_tensor(out=T[:, 8 + p, 0:w], in0=T[:, p, 0:w], scalar=v("qw" if s == 0 else "kw"),
                                         in1=T[:, 6 + p, 0:w], op0=ALU.mult, op1=ALU.mult) \
                   .then_inc(sem["k_hat"], 1)

            def v_evac(b):
                dve.wait_ge(sem["v_proj"], b + 1)
                dve.tensor_copy(pat(vx[:, b * KC, :], [[1, SK]]), bank[4 + b % 2][:, :]).then_inc(sem["v_evac"], 1)

            def q_blocks():
                dve.wait_ge(sem["k_done"], 1)
                for h in range(XH):
                    ins = dve.tensor_scalar(qblk[:, h // 4, :, h % 4, :], T[:, 10, 0:TOK].rearrange("p (b s) -> p b s", b=B),
                                            cst[:, C_HM16 + h:C_HM16 + h + 1], None, ALU.mult)
                ins.then_inc(sem["qblk_ready"], 1)

            for s in range(1 + B):
                k_hat(s)
                if s == 1:
                    q_blocks()
                if s >= 1:
                    v_evac(s - 1)

            def x_max(i):
                b = i // XG
                if i == 0:
                    dve.wait_ge(sem["mask_ready"], 1)
                dve.wait_ge(sem["x_score"], i + 1)
                if i >= 2:
                    dve.wait_ge(sem["x_exp"], i - 1)
                step(dve.tensor_tensor_reduce(T[:, i % 2, :], bank[i % 2][:, :], maskb[:, b * SK:(b + 1) * SK],
                                              1.0, FLOOR, ALU.add, ALU.max, xmax[:, i:i + 1]))
                dve.tensor_scalar(xneg[:, i:i + 1], xmax[:, i:i + 1], -1.0, None, ALU.mult) \
                   .then_inc(sem["x_max"], 1)

            def x_norm(i):
                dve.wait_ge(sem["x_exp"], i + 1)
                step(dve.reciprocal(xrz[:, i:i + 1], xz[:, i:i + 1]))
                if i >= 2:
                    dve.wait_ge(sem["x_tr"], i - 1)
                dve.tensor_scalar(T[:, 4 + i % 2, :], T[:, 2 + i % 2, :], xrz[:, i:i + 1], None, ALU.mult) \
                   .then_inc(sem["x_norm"], 1)

            def x_heads(b):
                dve.wait_ge(sem["x_pv"], XG * (b + 1))
                dve.wait_ge(sem["x_oT"], b) if b else None
                o = bank[4 + b % 2]
                step(dve.tensor_tensor(T[:, 8, 0:P].rearrange("p (h q) -> p h q", h=4),
                                       o[:, 0:P].rearrange("p (h q) -> p h q", h=4),
                                       pat(cst[:, C_HM:C_HM + 4], [[1, 4], [0, S]]), ALU.mult))
                dve.tensor_reduce(oT[:, b * S:(b + 1) * S], pat(T[:, 8, :], [[1, S], [S, 4]]), AX, ALU.add) \
                   .then_inc(sem["x_oT"], 1)

            for i in range(B * XG + 4):
                if i < B * XG:
                    x_max(i)
                if 1 <= i <= B * XG:
                    x_norm(i - 1)
                if i >= 4 and (i - 4) % XG == XG - 1:
                    x_heads((i - 4) // XG)
            dve.wait_ge(sem["x_oT"], B)
            dve.tensor_scalar(oT[:, :], oT[:, :], v("bv"), None, ALU.add).then_inc(sem["x_oT"], 1)
            dve.wait_ge(sem["xb_ready"], 1)
            dve.wait_ge(sem["x_o"], 1)
            dve.tensor_tensor(xres[:, :, :], xbias[:, :, :], bank[6][:, 0:TOK].rearrange("p (j d) -> p j d", j=NJ),
                              ALU.add).then_inc(sem["x_res"], 1)

            dve.wait_ge(sem["d_attn"], 32)
            step(dve.tensor_reduce(wmean[:, :], wqkv[:, 0:2 * AH * AD].rearrange("p (h d) -> p h d", d=AD), AX, ALU.add))
            dve.tensor_scalar(wmean[:, :], wmean[:, :], 1.0 / AD, None, ALU.mult).then_inc(sem["a_wmean"], 1)
            dve.wait_ge(sem["x_res"], 1)
            layernorm(1, xres)
            cos = pat(cst[:, C_COS:C_COS + S], [[0, 2 * B], [1, S]])
            sin = pat(cst[:, C_SIN:C_SIN + S], [[0, 2 * B], [1, S]])

            def by_time(t):
                return t.rearrange("p (n s) -> p n s", s=S)

            def a_z0(m):
                dve.wait_ge(sem["a_rstd"], m + 1)
                if m >= 2:
                    dve.wait_ge(sem["a_z"], m - 1)
                dve.scalar_tensor_tensor(out=T[:, 6 + m % 2, :], in0=bank[m % 2][:, :],
                                         scalar=v("aqw" if m < 4 else "akw"), in1=T[:, 4 + m % 2, :],
                                         op0=ALU.mult, op1=ALU.mult).then_inc(sem["a_z0"], 1)

            def a_rope(m):
                p = m % 2
                dve.wait_ge(sem["a_z"], m + 1)
                if m >= 2:
                    dve.wait_ge(sem["a_rope"], m - 1)
                step.mark(dve.tensor_tensor(by_time(T[:, 10 + p, :]), by_time(T[:, 8 + p, :]), cos, ALU.mult))
                dve.wait_ge(sem["a_rot"], m + 1)
                dve.tensor_tensor(by_time(T[:, 12 + p, :]), by_time(bank[4 + p][:, :]), sin, ALU.mult) \
                   .then_inc(sem["a_t2"], 1)
                step.sync()
                dve.wait_ge(sem["a_t2"], m + 1)
                dve.tensor_tensor(kT[:, m * 512:(m + 1) * 512], T[:, 10 + p, :], T[:, 12 + p, :], ALU.add) \
                   .then_inc(sem["a_rope"], 1)

            for m in range(9):
                if m < 8:
                    a_z0(m)
                if m >= 1:
                    a_rope(m - 1)
            dve.wait_ge(sem["a_rope"], 8)

            def heads(t):
                return t.rearrange("p (h k) -> p h k", h=AH)

            def over_keys(t):
                return pat(t, [[1, AH], [0, S]])

            for j in range(NJ):
                dve.wait_ge(sem["a_score"], j + 1)
                for odd in range(2):
                    step.mark(dve.scalar_tensor_tensor(
                        out=pat(T[:, j, :], [[2 * S, AH // 2], [1, S]], odd * S),
                        in0=bank[j + 2 * odd][:, 0:AH // 2 * S].rearrange("p (h k) -> p h k", k=S), scalar=AD ** -0.5,
                        in1=pat(cst[:, C_CAUSAL:C_CAUSAL + S], [[0, AH // 2], [1, S]]), op0=ALU.mult, op1=ALU.add))
                step.sync()
                step(dve.tensor_reduce(am[:, j, :], heads(T[:, j, :]), AX, ALU.max))
                step(dve.tensor_tensor(am[:, j, :], am[:, j, :], v("sink", 0, AH), ALU.max))
                step.mark(dve.tensor_tensor(asink[:, j, :], v("sink", 0, AH), am[:, j, :], ALU.subtract))
                step.sync()
                dve.tensor_tensor(heads(T[:, 2 + j, :]), heads(T[:, j, :]), over_keys(am[:, j, :]), ALU.subtract) \
                   .then_inc(sem["a_sub"], 1)
            for j in range(NJ):
                dve.wait_ge(sem["a_exp"], j + 1)
                step(dve.tensor_reduce(az[:, j, :], heads(T[:, 4 + j, :]), AX, ALU.add))
                step(dve.tensor_tensor(az[:, j, :], az[:, j, :], asink[:, j, :], ALU.add))
                step(dve.reciprocal(az[:, j, :], az[:, j, :]))
                step(dve.tensor_tensor(heads(T[:, 6 + j, :]), heads(T[:, 4 + j, :]), over_keys(az[:, j, :]), ALU.mult))
                dve.wait_ge(sem["a_zero"], 1)
                for b in range(BT):
                    part = slice(b * S, (b + 1) * S)
                    ins = dve.transpose(aprobT[part, j, :, part], heads(T[part, 6 + j, :]))
                ins.then_inc(sem["a_pt"], 1)
            for j in range(NJ):
                dve.wait_ge(sem["a_pv"], j + 1)
                dve.tensor_copy(T[:, 9 + 2 * j, :], bank[3 + 2 * j][:, :]).then_inc(sem["a_oTd"], 1)
            dve.wait_ge(sem["xb_ready"], 2)
            dve.wait_ge(sem["a_o"], 1)
            dve.tensor_tensor(xres[:, :, :], xbias[:, :, :], bank[6][:, 0:TOK].rearrange("p (j d) -> p j d", j=NJ),
                              ALU.add).then_inc(sem["x_res"], 1)

            dve.wait_ge(sem["x_res"], 2)
            layernorm(2, xres)

            def over_experts(t):
                return pat(t, [[1, NJ], [0, E]])

            def gate_softmax():
                step(dve.tensor_reduce(gm[:, :], lg[:, :, :], AX, ALU.max))
                dve.tensor_tensor(lg[:, :, :], lg[:, :, :], over_experts(gm[:, :]), ALU.subtract).then_inc(sem["f_sub"], 1)
                gate_softmax.n += 1
                dve.wait_ge(sem["f_exp"], gate_softmax.n)
                step(dve.tensor_reduce(gz[:, :], lg[:, :, :], AX, ALU.add))
                step(dve.reciprocal(gz[:, :], gz[:, :]))
                step(dve.tensor_tensor(lg[:, :, :], lg[:, :, :], over_experts(gz[:, :]), ALU.mult))
                for j in range(NJ):
                    step.mark(dve.max(m8[:, j, :], lg[:, j, :]))
                step.sync()
                for j in range(NJ):
                    step.mark(dve.max_index(i8[:, j, :], m8[:, j, :], lg[:, j, :]))
                step.sync()
                step(dve.tensor_copy(i8f[:, :, :], i8[:, :, :]))

            gate_softmax.n = 0
            def l_rest(i):
                dve.wait_ge(sem["l_hi"], i + 1)
                if i >= 2:
                    dve.wait_ge(sem["l_split"], i - 1)
                at = i // 2 * SK
                dve.tensor_tensor(T[:, 8 + i % 2, :], bank[6 + i % 2][:, :], (vs if i % 2 else ks)[0][:, at:at + SK],
                                  ALU.subtract).then_inc(sem["l_rest"], 1)

            iota = cst[:, C_IOTA:C_IOTA + E]
            dve.wait_ge(sem["f_gate"], 1)
            step(dve.tensor_copy(lg[:, :, :], bank[6][:, 0:NJ * E].rearrange("p (j e) -> p j e", j=NJ)))
            gate_softmax()
            step(dve.tensor_reduce(gm[:, :], m8[:, :, 0:2], AX, ALU.add))
            step(dve.tensor_scalar(gm[:, :], gm[:, :], 1e-9, None, ALU.add))
            step(dve.reciprocal(gm[:, :], gm[:, :]))
            step(dve.tensor_tensor(gw[:, :, :], m8[:, :, 0:2], pat(gm[:, :], [[1, NJ], [0, 2]]), ALU.mult))
            for j in range(NJ):
                for k in range(2):
                    step.mark(dve.tensor_scalar(cw[:, k, j, :], iota, i8f[:, j, k:k + 1], gw[:, j, k:k + 1],
                                                ALU.is_equal, ALU.mult))
            step.sync()
            dve.tensor_tensor(cw[:, 2, :, :], cw[:, 0, :, :], cw[:, 1, :, :], ALU.add).then_inc(sem["f_cw"], 1)
            dve.wait_ge(sem["f_cwps"], 1)
            dve.tensor_copy(cwT[0:E, :], bank[7][0:E, 0:TOK]).then_inc(sem["f_cwT"], 1)
            dve.wait_ge(sem["xb_ready"], 3)
            dve.wait_ge(sem["f_cw"], 1)
            for e in range(E + 1):
                dve.wait_ge(sem["f_y"], e + 1)
                if e:
                    dve.wait_ge(sem["f_acc"], NJ * e)
                for j in range(NJ):
                    ins = (dve.scalar_tensor_tensor(out=facc[:, j, :], in0=bank[4 + e % 2][:, j * D:(j + 1) * D],
                                                       scalar=cw[:, 2, j, e:e + 1] if e < E else 0.1,
                                                       in1=facc[:, j, :], op0=ALU.mult, op1=ALU.add))
                    ins.then_inc(sem["f_acc"], 1)
                if e >= 1:
                    l_rest(2 * (e - 1))
                    l_rest(2 * (e - 1) + 1)
            dve.wait_ge(sem["f_acc"], NJ * (E + 1))
            dve.wait_ge(sem["f_b2"], 1)
            dve.tensor_tensor(xres[:, :, :], facc[:, :, :], bank[6][:, 0:TOK].rearrange("p (j d) -> p j d", j=NJ),
                              ALU.add).then_inc(sem["x_res"], 1)

            dve.wait_ge(sem["l_hi"], 2 * B + 1)
            dve.tensor_tensor(T[:, 10:13, :].rearrange("p n d -> p (n d)")[:, 0:9 * D], lw[:, 4 * D:13 * D],
                              lsp[:, 0, :], ALU.subtract).then_inc(sem["l_rest"], 1)
            step(dve.tensor_tensor(gbias[:, :], v("bih", 0, 4), v("bhh", 0, 4), ALU.add))
            dve.tensor_scalar(gbias[:, 3:4], gbias[:, 3:4], 2.0, None, ALU.mult).then_inc(sem["l_gbias"], 1)
            zeroed = (hsp[:, :, :, :], asp[:, :, :, :], negmax[:, :, :], c2[:, :, :])
            for t in zeroed:
                dve.memset(t, 0.0).then_inc(sem["l_zero"], 1)
            dve.memset(ones[:, :], 1.0).then_inc(sem["l_zero"], 1)
            dve.wait_ge(sem["x_res"], 3)
            layernorm(3, xres)
            dve.wait_ge(sem["l_zero"], 3 + len(zeroed))

            def parts(t, n):
                return pat(t, [[1, n], [n, 3]])

            for g in (0, 2):
                dve.wait_ge(sem["l_gx"], g // 2 + 1)
                whole, rest = (t[:, :, g * B:(g + 2) * B] for t in (gx32, gxrest))
                high, mid, low = (gx[:, 0:S, k, g:g + 2, :].rearrange("p t g b -> p t (g b)") for k in range(3))
                step.mark(dve.tensor_tensor(mid, whole, high, ALU.subtract))
                step(dve.tensor_tensor(rest, whole, high, ALU.subtract))
                dve.tensor_tensor(low, rest, mid, ALU.subtract).then_inc(sem["l_gxlow"], 1)

            def half(main=None, out=None, gates=None):
                if out:
                    g, t = out
                    dve.wait_ge(sem["v_ps"], nth(g, t))
                    step(dve.tensor_reduce(opre[:, g, :], parts(bank[6][:, 0:1], BH), AX, ALU.add))
                    step.mark(dve.tensor_tensor(opre[:, g, :], opre[:, g, :], rz[:, g, :], ALU.mult))
                if main:
                    g, t = main
                    dve.wait_ge(sem["s_hi"], nth(g, t))
                    dve.tensor_reduce(mc[:, g, :], bank[1][:, 0:BH * KC].rearrange("p (b c) -> p b c", c=KC), AX, ALU.max) \
                       .then_inc(sem["m_c"], 1)
                if out:
                    g, t = out
                    step.sync()
                    dve.tensor_tensor(opre[:, g, :], opre[:, g, :], oh[:, g, :], ALU.add).then_inc(sem["o_pre"], 1)
                    g, t = out
                    dve.wait_ge(sem["at_32"], nth(g, t))
                    dve.tensor_tensor(asp[:, g, 1, :], a32[:, g, :], asp[:, g, 0, :], ALU.subtract).then_inc(sem["at_mid"], 1)
                    step.mark(dve.tensor_tensor(arest[:, g, :], a32[:, g, :], asp[:, g, 0, :], ALU.subtract))
                if main:
                    g, t = main
                    dve.wait_ge(sem["m_t"], nth(g, t))
                    step.mark(dve.tensor_reduce(m1[:, g:g + 1], bank[3][0:BH, 0:P], AX, ALU.max))
                step.sync()
                if main:
                    g, t = main
                    dve.tensor_scalar(negmax[0:BH, g, :], cst[0:BH, C_NEG:C_NEG + BH * KC], m1[:, g:g + 1], None, ALU.mult) \
                       .then_inc(sem["m_d"], 1)
                if out:
                    g, t = out
                    dve.wait_ge(sem["at_mid"], nth(g, t))
                    dve.tensor_tensor(asp[:, g, 2, :], arest[:, g, :], asp[:, g, 1, :], ALU.subtract).then_inc(sem["at_lo"], 1)
                if gates:
                    g, t = gates
                    dve.wait_ge(sem["g_ps"], nth(g, t))
                    dve.tensor_reduce(gsum[:, g, :], parts(bank[GATES[g]][:, 0:1], 4 * BH), AX, ALU.add) \
                       .then_inc(sem["g_sum"], 1)
                if main:
                    g, t = main
                    dve.wait_ge(sem["s_ps"], nth(g, t))
                    dve.tensor_reduce(ssum[:, g, :], parts(bank[2][:, 0:1], BH * KC), AX, ALU.add).then_inc(sem["s_sum"], 1)
                if gates:
                    g, t = gates
                    dve.wait_ge(sem["g_act"], nth(g, t))
                    i, f, o, gg = (gact[:, g, k * BH:(k + 1) * BH] for k in range(4))
                    step.mark(dve.scalar_tensor_tensor(out=fc2[:, g, :], in0=f, scalar=1.0, in1=c2[:, g, :],
                                                       op0=ALU.add, op1=ALU.mult))
                    step.mark(dve.scalar_tensor_tensor(out=ig[:, g, :], in0=i, scalar=1.0, in1=gg,
                                                       op0=ALU.add, op1=ALU.mult))
                    step.sync()
                    dve.scalar_tensor_tensor(out=c2[:, g, :], in0=fc2[:, g, :], scalar=0.5, in1=ig[:, g, :],
                                             op0=ALU.mult, op1=ALU.add).then_inc(sem["c_new"], 1)
                if main:
                    g, t = main
                    dve.wait_ge(sem["e_32"], nth(g, t))
                    dve.tensor_tensor(esp[:, g, 1, :], e32[:, g, :], esp[:, g, 0, :], ALU.subtract).then_inc(sem["e_mid"], 1)
                    step(dve.tensor_tensor(erest[:, g, :], e32[:, g, :], esp[:, g, 0, :], ALU.subtract))
                    dve.wait_ge(sem["e_mid"], nth(g, t))
                    dve.tensor_tensor(esp[:, g, 2, :], erest[:, g, :], esp[:, g, 1, :], ALU.subtract).then_inc(sem["e_lo"], 1)
                if gates:
                    g, t = gates
                    dve.wait_ge(sem["c_tanh"], nth(g, t))
                    dve.scalar_tensor_tensor(out=hsp[:, g, 0, :], in0=o, scalar=1.0, in1=tanhc[:, g, :],
                                             op0=ALU.add, op1=ALU.mult).then_inc(sem["h_hi"], 1)
                    step(dve.scalar_tensor_tensor(out=h32[:, g, :], in0=o, scalar=1.0, in1=tanhc[:, g, :],
                                                  op0=ALU.add, op1=ALU.mult))
                    dve.wait_ge(sem["h_hi"], nth(g, t))
                    dve.tensor_tensor(hsp[:, g, 1, :], h32[:, g, :], hsp[:, g, 0, :], ALU.subtract).then_inc(sem["h_mid"], 1)
                    step(dve.tensor_tensor(hrest[:, g, :], h32[:, g, :], hsp[:, g, 0, :], ALU.subtract))
                    dve.wait_ge(sem["h_mid"], nth(g, t))
                    dve.tensor_tensor(hsp[:, g, 2, :], hrest[:, g, :], hsp[:, g, 1, :], ALU.subtract).then_inc(sem["h_lo"], 1)
                if main:
                    g, t = main
                    dve.wait_ge(sem["oh_ps"], nth(g, t))
                    step.mark(dve.tensor_reduce(oh[:, g, :], parts(bank[5][:, 0:1], BH), AX, ALU.add))
                    dve.wait_ge(sem["z_ps"], nth(g, t))
                    step(dve.tensor_reduce(zs[:, g, :], pat(bank[4][:, 0:1], [[KC, BH], [BH * KC, 3], [1, KC]]),
                                           mybir.AxisListType.XY, ALU.add))
                    step.mark(dve.tensor_scalar(oh[:, g, :], oh[:, g, :], v("bout"), None, ALU.add))
                    step.mark(dve.reciprocal(rz[:, g, :], zs[:, g, :]))

            lstm_loop(dve, half, step)
            dve.wait_ge(sem["y_tr"], 1)
            dve.tensor_tensor(xres[:, :, :], xres[:, :, :], bank[7][:, 0:TOK].rearrange("p (j d) -> p j d", j=NJ),
                              ALU.add).then_inc(sem["x_res"], 1)

            for t, x in ((up[:, :, :, :], 0.0), (two[:, :], 2.0)):
                dve.memset(t, x).then_inc(sem["m_const"], 1)
            dve.tensor_copy(sel[:, :], cst[0:6 * MN, C_SEL:C_SEL + 2 * MN]).then_inc(sem["m_const"], 1)
            dve.wait_ge(sem["x_res"], 4)
            layernorm(4, xres)
            z, z2, poly, delta, du = (T[:, i, :] for i in (3, 13, 14, 6, 7))
            for l in range(ML):
                conv(dve, step, l, 0).then_inc(sem["m_conv"], 1)
                dve.wait_ge(sem["m_bc"], l + 1)
                dve.tensor_copy(dts[:, :], bank[3][0:MR, 0:TOK]).then_inc(sem["m_dts"], 1)
                bc, rest = bank[2][0:6 * MN, 0:TOK], T[0:6 * MN, 15, 0:TOK]
                step(dve.tensor_copy(bcs[:, :], bc))
                for k in (1, 2):
                    for q in range(k, 3):
                        part = slice(q * 2 * MN, (q + 1) * 2 * MN)
                        step.mark(dve.tensor_tensor(rest[part, :], (bc if k == 1 else rest)[part, :], bcs[part, :],
                                                    ALU.subtract))
                    step.sync()
                    for q in range(k, 3):
                        part = slice(q * 2 * MN, (q + 1) * 2 * MN)
                        ins = dve.tensor_copy(bcs[part, :], rest[part, :])
                        if k == 1:
                            step.mark(ins)
                    step.sync()
                ins.then_inc(sem["m_bcs"], 1)
                dve.wait_ge(sem["m_e"], l + 1)
                step(dve.tensor_tensor(z, T[:, 4, :], T[:, 5, :], ALU.mult))
                step(dve.tensor_tensor(z2, z, z, ALU.mult))
                step(dve.tensor_scalar(poly, z2, LOG1P[4], LOG1P[3], ALU.mult, ALU.add))
                step(dve.tensor_tensor(poly, poly, z2, ALU.mult))
                for c in (LOG1P[2], LOG1P[1]):
                    step(dve.scalar_tensor_tensor(out=poly, in0=poly, scalar=c, in1=z2, op0=ALU.add, op1=ALU.mult))
                step(dve.scalar_tensor_tensor(out=poly, in0=poly, scalar=LOG1P[0], in1=z, op0=ALU.add, op1=ALU.mult))
                step(dve.tensor_tensor(delta, poly, T[:, 12, :], ALU.add))
                dve.tensor_tensor(du, delta, T[:, 1, :], ALU.mult).then_inc(sem["m_delta"], 1)
                dve.wait_ge(sem["m_delta"], l + 1)
                if l:
                    dve.wait_ge(sem["m_y"], l)
                for i in range(MNP):
                    n = l * MNP + i
                    dve.wait_ge(sem["m_bsb"], n + 1)
                    dve.tensor_tensor(pairs(state[0], i), over_pair(du[:, 0:TOK]), both(T[:, 8 + i % 2, :]), ALU.mult) \
                       .then_inc(sem["m_dbu0"], 1)
                    at = slice(i * 2 * TOK, (i + 1) * 2 * TOK)
                    for ch in range(MC):
                        dve.wait_ge(sem["m_dbu0" if ch == 0 else "m_dbu1"], n + 1)
                        dve.wait_ge(sem["m_dA"], 2 * n + ch + 1)
                        dve.tensor_tensor_scan(out=state[ch][:, at], data0=decay[ch][:, at], data1=state[ch][:, at],
                                               initial=0.0, op0=ALU.mult, op1=ALU.add) \
                           .then_inc(sem["m_scan0" if ch == 0 else "m_scan1"], 1)
                    dve.wait_ge(sem["m_csb"], n + 1)
                    dve.wait_ge(sem["m_scan0"], n + 1)
                    dve.tensor_tensor(pairs(state[0], i), pairs(state[0], i), both(T[:, 10 + i % 2, :]), ALU.mult) \
                       .then_inc(sem["m_hc0"], 1)
                dve.wait_ge(sem["m_y"], l + 1)
                for ch in range(MC):
                    half = slice(ch * TOK, (ch + 1) * TOK)
                    step.mark(dve.scalar_tensor_tensor(out=T[:, 3, half], in0=T[:, 1, half], scalar=v("mD", l * MC + ch),
                                                       in1=bank[0][:, half], op0=ALU.mult, op1=ALU.add))
                step.sync()
                dve.wait_ge(sem["m_zs"], l + 1)
                dve.tensor_tensor(T[:, 13, :], T[:, 3, :], T[:, 2, :], ALU.mult).then_inc(sem["m_ys"], 1)
                dve.wait_ge(sem["m_o"], l + 1)
                res = T[:, 3, 0:TOK].rearrange("p (j d) -> p j d", j=NJ)
                step(dve.tensor_tensor(res, xn[:, :, :], bank[4][:, 0:TOK].rearrange("p (j d) -> p j d", j=NJ), ALU.add))
                layernorm(5 + l, res, l)
            step(dve.tensor_tensor(xres[:, :, :], xres[:, :, :], xn[:, :, :], ALU.add))
            layernorm(5 + ML, xres)
            step(dve.tensor_tensor(facc[:, :, :], xres[:, :, :], pat(r("wob"), [[0, NJ], [1, D]]), ALU.add))
            dve.wait_ge(sem["r_gate"], 1)
            step(dve.tensor_tensor(lg[:, :, :], bank[6][:, 0:NJ * E].rearrange("p (j e) -> p j e", j=NJ),
                                   pat(r("gateb", 0, E), [[0, NJ], [1, E]]), ALU.add))
            gate_softmax()
            for j in range(NJ):
                step.mark(dve.tensor_scalar(oneh[:, j, :], iota, i8f[:, j, 0:1], None, ALU.is_equal))
            step.sync()
            dve.wait_ge(sem["r_a"], 1)
            dve.tensor_tensor(loraa[:, :, :].rearrange("p j (e k) -> p (j e) k", k=LR),
                              bank[7][:, 0:NJ * E * LR].rearrange("p (n k) -> p n k", k=LR),
                              pat(oneh[:, :, :], [[1, NJ * E], [0, LR]]), ALU.mult).then_inc(sem["r_am"], 1)
            dve.wait_ge(sem["r_amps"], 1)
            dve.tensor_copy(cwT[:, :], bank[5][0:E * LR, 0:TOK]).then_inc(sem["r_amT"], 1)
            dve.wait_ge(sem["r_o"], 1)
            dve.tensor_tensor(xres[:, :, :], facc[:, :, :], bank[4][:, 0:TOK].rearrange("p (j d) -> p j d", j=NJ),
                              ALU.add).then_inc(sem["x_res"], 2)

        @block.tensor
        def _(pe):
            def ln_transpose(n):
                pe.wait_ge(sem["ln_xn"], n + 1)
                for j in range(NJ):
                    ins = pe.transpose(bank[7][:, j * P:(j + 1) * P], xn[:, j, :], ident)
                ins.then_inc(sem["ln_tr"], 1)

            pe.wait_ge(sem["d_par"], 48)
            cb8 = cst[:, C_CB8:C_CB8 + P]
            pe.matmul(bank[6][:, 0:D], wx[:, 0:D], cb8, start=True, stop=True)
            pe.matmul(bank[6][:, D:2 * D], wx[:, D:2 * D], cb8, start=True, stop=True)
            pe.matmul(bank[6][:, 2 * D:2 * D + 2], cb8, v("bq", 0, 2), start=True, stop=True).then_inc(sem["xw_ps"], 1)
            ln_transpose(0)
            pe.wait_ge(sem["xw_sb"], 1)

            def k_proj(s):
                if s >= 2:
                    pe.wait_ge(sem["k_sq"], s - 1)
                if s == 0:
                    pe.wait_ge(sem["ln_xT"], 1)
                    pe.matmul(bank[0][:, 0:TOK], xw[:, D:2 * D], xnT[:, :], start=True, stop=True) \
                      .then_inc(sem["k_proj"], 1)
                    return
                b = s - 1
                pe.wait_ge(d_ctx[b], 16)
                pe.matmul(bank[s % 2][:, :], xw[:, 0:D], ctxT[:, b * SK:(b + 1) * SK], start=True, stop=True) \
                  .then_inc(sem["k_proj"], 1)
                if b >= 2:
                    pe.wait_ge(sem["v_evac"], b - 1)
                for c in range(KC):
                    at = b * SK + c * P
                    ins = pe.matmul(bank[4 + b % 2][:, c * P:(c + 1) * P], ctxT[:, at:at + P], wx[:, 2 * D:3 * D],
                                    start=True, stop=True)
                ins.then_inc(sem["v_proj"], 1)

            def k_var(s):
                w, p = (TOK if s == 0 else SK), s % 2
                pe.wait_ge(sem["k_sq"], s + 1)
                if s >= 2:
                    pe.wait_ge(sem["k_rstd"], s - 1)
                pe.matmul(bank[2 + p][:, 0:w], cst[:, C_BLK8:C_BLK8 + P], T[:, 2 + p, 0:w], start=True, stop=True) \
                  .then_inc(sem["k_var"], 1)

            for s in range(2 + B):
                if s <= B:
                    k_proj(s)
                if s >= 1:
                    k_var(s - 1)

            def x_scores(i):
                b, g = divmod(i, XG)
                if i == 0:
                    pe.wait_ge(sem["qblk_ready"], 1)
                    pe.wait_ge(sem["k_done"], 1 + B)
                    pe.wait_ge(sem["v_evac"], B)
                    pe.wait_ge(sem["k_rstd"], 1 + B)
                if i >= 2:
                    pe.wait_ge(sem["x_max"], i - 1)
                pe.matmul(bank[i % 2][:, :], qblk[:, g, b, :, :], kT[:, b * SK:(b + 1) * SK],
                          start=True, stop=True).then_inc(sem["x_score"], 1)

            def x_transpose(i):
                pe.wait_ge(sem["x_norm"], i + 1)
                if i >= 2:
                    pe.wait_ge(sem["x_pt"], i - 1)
                for c in range(KC):
                    ins = pe.transpose(bank[2 + i % 2][:, c * P:(c + 1) * P], T[:, 4 + i % 2, c * P:(c + 1) * P], ident)
                ins.then_inc(sem["x_tr"], 1)

            def x_pv(i):
                b, g = divmod(i, XG)
                pe.wait_ge(sem["x_pt"], i + 1)
                if g == 0 and b >= 2:
                    pe.wait_ge(sem["x_oT"], b - 1)
                for c in range(KC):
                    ins = pe.matmul(bank[4 + b % 2][32 * g:32 * g + 32, 0:P], vx[:, b * KC + c, 32 * g:32 * g + 32],
                                    T[:, 6 + i % 2, c * P:(c + 1) * P], start=(c == 0), stop=(c == KC - 1))
                ins.then_inc(sem["x_pv"], 1)

            for i in range(B * XG + 3):
                if i < B * XG:
                    x_scores(i)
                if 2 <= i < B * XG + 2:
                    x_transpose(i - 2)
                if i >= 3:
                    x_pv(i - 3)
            pe.wait_ge(sem["x_oT"], B + 1)
            for j in range(NJ):
                ins = pe.matmul(bank[6][:, j * D:(j + 1) * D], oT[:, j * P:(j + 1) * P], wx[:, 3 * D:4 * D],
                                start=True, stop=True)
            ins.then_inc(sem["x_o"], 1)

            ln_transpose(1)

            def a_proj(m):
                if m == 0:
                    pe.wait_ge(sem["a_wc"], 1)
                    pe.wait_ge(sem["ln_xT"], 2)
                if m >= 2:
                    pe.wait_ge(sem["a_z0"], m - 1)
                for h in range(2):
                    ins = pe.matmul(bank[m % 2][:, h * TOK:(h + 1) * TOK], wqkv[:, (2 * m + h) * P:(2 * m + h + 1) * P],
                                    xnT[:, :], start=True, stop=True)
                ins.then_inc(sem["a_proj"], 1)

            def a_var(m):
                pe.wait_ge(sem["a_sq"], m + 1)
                if m >= 2:
                    pe.wait_ge(sem["a_rstd"], m - 1)
                pe.matmul(bank[2 + m % 2][:, :], cst[:, C_BLK64:C_BLK64 + P], T[:, m % 2, :], start=True, stop=True) \
                  .then_inc(sem["a_var"], 1)

            def a_rot(m):
                pe.wait_ge(sem["a_z"], m + 1)
                if m >= 2:
                    pe.wait_ge(sem["a_t2"], m - 1)
                pe.matmul(bank[4 + m % 2][:, :], cst[:, C_ROT:C_ROT + P], T[:, 8 + m % 2, :], start=True, stop=True) \
                  .then_inc(sem["a_rot"], 1)

            def a_vproj(n):
                if n >= 1:
                    pe.wait_ge(sem["a_vev"], n)
                at = 2 * AH * AD + (n % 2) * 512
                pe.matmul(bank[6][:, :], xnT[:, (n // 2) * P:(n // 2 + 1) * P], wqkv[:, at:at + 512],
                          start=True, stop=True).then_inc(sem["a_vproj"], 1)

            for m in range(10):
                if m < 8:
                    a_proj(m)
                if 1 <= m <= 8:
                    a_var(m - 1)
                if m >= 2:
                    a_rot(m - 2)
                if 4 <= m < 8:
                    a_vproj(m - 4)
            pe.wait_ge(sem["a_rope"], 8)
            for j in range(NJ):
                for h in range(AH):
                    rowsh = slice(AD * (h % 2), AD * (h % 2) + AD)
                    for b in range(BT):
                        at = (h // 2) * TOK + (j * BT + b) * S
                        ins = pe.matmul(bank[j + 2 * (h % 2)][b * S:(b + 1) * S, h // 2 * S:(h // 2 + 1) * S], kT[rowsh, at:at + S],
                                        kT[rowsh, 4 * 512 + at:4 * 512 + at + S], start=True, stop=True)
                ins.then_inc(sem["a_score"], 1)
            pe.wait_ge(sem["a_vev"], 4)
            pe.wait_ge(sem["d_attn"], 32)
            for j in range(NJ):
                pe.wait_ge(sem["a_pt"], j + 1)
                for h in range(AH):
                    o = bank[2 + 2 * j + h // 8]
                    ins = pe.matmul(o[AD * (h % 2):AD * (h % 2) + AD, (h // 2 % 4) * P:(h // 2 % 4 + 1) * P],
                                    avals[:, j, h * AD:(h + 1) * AD], aprobT[:, j, h, :], start=True, stop=True)
                ins.then_inc(sem["a_pv"], 1)
            for j in range(NJ):
                pe.wait_ge(sem["a_oT"], j + 1)
                pe.wait_ge(sem["a_oTd"], j + 1)
                for n in range(AH // 2):
                    ins = pe.matmul(bank[6][:, j * D:(j + 1) * D], T[:, 8 + 2 * j + n // 4, (n % 4) * P:(n % 4 + 1) * P],
                                    projT[:, n * D:(n + 1) * D], start=(n == 0), stop=(n == AH // 2 - 1))
            ins.then_inc(sem["a_o"], 1)

            ln_transpose(2)
            pe.wait_ge(sem["ln_xT"], 3)
            pe.wait_ge(sem["d_ffn"], 80)
            for j in range(NJ):
                ins = pe.matmul(bank[6][:, j * E:(j + 1) * E], xnT[:, j * P:(j + 1) * P], wg[:, :], start=True, stop=True)
            ins.then_inc(sem["f_gate"], 1)
            pe.wait_ge(sem["d_ffn"], 80)

            def f_hidden(e):
                if e >= 2:
                    pe.wait_ge(sem["f_act"], 2 * (e - 1))
                w = w1[:, e * F:(e + 1) * F] if e < E else ws[:, 0:F]
                for fc in range(FC):
                    half = slice((fc % 2) * TOK, (fc % 2) * TOK + TOK)
                    ins = pe.matmul(bank[2 * (e % 2) + fc // 2][:, half], w[:, fc * P:(fc + 1) * P], xnT[:, :],
                                    start=True, stop=True)
                    if fc % 2:
                        ins.then_inc(sem["f_h"], 1)

            def f_out(e):
                pe.wait_ge(sem["f_act"], 2 * (e + 1))
                if e >= 2:
                    pe.wait_ge(sem["f_acc"], NJ * (e - 1))
                w = w2[:, e * F:(e + 1) * F] if e < E else ws[:, F:2 * F]
                for j in range(NJ):
                    for fc in range(FC):
                        at = (fc % 2) * TOK + j * P
                        ins = pe.matmul(bank[4 + e % 2][:, j * D:(j + 1) * D], T[:, 2 * (e % 2) + fc // 2, at:at + P],
                                        w[:, fc * D:(fc + 1) * D], start=(fc == 0), stop=(fc == FC - 1))
                ins.then_inc(sem["f_y"], 1)

            def l_keys_values(b):
                if b == 0:
                    pe.wait_ge(sem["d_lw"], 16)
                    pe.wait_ge(sem["f_cwT"], 1)
                else:
                    pe.wait_ge(sem["l_rest"], 2 * b - 1)
                pe.matmul(bank[6][:, :], lw[:, 14 * D:15 * D], ctxT[:, b * SK:(b + 1) * SK], start=True, stop=True) \
                  .then_inc(sem["l_kv"], 1)
                if b:
                    pe.wait_ge(sem["l_rest"], 2 * b)
                for c in range(KC):
                    at = b * SK + c * P
                    ins = pe.matmul(bank[7][:, c * P:(c + 1) * P], ctxT[:, at:at + P], lw[:, 13 * D:14 * D],
                                    start=True, stop=True)
                ins.then_inc(sem["l_kv"], 1)

            for e in range(E + 2):
                if e <= E:
                    f_hidden(e)
                if e == 1:
                    pe.wait_ge(sem["f_cw"], 1)
                    for j in range(NJ):
                        ins = pe.transpose(bank[7][0:E, j * P:(j + 1) * P], cw[:, 2, j, :], ident)
                    ins.then_inc(sem["f_cwps"], 1)
                if e >= 1:
                    f_out(e - 1)
                if e >= 2:
                    l_keys_values(e - 2)
            pe.wait_ge(sem["l_rest"], 2 * B)
            pe.wait_ge(sem["f_cwT"], 1)
            pe.wait_ge(sem["d_ffn"], 80)
            for j in range(NJ):
                ins = pe.matmul(bank[6][:, j * D:(j + 1) * D], cwT[0:E, j * P:(j + 1) * P], b2[:, :], start=True, stop=True)
            ins.then_inc(sem["f_b2"], 1)

            ln_transpose(3)
            pe.wait_ge(sem["ln_xT"], 4)
            for g in range(4):
                ins = pe.matmul(bank[g // 2][:, (g % 2) * TOK:(g % 2 + 1) * TOK], lw[:, g * D:(g + 1) * D], xnT[:, :],
                                start=True, stop=True)
            ins.then_inc(sem["l_gxps"], 1)

            def mm(out, lhsT, rhs, start=False, stop=False):
                return pe.matmul(out, lhsT, rhs, start=start, stop=stop, skip_group_check=True)

            def weight(k, m):
                return lsp[:, k, m * D:(m + 1) * D]

            MEETS = ((2, 1), (1, 2), (0, 3))

            def x_gates(g, t):
                mm(bank[GATES[g]][:, 0:12 * BH], identb, gx[:, bass.ds(t, 1), :, :, g * BH:(g + 1) * BH], start=True)

            def h_gates(g):
                for k, n in MEETS:
                    for m in range(4):
                        mm(pat(bank[GATES[g]][:, 0:1], [[4 * BH, n], [1, BH]], m * BH), weight(k, 4 + m), hsp[:, g, 0:n, :])

            def output_gates(gates, part):
                g, t = gates
                (k, n), ready = MEETS[part], ("at_hi", "at_mid", "at_lo")[part]
                if not (isinstance(t, int) and t == 0):
                    pe.wait_ge(sem[ready], nth(g, t - 1))
                for m in range(4):
                    ins = mm(pat(bank[GATES[g]][:, 0:1], [[4 * BH, n], [1, BH]], m * BH), weight(k, m), asp[:, g, 0:n, :],
                             stop=(part == 2))
                if part == 2:
                    ins.then_inc(sem["g_ps"], 1)

            def half(main=None, out=None, gates=None):
                if main is None:
                    if gates:
                        for part in range(3):
                            output_gates(gates, part)
                    return
                g, t = main

                def scores(k, n, start=False):
                    for i in range(BH * KC):
                        at = (g * BH * KC + i) * P
                        mm(pat(bank[2][:, 0:1], [[BH * KC, n]], i), ks[k][:, at:at + P],
                           pat(hsp[:, g, 0, 0:1], [[BH, n]], i // KC), start=(start and i == 0))

                pe.wait_ge(sem["h_hi"], nth(g, t))
                for i in range(BH * KC):
                    at = (g * BH * KC + i) * P
                    ins = mm(bank[1][:, i:i + 1], ks[0][:, at:at + P], hsp[:, g, 0, i // KC:i // KC + 1],
                             start=(i == 0), stop=True)
                ins.then_inc(sem["s_hi"], 1)
                pe.wait_ge(sem["h_mid"], nth(g, t))
                scores(1, 2, True)
                pe.wait_ge(sem["m_c"], nth(g, t))
                pe.transpose(bank[3][0:BH, 0:P], mc[:, g, :], ident).then_inc(sem["m_t"], 1)
                scores(2, 1)
                if gates:
                    output_gates(gates, 0)
                pe.wait_ge(sem["h_lo"], nth(g, t))
                scores(0, 3)
                if gates:
                    output_gates(gates, 1)
                if gates:
                    output_gates(gates, 2)
                pe.wait_ge(sem["m_d"], nth(g, t))
                mm(bank[2][:, 0:BH * KC], ones[:, :], negmax[:, g, :], stop=True).then_inc(sem["s_ps"], 1)
                x_gates(g, t + 1)
                h_gates(g)
                for k, n in MEETS:
                    ins = mm(bank[5][:, 0:n * BH], weight(k, 8), hsp[:, g, 0:n, :].rearrange("p k b -> p (k b)"),
                             start=(k == 2), stop=(k == 0))
                ins.then_inc(sem["oh_ps"], 1)

                def values(k, n):
                    for i in range(BH * KC):
                        at = (g * BH * KC + i) * P
                        ins = mm(pat(bank[6][:, 0:1], [[BH, n]], i // KC), vs[k][:, at:at + P],
                                 pat(esp[:, g, 0, 0:1], [[BH * KC, n]], i), start=(k == 2 and i == 0), stop=(k == 0))
                    return ins

                pe.wait_ge(sem["e_hi"], nth(g, t))
                values(2, 1)
                pe.wait_ge(sem["e_mid"], nth(g, t))
                values(1, 2)
                pe.wait_ge(sem["e_lo"], nth(g, t))
                mm(bank[4][:, 0:3 * BH * KC], ones[:, :], esp[:, g, :, :].rearrange("p k i -> p (k i)"),
                   start=True, stop=True).then_inc(sem["z_ps"], 1)
                values(0, 3).then_inc(sem["v_ps"], 1)

            pe.wait_ge(sem["l_gxlow"], 2)
            pe.wait_ge(sem["l_split"], 2 * B + 1)
            pe.wait_ge(sem["l_zero"], 3 + 4)
            for g in range(2):
                x_gates(g, 0)
                h_gates(g)
            lstm_loop(pe, half)
            pe.wait_ge(sem["y_st"], 2 * S)
            for j in range(NJ):
                ins = pe.transpose(bank[7][:, j * P:(j + 1) * P],
                                   yT[:, j * BT:(j + 1) * BT, :].rearrange("p b t -> p (b t)"), ident)
            ins.then_inc(sem["y_tr"], 1)

            ln_transpose(4)
            pe.wait_ge(sem["d_late"], 64)
            pe.wait_ge(sem["m_const"], MC + 3)
            for l in range(ML):
                pe.wait_ge(sem["ln_xT"], 5 + l)
                if l:
                    pe.wait_ge(sem["m_ys"], l)
                for n in range(2 * MC):
                    ins = pe.matmul(bank[n // 2][:, (n % 2) * TOK:(n % 2 + 1) * TOK],
                                    m_in[:, (4 * l + n) * P:(4 * l + n + 1) * P], xnT[:, :], start=True, stop=True)
                ins.then_inc(sem["m_uz"], 1)
                pe.wait_ge(sem["m_us"], l + 1)
                if l:
                    pe.wait_ge(sem["m_csb"], l * MNP)
                for out, a, z in ((bank[2][0:6 * MN, 0:TOK], 0, 6 * MN), (bank[3][0:MR, 0:TOK], 6 * MN, 6 * MN + MR)):
                    for ch in range(MC):
                        at = (l * MC + ch) * (6 * MN + MR)
                        ins = pe.matmul(out, m_x[:, at + a:at + z], T[:, 1, ch * TOK:(ch + 1) * TOK],
                                        start=(ch == 0), stop=(ch == MC - 1))
                ins.then_inc(sem["m_bc"], 1)
                pe.wait_ge(sem["m_dts"], l + 1)
                for ch in range(MC):
                    at = l * MI + ch * P
                    ins = pe.matmul(bank[4][:, ch * TOK:(ch + 1) * TOK], dtw[:, at:at + P], dts[:, :], start=True, stop=True)
                ins.then_inc(sem["m_dps"], 1)
                pe.wait_ge(sem["m_bcs"], l + 1)

                def spread(b, n):
                    for k in range(2):
                        ins = pe.matmul(bank[b][:, k * TOK:(k + 1) * TOK], pat(sel[:, n + k:n + k + 1], [[0, P]]),
                                        bcs[:, :], start=True, stop=True)
                    return ins

                for i in range(MNP + 2):
                    if i < MNP:
                        n = l * MNP + i
                        if i >= 2:
                            pe.wait_ge(sem["m_bsb"], n - 1)
                            pe.wait_ge(sem["m_csb"], n - 1)
                        spread(2 + i % 2, 2 * i).then_inc(sem["m_bps"], 1)
                        spread(5 + i % 2, MN + 2 * i).then_inc(sem["m_cps"], 1)
                    if i >= 2:
                        n = l * MNP + i - 2
                        for ch in range(MC):
                            pe.wait_ge(sem["m_hc0" if ch == 0 else "m_hc1"], n + 1)
                            for k in range(2):
                                at = (2 * (i - 2) + k) * TOK
                                ins = pe.matmul(bank[0][:, ch * TOK:(ch + 1) * TOK], ident, state[ch][:, at:at + TOK],
                                                start=(i == 2 and ch == 0 and k == 0), stop=(i == MNP + 1),
                                                skip_group_check=True)
                ins.then_inc(sem["m_y"], 1)
                pe.wait_ge(sem["m_ys"], l + 1)
                for j in range(NJ):
                    for ch in range(MC):
                        at = (l * MC + ch) * D
                        ins = pe.matmul(bank[4][:, j * D:(j + 1) * D], T[:, 13, ch * TOK + j * P:ch * TOK + (j + 1) * P],
                                        m_out[:, at:at + D], start=(ch == 0), stop=(ch == MC - 1))
                ins.then_inc(sem["m_o"], 1)
                ln_transpose(5 + l)

            ln_transpose(5 + ML)
            pe.wait_ge(sem["ln_xT"], 6 + ML)
            pe.wait_ge(sem["d_late"], 64)
            lora, wi, wo = fw[:, E:E + E * LR], fw[:, E + E * LR:E + E * LR + F], fw[:, E + E * LR + F:]
            for j in range(NJ):
                ins = pe.matmul(bank[6][:, j * E:(j + 1) * E], xnT[:, j * P:(j + 1) * P], fw[:, 0:E], start=True, stop=True)
            ins.then_inc(sem["r_gate"], 1)
            for j in range(NJ):
                ins = pe.matmul(bank[7][:, j * E * LR:(j + 1) * E * LR], xnT[:, j * P:(j + 1) * P], lora,
                                start=True, stop=True)
            ins.then_inc(sem["r_a"], 1)
            for fc in range(FC):
                pe.matmul(bank[fc][:, 0:TOK], wi[:, fc * P:(fc + 1) * P], xnT[:, :], start=True, stop=False)
            pe.wait_ge(sem["r_am"], 1)
            for j in range(NJ):
                ins = pe.transpose(bank[5][0:E * LR, j * P:(j + 1) * P], loraa[:, j, :], ident)
            ins.then_inc(sem["r_amps"], 1)
            pe.wait_ge(sem["r_amT"], 1)
            for fc in range(FC):
                pe.matmul(bank[fc][:, 0:TOK], lb[:, fc * P:(fc + 1) * P], cwT[:, :], start=False, stop=True) \
                  .then_inc(sem["r_h"], 1)
            pe.wait_ge(sem["r_act"], FC)
            for j in range(NJ):
                for fc in range(FC):
                    at = (fc % 2) * TOK + j * P
                    ins = pe.matmul(bank[4][:, j * D:(j + 1) * D], T[:, fc // 2, at:at + P], wo[:, fc * D:(fc + 1) * D],
                                    start=(fc == 0), stop=(fc == FC - 1))
            ins.then_inc(sem["r_o"], 1)


def lay_out(i):
    a = {k: np.asarray(x) for k, x in i.items()}

    def wide(m):
        return m.reshape(-1, P, m.shape[-1]).transpose(1, 0, 2).reshape(P, -1)

    ctxT = a["ctx_1024"].reshape(B * SK, D).T
    kv = a["L0_xattn_Wkv"]
    wx = np.concatenate([kv[:D], a["L0_xattn_Wq"], kv[D:].T, a["L0_xattn_Wo"].T], 1)

    def col(x, times=1):
        return np.tile(x, times).reshape(-1, P).T

    n = "L1_attn_"
    parts = {
        "bq": col(a["L0_xattn_bq"]), "bk": col(a["L0_xattn_bkv"][:D]), "bv": col(a["L0_xattn_bkv"][D:]),
        "qw": col(a["L0_xattn_qn_w"], XH), "qb": col(a["L0_xattn_qn_b"], XH),
        "kw": col(a["L0_xattn_kn_w"], XH), "kb": col(a["L0_xattn_kn_b"], XH),
        "aqw": col(a["L0_attn_qn_w"], 2), "aqb": col(a["L0_attn_qn_b"], 2),
        "akw": col(a["L0_attn_kn_w"], 2), "akb": col(a["L0_attn_kn_b"], 2),
        "sink": np.broadcast_to(a["L0_attn_sinks"], (P, AH)),
        "b1": a["L0_ffn_b1"].reshape(E * FC, P).T, "bs1": col(a["L0_ffn_bs1"]),
        "bih": lstm_order(a["L1_xattn_b_ih"]).reshape(4, P).T, "bhh": lstm_order(a["L1_xattn_b_hh"]).reshape(4, P).T,
        "bout": col(a["L1_xattn_b_out"]),
        "convw": a[n + "conv_w"].reshape(ML * MC, P, MK).transpose(1, 0, 2).reshape(P, -1),
        "convb": a[n + "conv_b"].reshape(ML * MC, P).T, "dtb": a[n + "dt_proj_b"].reshape(ML * MC, P).T,
        "mD": a[n + "D"].reshape(ML * MC, P).T,
        "alog": a[n + "A_log"].reshape(ML * MC, P, MN).transpose(1, 0, 2).reshape(P, -1),
        "wib": col(a["L1_ffn_wi_b"]),
    }
    vec = np.concatenate([parts[k].reshape(P, w) for k, w in V_NAMES], 1)
    lines = {"bo": a["L0_xattn_bo"], "projb": a["L0_attn_proj_b"], "bs2": a["L0_ffn_bs2"], "wob": a["L1_ffn_wo_b"],
             "gateb": a["L1_ffn_gate_b"], "lnw": a[n + "ln_w"].reshape(-1), "lnb": a[n + "ln_b"].reshape(-1)}
    rows = np.broadcast_to(np.concatenate([lines[k] for k, _ in R_NAMES]), (P, R_END))
    w_ih = lstm_order(a["L1_xattn_W_ih"])
    xp = a[n + "x_proj_w"].reshape(ML, MC, P, MR + 2 * MN)
    xp = np.concatenate([xp[..., MR:]] * 3 + [xp[..., :MR]], -1).transpose(2, 0, 1, 3).reshape(P, -1)
    outs = {
        "x": a["x"].reshape(TOK, D), "cst": shape_constants(), "vec": vec, "rows": rows, "wx": wx, "ctxT": ctxT,
        "mask": a["mask_BxS2_bk0"].reshape(1, B * SK),
        "qkvT": a["L0_attn_qkv_w"].T, "projT": wide(a["L0_attn_proj_w"].T),
        "wg": a["L0_ffn_Wg"], "w1": a["L0_ffn_W1"].transpose(1, 0, 2).reshape(P, E * F),
        "w2": wide(a["L0_ffn_W2"].reshape(E * F, D)), "b2": a["L0_ffn_b2"],
        "ws": np.concatenate([a["L0_ffn_Ws1"], wide(a["L0_ffn_Ws2"])], 1),
        "lw": np.concatenate([w_ih[:, :D].T, w_ih[:, D:].T, lstm_order(a["L1_xattn_W_hh"]).T,
                              a["L1_xattn_Wout"][:, D:].T, a["L1_xattn_Wout"][:, :D].T, a["L1_xattn_Wq"]], 1),
        "mw": np.concatenate([a[n + "in_proj_w"].transpose(1, 0, 2).reshape(P, -1), xp,
                              a[n + "out_proj_w"].reshape(ML * MC, P, D).transpose(1, 0, 2).reshape(P, -1)], 1),
        "dtw": a[n + "dt_proj_w"].transpose(1, 0, 2).reshape(MR, -1),
        "fw": np.concatenate([a["L1_ffn_gate_W"].T, a["L1_ffn_lora_A"].reshape(E * LR, D).T,
                              a["L1_ffn_wi_W"].T, wide(a["L1_ffn_wo_W"].T)], 1),
        "lb": a["L1_ffn_lora_B"].transpose(0, 2, 1).reshape(E * LR, F),
    }
    return {k: np.ascontiguousarray(x) for k, x in outs.items()}


def lstm_order(w):
    i, f, g, o = np.split(w, 4, 0)
    return np.concatenate([i, f, o, g], 0)


def kernel(**inputs):
    import concourse.bacc as _bacc
    from concourse.bass_utils import run_bass_kernel_spmd as _run

    nc = _bacc.Bacc("TRN2", target_bir_lowering=False, num_devices=1)
    arrays = {f"in_{k}_dram": x for k, x in lay_out(inputs).items()}
    arr = {k[3:-5]: nc.dram_tensor(k, x.shape, mybir.dt.from_np(x.dtype), kind="ExternalInput").ap()
           for k, x in arrays.items()}
    out = nc.dram_tensor("out_0_dram", (TOK, D), F32, kind="ExternalOutput").ap()
    build(nc, arr, out)
    got = _run(nc, [arrays], core_ids=[0])
    return got.results[0]["out_0_dram"].reshape(B, S, D)
```

```python
from contextlib import ExitStack

import concourse.bass as bass
import numpy as np
from concourse import mybir

ALU = mybir.AluOpType
ACT = mybir.ActivationFunctionType
AX = mybir.AxisListType.X
F32 = mybir.dt.float32
BF16 = mybir.dt.bfloat16
U32 = mybir.dt.uint32
U8 = mybir.dt.uint8

P = 128
B, S, D = 8, 32, 128
SK = 512
TOK = B * S
NJ = TOK // P
BT = B // NJ
BH = B // 2
QK = (0, 1, 7)
GATES = (0, 7)
XH, XD = 16, 8
XG = 4
AH, AD = 16, 64
E, F = 8, 512
FC = F // P
ML, MI, MN, MR, MK = 4, 256, 16, 8, 4
MC = MI // P
LR = 4
KC = SK // P
MASKED = -1e30
FLOOR = -1e29

C_ID, C_CB8, C_BLK8, C_CB64, C_BLK64, C_ROT, C_COS, C_SIN, C_CAUSAL, C_HM, C_HM16, C_IOTA, C_NEG, C_SEL = np.cumsum(
    [0, P, P, P, P, P, P, S, S, S, 4, 16, 8, B * KC]).tolist()
C_END = C_SEL + 2 * MN

V_NAMES = [("bq", 1), ("bk", 1), ("bv", 1), ("qw", 1), ("qb", 1), ("kw", 1), ("kb", 1), ("aqw", 1), ("aqb", 1),
           ("akw", 1), ("akb", 1), ("sink", AH), ("b1", E * FC), ("bs1", FC), ("bih", 4), ("bhh", 4),
           ("bout", 1), ("convw", ML * MC * MK), ("convb", ML * MC), ("dtb", ML * MC), ("mD", ML * MC),
           ("alog", ML * MC * MN), ("wib", FC)]
V_AT = dict(zip([n for n, _ in V_NAMES], np.cumsum([0] + [w for _, w in V_NAMES]).tolist()))
V_END = sum(w for _, w in V_NAMES)

R_NAMES = [("bo", D), ("projb", D), ("bs2", D), ("wob", D), ("gateb", E), ("lnw", ML * D), ("lnb", ML * D)]
R_AT = dict(zip([n for n, _ in R_NAMES], np.cumsum([0] + [w for _, w in R_NAMES]).tolist()))
R_END = sum(w for _, w in R_NAMES)


def shape_constants():
    p = np.arange(P)
    c = np.zeros((P, C_END), np.float32)
    c[:, C_ID:C_ID + P] = np.eye(P)
    for size, centre, mean in ((XD, C_CB8, C_BLK8), (AD, C_CB64, C_BLK64)):
        same = (p[:, None] // size == p[None, :] // size) / size
        c[:, mean:mean + P] = same
        c[:, centre:centre + P] = np.eye(P) - same
    half = AD // 2
    for m in range(P):
        k = m + half if m % AD < half else m - half
        c[k, C_ROT + m] = -1.0 if m % AD < half else 1.0
    freq = (1.0 / np.float32(10000.0) ** (np.arange(0, AD, 2, dtype=np.float32) / AD)).astype(np.float32)
    angle = np.arange(S, dtype=np.float32)[None, :] * freq[(p % half)][:, None]
    c[:, C_COS:C_COS + S] = np.cos(angle)
    c[:, C_SIN:C_SIN + S] = np.sin(angle)
    c[:, C_CAUSAL:C_CAUSAL + S] = np.where(np.arange(S)[None, :] <= (p % S)[:, None], 0.0, MASKED)
    c[:, C_HM:C_HM + 4] = (p[:, None] % 32) // XD == np.arange(4)[None, :]
    c[:, C_HM16:C_HM16 + 16] = (p[:, None] // XD == np.arange(16)[None, :]) * np.float32(XD ** -0.5)
    c[:, C_IOTA:C_IOTA + 8] = np.arange(8)[None, :]
    c[:, C_NEG:C_NEG + B * KC] = -1.0 * (p[:, None] == np.arange(B * KC)[None, :] // KC)
    c[:, C_SEL:C_SEL + 2 * MN] = (p[:, None] % 32 == np.arange(32)[None, :]) * (p[:, None] < 96)
    return c


LEAD = 0.28157778313522575
SHIFTS = (1.2677443514519067, -0.7711647306200196)
PLUS = (1.127527981270037, 2.00260026175586)


def pat(t, dims, off=0):
    return bass.AP(tensor=t.tensor, offset=t.offset + off, ap=[list(t.ap[0])] + [list(d) for d in dims])


class Steps:

    def __init__(self, eng, sem):
        self.eng, self.sem, self.n, self.base = eng, sem, 0, 0

    def __call__(self, ins):
        self.mark(ins)
        self.sync()

    def mark(self, ins):
        ins.then_inc(self.sem, 1)
        self.n += 1

    def sync(self):
        self.eng.wait_ge(self.sem, self.base + self.n)


def build(nc, arr, out, upto=99):
    with ExitStack() as ctx:
        def sb(name, shape, dt=F32):
            return ctx.enter_context(nc.sbuf_tensor(name, shape, dt))

        sem = {}

        def sems(*names):
            for n in names:
                sem[n] = ctx.enter_context(nc.semaphore(n))

        cst = sb("cst", [P, C_END])
        vec = sb("vec", [P, V_END])
        rows = sb("rows", [P, R_END])
        wx = sb("wx", [P, 4 * D])
        ident = cst[:, C_ID:C_ID + P]

        def v(name, i=0, n=1):
            return vec[:, V_AT[name] + i:V_AT[name] + i + n]

        def r(name, i=0, n=D):
            return rows[:, R_AT[name] + i:R_AT[name] + i + n]

        wqkv = sb("wqkv", [P, 3 * AH * AD])
        projT = sb("projT", [P, AH * AD])
        w1 = sb("w1", [P, E * F])
        w2 = sb("w2", [P, E * F])
        ws = sb("ws", [P, 2 * F])
        wg = sb("wg", [P, E])
        b2 = sb("b2", [E, D])
        x_in = sb("x_in", [P, NJ, D])
        xres = sb("xres", [P, NJ, D])
        xbias = sb("xbias", [P, NJ, D])
        xn = sb("xn", [P, NJ, D])
        xnT = sb("xnT", [P, TOK])
        bn = sb("bn", [P, NJ, 6])
        mv = sb("mv", [P, NJ, 2])
        lnv = sb("lnv", [P, NJ])
        rs = sb("rs", [P, NJ])

        ctxT = sb("ctxT", [P, B * SK])
        kT = sb("kT", [P, B * SK])
        vx = sb("vx", [P, B * KC, D])
        qblk = sb("qblk", [P, XG, B, 4, S])
        T = sb("T", [P, 16, 512])
        maskb = sb("maskb", [P, B * SK], BF16)
        mask8 = T[:, 12:14, :].rearrange("p n k -> p (n k)").bitcast(U8)
        xw = sb("xw", [P, 2 * D + 2])
        oT = sb("oT", [P, TOK])
        xmax = sb("xmax", [P, B * XG])
        xneg = sb("xneg", [P, B * XG])
        xz = sb("xz", [P, B * XG])
        xrz = sb("xrz", [P, B * XG])

        eps5 = sb("eps5", [P, 1])
        eps6 = sb("eps6", [P, 1])
        wmean = sb("wmean", [P, 2 * AH])
        am = sb("am", [P, NJ, AH])
        asink = sb("asink", [P, NJ, AH])
        az = sb("az", [P, NJ, AH])
        lg = sb("lg", [P, NJ, E])
        gm = sb("gm", [P, NJ])
        gz = sb("gz", [P, NJ])
        m8 = sb("m8", [P, NJ, E])
        i8 = sb("i8", [P, NJ, E], U32)
        i8f = sb("i8f", [P, NJ, E])
        gw = sb("gw", [P, NJ, 2])
        cw = sb("cw", [P, 3, NJ, E])
        cwT = sb("cwT", [E * LR, TOK])
        facc = sb("facc", [P, NJ, D])
        avals = vx[:, :, :].rearrange("p n d -> p (n d)")[:, 0:NJ * AH * AD].rearrange("p (j n) -> p j n", j=NJ)
        aprobT = bass.AP(tensor=qblk[:, 0, 0, 0, 0:1].tensor, offset=0, ap=[[XG * B * 4 * S, P], [AH * P, NJ], [P, AH], [1, P]])
        lw = sb("lw", [P, 3 * 4 * D + 3 * D])
        bf = [t.bitcast(BF16) for t in (kT[:, :], qblk[:, :, :, :, :].rearrange("p a b c d -> p (a b c d)"),
                                        vx[:, :, :].rearrange("p n d -> p (n d)"))]
        half_b = B * SK
        ks = [bf[0][:, 0:half_b], bf[0][:, half_b:2 * half_b], maskb[:, :]]
        vs = [bf[1][:, 0:half_b], bf[1][:, half_b:2 * half_b], bf[2][:, 0:half_b]]
        lsp = sb("lsp", [P, 3, 9 * D], BF16)
        gbias = sb("gbias", [P, 4])
        gx = sb("gx", [P, S + 1, 3, 4, B], BF16)
        gx32, gxrest = (T[:, i:i + 2, :].rearrange("p a (t g b) -> p (a t) (g b)", g=4, b=B) for i in (0, 2))
        identb = T[:, 14, :].bitcast(BF16)[:, 0:P]
        yT = sb("yT", [P, B, S])
        ones = sb("ones", [P, P], BF16)
        hsp = sb("hsp", [P, 2, 3, BH], BF16)
        asp = sb("asp", [P, 2, 3, BH], BF16)
        esp = sb("esp", [P, 2, 3, BH * KC], BF16)
        negmax = sb("negmax", [P, 2, BH * KC], BF16)
        (h32, a32, c2, tanhc, fc2, ig, hrest, arest, mc, zs, rz, oh, opre) = [
            sb(n, [P, 2, BH]) for n in ("h32", "a32", "c2", "tanhc", "fc2", "ig", "hrest", "arest", "mc", "zs", "rz",
                                        "oh", "opre")]
        m1 = sb("m1", [BH, 2])
        (gsum, gact, ssum, e32, erest) = [sb(n, [P, 2, BH * KC]) for n in ("gsum", "gact", "ssum", "e32", "erest")]
        MNP = MN // 2
        LAG = 3
        mw = w1[:, 0:ML * (2 * MI + MC * (6 * MN + MR) + MC * D)]
        m_in = mw[:, 0:ML * 2 * MI]
        m_x = mw[:, ML * 2 * MI:ML * 2 * MI + ML * MC * (6 * MN + MR)]
        m_out = mw[:, ML * 2 * MI + ML * MC * (6 * MN + MR):]
        dtw = projT[0:MR, 0:ML * MI]
        decay = [ctxT[:, :], kT[:, :]]
        state = [qblk[:, :, :, :, :].rearrange("p a b c d -> p (a b c d)"), vx[:, :, :].rearrange("p n d -> p (n d)")]
        up = sb("up", [P, MC, B, S + MK - 1])
        aneg = sb("aneg", [P, ML * MC * MN])
        bcs = sb("bcs", [6 * MN, TOK], BF16)
        sel = sb("sel", [6 * MN, 2 * MN], BF16)
        dts = sb("dts", [MR, TOK])
        consts = sb("m_consts", [P, 3])
        two, shifts = consts[:, 0:1], (consts[:, 1:2], consts[:, 2:3])
        fw = wqkv[:, 0:E + E * LR + F + FC * D]
        lb = wqkv[0:E * LR, 2048:2048 + F]
        oneh = sb("oneh", [P, NJ, E])
        loraa = T[:, 14, 0:NJ * E * LR].rearrange("p (j n) -> p j n", j=NJ)
        bank = [ctx.enter_context(nc.psum_tensor(f"bank{i}", [P, 512], F32)) for i in range(8)]

        sems("d_par", "d_rows", "d_x", "d_mask", "d_out",
             "pe_step", "act_step", "dve_step", "pool_step",
             "ln_var", "ln_rstd", "ln_xn", "ln_tr", "ln_xT",
             "xw_ps", "xw_sb", "k_proj", "k_sq", "k_var", "k_rstd", "k_hat", "k_done", "v_proj", "v_evac",
             "eps_ready", "mask_ready", "qblk_ready", "x_score", "x_max", "x_exp", "x_norm", "x_tr", "x_pt", "x_pv",
             "x_oT", "x_o", "xb_ready", "x_res")
        d_ctx = [ctx.enter_context(nc.semaphore(f"d_ctx{b}")) for b in range(B)]

        sems("d_attn", "d_ffn",
             "a_wmean", "a_wc", "a_proj", "a_sq", "a_var", "a_rstd", "a_z0", "a_z", "a_rot", "a_t2", "a_rope",
             "a_vproj", "a_vev", "a_score", "a_sub", "a_exp", "a_zero", "a_pt", "a_pv", "a_oT", "a_oTd", "a_o",
             "f_gate", "f_sub", "f_exp", "f_cw", "f_cwps", "f_cwT", "f_h", "f_act", "f_y", "f_acc", "f_b2")
        sems("d_lw", "l_w", "l_kv", "l_hi", "l_rest", "l_split", "l_gbias", "l_gxps", "l_gx", "l_gxlow", "l_zero",
             "g_ps", "g_sum", "g_act", "c_new", "c_tanh", "h_hi", "h_mid", "h_lo", "s_hi", "m_c", "m_t", "m_d", "s_ps",
             "s_sum", "e_hi", "e_32", "e_mid", "e_lo", "oh_ps", "z_ps", "v_ps", "o_pre", "at_hi", "at_32", "at_mid",
             "at_lo", "y_st", "y_tr")
        sems("d_late", "m_const", "m_uz", "m_up", "m_conv", "m_us", "m_ud", "m_z", "m_sq", "m_bc",
             "m_dts", "m_bcs", "m_dps", "m_e", "m_delta", "m_bps", "m_cps", "m_bsb", "m_csb", "m_dA", "m_dbu0",
             "m_dbu1", "m_scan0", "m_scan1", "m_hc0", "m_hc1", "m_y", "m_ys", "m_o",
             "r_gate", "r_a", "r_am", "r_amps", "r_amT", "r_h", "r_act", "r_o")
        N_OUT = 6
        LN_LAST = 4 + ML
        LSTM_STEPS = 26
        CENTRED = (0, 1, 14)
        block = ctx.enter_context(nc.Block())

        def lstm_loop(engine, half, steps=None):
            def turn(t):
                half(main=(1, t), out=(0, t), gates=(0, t + 1))
                half(main=(0, t + 1), out=(1, t), gates=(1, t + 1))

            half(gates=(0, 0))
            half(main=(0, 0), gates=(1, 0))
            turn(0)
            before = steps.n if steps else 0
            with engine.Fori(0, (S - 2) // 2) as i:
                if steps:
                    steps.n, steps.base = 0, before + i * (2 * LSTM_STEPS)
                turn(i * 2 + 1)
                turn(i * 2 + 2)
            if steps:
                assert steps.n == 2 * LSTM_STEPS
                steps.n, steps.base = before + (S - 2) * LSTM_STEPS, 0
            half(main=(1, S - 1), out=(0, S - 1))
            half(out=(1, S - 1))

        def transposed(n):
            return n + 1 - (n > LN_LAST)

        def nth(stream, t):
            return t * 2 + (stream + 1)

        def both(t):
            return t.rearrange("p (n k) -> p n k", n=2)

        def pairs(t, i):
            return both(t[:, i * 2 * TOK:(i + 1) * 2 * TOK])

        def over_pair(t):
            return pat(t, [[0, 2], [1, TOK]])

        @block.sync
        def _(sp):
            sp.dma_start(x_in[:, :, :], arr["x"].rearrange("(j p) d -> p j d", p=P)).then_inc(sem["d_x"], 16)
            sp.dma_start(cst[:, :], arr["cst"]).then_inc(sem["d_par"], 16)
            sp.dma_start(wx[:, :], arr["wx"]).then_inc(sem["d_par"], 16)
            for b in range(B):
                sp.dma_start(ctxT[:, b * SK:(b + 1) * SK], arr["ctxT"][:, b * SK:(b + 1) * SK]) \
                  .then_inc(d_ctx[b], 16)
            sp.dma_start(wg[:, :], arr["wg"]).then_inc(sem["d_ffn"], 16)
            sp.dma_start(b2[:, :], arr["b2"]).then_inc(sem["d_ffn"], 16)
            sp.dma_start(ws[:, :], arr["ws"]).then_inc(sem["d_ffn"], 16)
            sp.dma_start(w1[:, :], arr["w1"]).then_inc(sem["d_ffn"], 16)
            sp.dma_start(w2[:, :], arr["w2"]).then_inc(sem["d_ffn"], 16)
            sp.dma_start(lw[:, :], arr["lw"]).then_inc(sem["d_lw"], 16)
            sp.wait_ge(sem["a_o"], NJ)
            sp.dma_start(dtw, arr["dtw"]).then_inc(sem["d_late"], 16)
            sp.dma_start(fw, arr["fw"]).then_inc(sem["d_late"], 16)
            sp.dma_start(lb, arr["lb"]).then_inc(sem["d_late"], 16)
            sp.wait_ge(sem["f_y"], E + 1)
            sp.dma_start(mw, arr["mw"]).then_inc(sem["d_late"], 16)
            sp.wait_ge(sem["x_res"], N_OUT)
            sp.dma_start(out.rearrange("(j p) d -> p j d", p=P), xres[:, :, :]).then_inc(sem["d_out"], 16)
            sp.wait_ge(sem["d_out"], 16)

        @block.gpsimd
        def _(pool):
            step = Steps(pool, sem["pool_step"])
            pool.memset(qblk[:, :, :, :, :], 0.0).then_inc(sem["mask_ready"], 1)
            pool.wait_ge(sem["d_mask"], 16)
            pool.tensor_scalar(maskb[:, :], mask8[:, :], -MASKED, MASKED, ALU.mult, ALU.add) \
                .then_inc(sem["mask_ready"], 1)
            pool.wait_ge(sem["d_par"], 48)
            for s in range(1 + B):
                pool.wait_ge(sem["k_hat"], s + 1)
                if s == 0:
                    ins = pool.tensor_scalar(T[:, 10, 0:TOK], T[:, 8, 0:TOK], 1.0, v("qb"), ALU.mult, ALU.add)
                else:
                    ins = pool.tensor_scalar(kT[:, (s - 1) * SK:s * SK], T[:, 8 + s % 2, :], 1.0, v("kb"),
                                             ALU.mult, ALU.add)
                ins.then_inc(sem["k_done"], 1)
            pool.wait_ge(sem["d_rows"], 16)
            pool.wait_ge(sem["d_x"], 16)
            pool.tensor_tensor(xbias[:, :, :], x_in[:, :, :], pat(r("bo"), [[0, NJ], [1, D]]), ALU.add) \
                .then_inc(sem["xb_ready"], 1)

            pool.wait_ge(sem["a_wmean"], 1)
            wqk = wqkv[:, 0:2 * AH * AD].rearrange("p (h d) -> p h d", d=AD)
            pool.tensor_tensor(wqk, wqk, pat(wmean[:, :], [[1, 2 * AH], [0, AD]]), ALU.subtract) \
                .then_inc(sem["a_wc"], 1)
            pool.wait_ge(sem["x_res"], 1)
            pool.tensor_tensor(xbias[:, :, :], xres[:, :, :], pat(r("projb"), [[0, NJ], [1, D]]), ALU.add) \
                .then_inc(sem["xb_ready"], 1)
            pool.memset(qblk[:, :, :, :, :], 0.0).then_inc(sem["a_zero"], 1)
            for m in range(8):
                pool.wait_ge(sem["a_z0"], m + 1)
                if m >= 2:
                    pool.wait_ge(sem["a_t2"], m - 1)
                pool.tensor_scalar(T[:, 8 + m % 2, :], T[:, 6 + m % 2, :], 1.0, v("aqb" if m < 4 else "akb"),
                                   ALU.mult, ALU.add).then_inc(sem["a_z"], 1)

            pool.wait_ge(sem["x_res"], 2)
            step(pool.tensor_scalar(T[:, 15, 0:D], r("bs2"), 0.1, 0.0, ALU.mult, ALU.add))
            pool.tensor_tensor(facc[:, :, :], xres[:, :, :], pat(T[:, 15, :], [[0, NJ], [1, D]]), ALU.add) \
                .then_inc(sem["xb_ready"], 1)

            pool.wait_ge(sem["d_lw"], 16)
            for at, end, by in ((7, 8, 2.0), (8, 11, 0.5), (12, 13, 0.5)):
                pool.tensor_scalar(lw[:, at * D:end * D], lw[:, at * D:end * D], by, 0.0, ALU.mult, ALU.add) \
                    .then_inc(sem["l_w"], 1)
            pool.memset(gx[:, S, :, :, :], 0.0).then_inc(sem["l_zero"], 1)
            pool.tensor_scalar(identb, ident, 1.0, 0.0, ALU.mult, ALU.add).then_inc(sem["l_zero"], 1)
            for i in range(-1, 2 * B):
                if i >= 0:
                    b = i // 2
                    parts = [t[:, b * SK:(b + 1) * SK] for t in (vs if i % 2 else ks)]
                    rest = T[:, 8 + i % 2, :]
                else:
                    parts = [lsp[:, k, :] for k in range(3)]
                    rest = T[:, 10:13, :].rearrange("p n d -> p (n d)")[:, 0:9 * D]
                pool.wait_ge(sem["l_rest"], i + 2)
                step(pool.tensor_scalar(parts[1], rest, 1.0, 0.0, ALU.mult, ALU.add))
                pool.tensor_tensor(parts[2], rest, parts[1], ALU.subtract).then_inc(sem["l_split"], 1)

            pool.wait_ge(sem["x_res"], 4)
            for ch in range(MC):
                pool.memset(decay[ch].rearrange("p (n s) -> p n s", s=S)[:, :, 0], 0.0).then_inc(sem["m_const"], 1)
            for l in range(ML):
                pool.wait_ge(sem["m_delta"], 3 * l + 2)
                for i in range(MNP + 1):
                    if i < MNP:
                        if l:
                            pool.wait_ge(sem["m_y"], l)
                        pool.wait_ge(sem["m_bsb"], l * MNP + i + 1)
                        pool.tensor_tensor(pairs(state[1], i), over_pair(T[:, 7, TOK:2 * TOK]), both(T[:, 8 + i % 2, :]),
                                           ALU.mult).then_inc(sem["m_dbu1"], 1)
                    if i >= 1:
                        pool.wait_ge(sem["m_csb"], l * MNP + i)
                        pool.wait_ge(sem["m_scan1"], l * MNP + i)
                        pool.tensor_tensor(pairs(state[1], i - 1), pairs(state[1], i - 1), both(T[:, 10 + (i - 1) % 2, :]),
                                           ALU.mult).then_inc(sem["m_hc1"], 1)

        @block.scalar
        def _(act):
            step = Steps(act, sem["act_step"])
            act.dma_start(vec[:, :], arr["vec"]).then_inc(sem["d_par"], 16)
            act.dma_start(mask8[:, :], bass.AP(tensor=arr["mask"].tensor, offset=0, ap=[[0, P], [1, B * SK]])) \
               .then_inc(sem["d_mask"], 16)
            act.dma_start(rows[:, :], arr["rows"]).then_inc(sem["d_rows"], 16)
            act.dma_start(wqkv[:, :], arr["qkvT"]).then_inc(sem["d_attn"], 16)
            act.dma_start(projT[:, :], arr["projT"]).then_inc(sem["d_attn"], 16)

            def ln_rstd(n):
                act.wait_ge(sem["ln_var"], n + 1)
                step(act.activation(lnv[:, :], mv[:, :, 1], ACT.Ln, bias=eps5[:, :]))
                act.activation(rs[:, :], lnv[:, :], ACT.Exp, scale=-0.5).then_inc(sem["ln_rstd"], 1)

            act.preload_act_table_set("natural_log_exp_and_others")
            act.wait_ge(sem["eps_ready"], 2)
            act.wait_ge(sem["d_par"], 48)
            ln_rstd(0)

            def k_square(s):
                w, p = (TOK if s == 0 else SK), s % 2
                act.wait_ge(sem["k_proj"], s + 1)
                if s == 0:
                    act.wait_ge(sem["xw_sb"], 1)
                if s >= 3:
                    act.wait_ge(sem["k_hat"], s - 2)
                bias = xw[:, 2 * D:2 * D + 1] if s == 0 else xw[:, 2 * D + 1:2 * D + 2]
                act.activation(T[:, CENTRED[s % 3], 0:w], bank[p][:, 0:w], ACT.Identity, bias=bias)
                act.activation(T[:, 2 + p, 0:w], bank[p][:, 0:w], ACT.Square, bias=bias).then_inc(sem["k_sq"], 1)

            def k_rstd(s):
                w, p = (TOK if s == 0 else SK), s % 2
                act.wait_ge(sem["k_var"], s + 1)
                step(act.activation(T[:, 4 + p, 0:w], bank[2 + p][:, 0:w], ACT.Ln, bias=eps6[:, :]))
                if s >= 2:
                    act.wait_ge(sem["k_hat"], s - 1)
                act.activation(T[:, 6 + p, 0:w], T[:, 4 + p, 0:w], ACT.Exp, scale=-0.5).then_inc(sem["k_rstd"], 1)

            for s in range(2 + B):
                if s <= B:
                    k_square(s)
                if s >= 1:
                    k_rstd(s - 1)

            def x_exp(i):
                act.wait_ge(sem["x_max"], i + 1)
                if i >= 2:
                    act.wait_ge(sem["x_norm"], i - 1)
                act.activation(T[:, 2 + i % 2, :], T[:, i % 2, :], ACT.Exp, bias=xneg[:, i:i + 1],
                               accum_out=xz[:, i:i + 1]).then_inc(sem["x_exp"], 1)

            def x_copy_pt(i):
                act.wait_ge(sem["x_tr"], i + 1)
                if i >= 2:
                    act.wait_ge(sem["x_pv"], i - 1)
                act.activation(T[:, 6 + i % 2, :], bank[2 + i % 2][:, :], ACT.Copy).then_inc(sem["x_pt"], 1)

            for i in range(B * XG + 2):
                if i < B * XG:
                    x_exp(i)
                if i >= 2:
                    x_copy_pt(i - 2)

            ln_rstd(1)

            def a_square(m):
                act.wait_ge(sem["a_proj"], m + 1)
                if m >= 2:
                    act.wait_ge(sem["a_var"], m - 1)
                act.activation(T[:, m % 2, :], bank[QK[m % 3]][:, :], ACT.Square).then_inc(sem["a_sq"], 1)

            def a_rstd(m):
                act.wait_ge(sem["a_var"], m + 1)
                step(act.activation(T[:, 2 + m % 2, :], bank[2 + m % 2][:, :], ACT.Ln, bias=eps5[:, :]))
                if m >= 2:
                    act.wait_ge(sem["a_z0"], m - 1)
                act.activation(T[:, 4 + m % 2, :], T[:, 2 + m % 2, :], ACT.Exp, scale=-0.5).then_inc(sem["a_rstd"], 1)

            def a_vev(n):
                act.wait_ge(sem["a_vproj"], n + 1)
                act.activation(avals[:, n // 2, (n % 2) * 512:(n % 2) * 512 + 512], bank[4 + n][:, :], ACT.Copy) \
                   .then_inc(sem["a_vev"], 1)

            for m in range(9):
                if m < 8:
                    a_square(m)
                if m >= 1:
                    a_rstd(m - 1)
            for j in range(NJ):
                act.wait_ge(sem["a_sub"], j + 1)
                act.activation(T[:, 4 + j, :], T[:, 2 + j, :], ACT.Exp)
                act.activation(asink[:, j, :], asink[:, j, :], ACT.Exp).then_inc(sem["a_exp"], 1)
                for n in ((0,), (1, 2, 3))[j]:
                    a_vev(n)
            for j in range(NJ):
                act.wait_ge(sem["a_pv"], j + 1)
                for half in range(2 - j):
                    act.activation(T[:, 8 + 2 * j + half, :], bank[2 + 2 * j + half][:, :], ACT.Copy) \
                       .then_inc(sem["a_oT"], 1)

            def l_high(i):
                act.wait_ge(sem["l_kv"], i + 1)
                at = i // 2 * SK
                act.activation((vs if i % 2 else ks)[0][:, at:at + SK], bank[6 + i % 2][:, :], ACT.Copy) \
                   .then_inc(sem["l_hi"], 1)

            ln_rstd(2)
            act.wait_ge(sem["f_sub"], 1)
            act.activation(lg[:, :, :], lg[:, :, :], ACT.Exp).then_inc(sem["f_exp"], 1)
            act.preload_act_table_set("silu_and_others")
            for e in range(E + 1):
                for q in range(2):
                    act.wait_ge(sem["f_h"], 2 * e + q + 1)
                    if e >= 2:
                        act.wait_ge(sem["f_y"], e - 1)
                    for fc in (2 * q, 2 * q + 1):
                        half = slice((fc % 2) * TOK, (fc % 2) * TOK + TOK)
                        bias = v("b1", e * FC + fc) if e < E else v("bs1", fc)
                        ins = act.activation(T[:, 2 * (e % 2) + q, half], bank[2 * (e % 2) + q][:, half], ACT.Silu,
                                             bias=bias)
                    ins.then_inc(sem["f_act"], 1)
                if e == 1:
                    act.wait_ge(sem["l_w"], 3)
                    act.activation(lsp[:, 0, :], lw[:, 4 * D:13 * D], ACT.Copy).then_inc(sem["l_hi"], 1)
                if e >= 1:
                    l_high(2 * (e - 1))
                    l_high(2 * (e - 1) + 1)
            act.preload_act_table_set("natural_log_exp_and_others")

            ln_rstd(3)
            act.wait_ge(sem["l_gbias"], 1)

            def to_time(first):
                at = first.ap[1][0]
                return pat(first, [[1, B], [at, S]])

            for g in range(4):
                act.wait_ge(sem["l_gxps"], g + 1)
                share = bank[g][:, 0:TOK].rearrange("p (b t) -> p b t", b=B)
                for to in (gx32[:, 0:1, g * B:(g + 1) * B], gx[:, 0:1, 0, g, :]):
                    ins = act.activation(to_time(to), share, ACT.Identity, bias=gbias[:, g:g + 1],
                                         scale=2.0 if g == 3 else 1.0)
                ins.then_inc(sem["l_gx"], 1)
            act.preload_act_table_set("exp_and_others")

            def half(main=None, out=None, gates=None):
                if out:
                    g, t = out
                    act.wait_ge(sem["o_pre"], nth(g, t))
                    act.activation(asp[:, g, 0, :], opre[:, g, :], ACT.Tanh).then_inc(sem["at_hi"], 1)
                    act.activation(a32[:, g, :], opre[:, g, :], ACT.Tanh).then_inc(sem["at_32"], 1)
                    t = bass.ds(t, 1)
                    act.activation(yT[:, g * BH:(g + 1) * BH, t].rearrange("p b t -> p (b t)"), opre[:, g, :], ACT.Tanh) \
                       .then_inc(sem["y_st"], 1)
                if gates:
                    g, t = gates
                    act.wait_ge(sem["g_sum"], nth(g, t))
                    act.activation(gact[:, g, :], gsum[:, g, :], ACT.Tanh, scale=0.5).then_inc(sem["g_act"], 1)
                if main:
                    g, t = main
                    act.wait_ge(sem["s_sum"], nth(g, t))
                    act.activation(esp[:, g, 0, :], ssum[:, g, :], ACT.Exp, scale=0.5).then_inc(sem["e_hi"], 1)
                    act.activation(e32[:, g, :], ssum[:, g, :], ACT.Exp, scale=0.5).then_inc(sem["e_32"], 1)
                if gates:
                    g, t = gates
                    act.wait_ge(sem["c_new"], nth(g, t))
                    act.activation(tanhc[:, g, :], c2[:, g, :], ACT.Tanh, scale=0.5).then_inc(sem["c_tanh"], 1)

            lstm_loop(act, half)

            act.preload_act_table_set("natural_log_exp_and_others")
            ln_rstd(4)
            step(act.activation(aneg[:, :], v("alog", 0, ML * MC * MN), ACT.Exp))
            step(act.activation(aneg[:, :], aneg[:, :], ACT.Copy, scale=-1.0))
            for l in range(ML):
                act.preload_act_table_set("silu_and_others")
                act.wait_ge(sem["m_uz"], 2 * l + 1)
                act.wait_ge(sem["m_const"], MC + 5)
                for ch in range(MC):
                    u = bank[0][:, ch * TOK:(ch + 1) * TOK]
                    act.activation(up[:, ch, :, MK - 1:], u.rearrange("p (b t) -> p b t", b=B), ACT.Copy)
                    act.activation(T[:, 0, ch * TOK:(ch + 1) * TOK], u, ACT.Identity, bias=v("convb", l * MC + ch),
                                   scale=v("convw", (l * MC + ch) * MK + MK - 1)).then_inc(sem["m_up"], 1)
                act.wait_ge(sem["m_uz"], 2 * l + 2)
                act.activation(T[:, 2, :], bank[1][:, :], ACT.Silu)
                for ch in range(MC):
                    half = slice(ch * TOK, (ch + 1) * TOK)
                    act.wait_ge(sem["m_conv"], l * MC + ch + 1)
                    act.activation(T[:, 1, half], T[:, 0, half], ACT.Silu).then_inc(sem["m_us"], 1)
                act.preload_act_table_set("natural_log_exp_and_others")
                act.wait_ge(sem["m_dps"], l + 1)
                for ch in range(MC):
                    half = slice(ch * TOK, (ch + 1) * TOK)
                    step.mark(act.activation(T[:, 3, half], bank[4][:, half], ACT.Abs, bias=v("dtb", l * MC + ch)))
                step.sync()
                step(act.activation(T[:, 4, :], T[:, 3, :], ACT.Exp, scale=-1.0))
                step(act.activation(T[:, 5, :], T[:, 4, :], ACT.Ln, bias=two))
                act.activation(T[:, 5, :], T[:, 5, :], ACT.Exp, scale=-1.0).then_inc(sem["m_e"], 1)
                for ch in range(MC):
                    half = slice(ch * TOK, (ch + 1) * TOK)
                    act.activation(T[:, 12, half], bank[4][:, half], ACT.Relu, bias=v("dtb", l * MC + ch))
                act.wait_ge(sem["m_z"], l + 1)
                step(act.activation(T[:, 13, :], T[:, 3, :], ACT.Square))
                for k in range(2):
                    act.activation(T[:, 14 + k, :], T[:, 13, :], ACT.Square, bias=shifts[k]).then_inc(sem["m_sq"], 1)

                def copy_b(i):
                    n = l * MNP + i
                    act.wait_ge(sem["m_bps"], n + 1)
                    if n >= 2:
                        act.wait_ge(sem["m_dbu0"], n - 1)
                        act.wait_ge(sem["m_dbu1"], n - 1)
                    act.activation(T[:, 8 + i % 2, :], bank[2 + i % 2][:, :], ACT.Copy).then_inc(sem["m_bsb"], 1)

                copy_b(0)
                act.wait_ge(sem["m_delta"], 3 * l + 1)
                for i in range(MNP):
                    n = l * MNP + i
                    for ch in range(MC):
                        for k in range(2):
                            at = (l * MC + ch) * MN + 2 * i + k
                            seqs = decay[ch][:, (2 * i + k) * TOK:(2 * i + k + 1) * TOK].rearrange("p (b t) -> p b t", b=B)
                            ins = act.activation(seqs[:, :, 1:], T[:, 6, ch * TOK:(ch + 1) * TOK]
                                                 .rearrange("p (b t) -> p b t", b=B)[:, :, 1:],
                                                 ACT.Exp, scale=aneg[:, at:at + 1])
                        ins.then_inc(sem["m_dA"], 1)
                    if i + 1 < MNP:
                        copy_b(i + 1)
                    act.wait_ge(sem["m_cps"], n + 1)
                    if n >= 2:
                        act.wait_ge(sem["m_hc0"], n - 1)
                        act.wait_ge(sem["m_hc1"], n - 1)
                    act.activation(T[:, 10 + i % 2, :], bank[5 + i % 2][:, :], ACT.Copy).then_inc(sem["m_csb"], 1)
                ln_rstd(5 + l)

            ln_rstd(5 + ML)
            act.wait_ge(sem["f_sub"], 2)
            act.activation(lg[:, :, :], lg[:, :, :], ACT.Exp).then_inc(sem["f_exp"], 1)
            for fc in range(FC):
                half = slice((fc % 2) * TOK, (fc % 2) * TOK + TOK)
                act.wait_ge(sem["r_h"], fc + 1)
                act.activation(T[:, fc // 2, half], bank[fc][:, 0:TOK], ACT.Relu, bias=v("wib", fc)) \
                   .then_inc(sem["r_act"], 1)

        @block.vector
        def _(dve):
            step = Steps(dve, sem["dve_step"])
            dve.memset(eps5[:, :], 1e-5).then_inc(sem["eps_ready"], 1)
            dve.memset(eps6[:, :], 1e-6).then_inc(sem["eps_ready"], 1)

            def layernorm(n, src, affine=None):
                for j in range(NJ):
                    step.mark(dve.bn_stats(bn[:, j, :], src[:, j, :]))
                step.sync()
                for j in range(NJ):
                    ins = dve.bn_aggr(mv[:, j, :], bn[:, j, :])
                    if j < NJ - 1:
                        step.mark(ins)
                ins.then_inc(sem["ln_var"], 1)
                if affine is not None:
                    dve.wait_ge(sem["ln_var"], n + 1)
                    step.sync()
                    for j in range(NJ):
                        step.mark(dve.scalar_tensor_tensor(out=xn[:, j, :], in0=src[:, j, :], scalar=mv[:, j, 0:1],
                                                           in1=r("lnw", affine * D, D), op0=ALU.subtract, op1=ALU.mult))
                dve.wait_ge(sem["ln_rstd"], n + 1)
                step.sync()
                for j in range(NJ):
                    if affine is not None:
                        ins = dve.scalar_tensor_tensor(out=xn[:, j, :], in0=xn[:, j, :], scalar=rs[:, j:j + 1],
                                                       in1=r("lnb", affine * D, D), op0=ALU.mult, op1=ALU.add)
                    else:
                        ins = dve.tensor_scalar(xn[:, j, :], src[:, j, :], mv[:, j, 0:1], rs[:, j:j + 1],
                                                ALU.subtract, ALU.mult)
                ins.then_inc(sem["ln_xn"], 1)
                if n != LN_LAST:
                    dve.wait_ge(sem["ln_tr"], transposed(n))
                    dve.tensor_copy(xnT[:, :], bank[7][:, 0:TOK]).then_inc(sem["ln_xT"], 1)

            dve.wait_ge(sem["d_x"], 16)
            layernorm(0, x_in)
            dve.wait_ge(sem["xw_ps"], 1)
            dve.tensor_copy(xw[:, :], bank[6][:, 0:2 * D + 2]).then_inc(sem["xw_sb"], 1)
            dve.wait_ge(sem["d_par"], 48)

            def k_hat(s):
                w, p = (TOK if s == 0 else SK), s % 2
                dve.wait_ge(sem["k_rstd"], s + 1)
                if s >= 2:
                    dve.wait_ge(sem["k_done"], s - 1)
                dve.scalar_tensor_tensor(out=T[:, 8 + p, 0:w], in0=T[:, CENTRED[s % 3], 0:w], scalar=v("qw" if s == 0 else "kw"),
                                         in1=T[:, 6 + p, 0:w], op0=ALU.mult, op1=ALU.mult) \
                   .then_inc(sem["k_hat"], 1)

            def v_evac(b):
                dve.wait_ge(sem["v_proj"], b + 1)
                dve.tensor_copy(pat(vx[:, b * KC, :], [[1, SK]]), bank[4 + b % 2][:, :]).then_inc(sem["v_evac"], 1)

            def q_blocks(first):
                if first == 0:
                    dve.wait_ge(sem["k_done"], 1)
                    dve.wait_ge(sem["mask_ready"], 1)
                for h in (first, first + 1):
                    ins = dve.tensor_scalar(qblk[:, h // 4, :, h % 4, :], T[:, 10, 0:TOK].rearrange("p (b s) -> p b s", b=B),
                                            cst[:, C_HM16 + h:C_HM16 + h + 1], None, ALU.mult)
                ins.then_inc(sem["qblk_ready"], 1)

            for s in range(1 + B):
                if s < B:
                    v_evac(s)
                k_hat(s)
                if s >= 1:
                    q_blocks(2 * (s - 1))
            dve.wait_ge(sem["d_attn"], 32)
            step(dve.tensor_reduce(wmean[:, :], wqkv[:, 0:2 * AH * AD].rearrange("p (h d) -> p h d", d=AD), AX, ALU.add))
            dve.tensor_scalar(wmean[:, :], wmean[:, :], 1.0 / AD, None, ALU.mult).then_inc(sem["a_wmean"], 1)

            def x_max(i):
                b = i // XG
                if i == 0:
                    dve.wait_ge(sem["mask_ready"], 2)
                dve.wait_ge(sem["x_score"], i + 1)
                if i >= 2:
                    dve.wait_ge(sem["x_exp"], i - 1)
                step(dve.tensor_tensor_reduce(T[:, i % 2, :], bank[i % 2][:, :], maskb[:, b * SK:(b + 1) * SK],
                                              1.0, FLOOR, ALU.add, ALU.max, xmax[:, i:i + 1]))
                dve.tensor_scalar(xneg[:, i:i + 1], xmax[:, i:i + 1], -1.0, None, ALU.mult) \
                   .then_inc(sem["x_max"], 1)

            def x_norm(i):
                dve.wait_ge(sem["x_exp"], i + 1)
                step(dve.reciprocal(xrz[:, i:i + 1], xz[:, i:i + 1]))
                if i >= 2:
                    dve.wait_ge(sem["x_tr"], i - 1)
                dve.tensor_scalar(T[:, 4 + i % 2, :], T[:, 2 + i % 2, :], xrz[:, i:i + 1], None, ALU.mult) \
                   .then_inc(sem["x_norm"], 1)

            def x_heads(b):
                dve.wait_ge(sem["x_pv"], XG * (b + 1))
                dve.wait_ge(sem["x_oT"], b) if b else None
                o = bank[4 + b % 2]
                step(dve.tensor_tensor(T[:, 8, 0:P].rearrange("p (h q) -> p h q", h=4),
                                       o[:, 0:P].rearrange("p (h q) -> p h q", h=4),
                                       pat(cst[:, C_HM:C_HM + 4], [[1, 4], [0, S]]), ALU.mult))
                dve.tensor_reduce(oT[:, b * S:(b + 1) * S], pat(T[:, 8, :], [[1, S], [S, 4]]), AX, ALU.add) \
                   .then_inc(sem["x_oT"], 1)

            for i in range(B * XG + 4):
                if i < B * XG:
                    x_max(i)
                if 1 <= i <= B * XG:
                    x_norm(i - 1)
                if i >= 4 and (i - 4) % XG == XG - 1:
                    x_heads((i - 4) // XG)
            dve.wait_ge(sem["x_oT"], B)
            dve.tensor_scalar(oT[:, :], oT[:, :], v("bv"), None, ALU.add).then_inc(sem["x_oT"], 1)
            dve.wait_ge(sem["xb_ready"], 1)
            dve.wait_ge(sem["x_o"], 1)
            dve.tensor_tensor(xres[:, :, :], xbias[:, :, :], bank[6][:, 0:TOK].rearrange("p (j d) -> p j d", j=NJ),
                              ALU.add).then_inc(sem["x_res"], 1)

            dve.wait_ge(sem["x_res"], 1)
            layernorm(1, xres)
            cos = pat(cst[:, C_COS:C_COS + S], [[0, 2 * B], [1, S]])
            sin = pat(cst[:, C_SIN:C_SIN + S], [[0, 2 * B], [1, S]])

            def by_time(t):
                return t.rearrange("p (n s) -> p n s", s=S)

            def a_z0(m):
                dve.wait_ge(sem["a_rstd"], m + 1)
                if m >= 2:
                    dve.wait_ge(sem["a_z"], m - 1)
                dve.scalar_tensor_tensor(out=T[:, 6 + m % 2, :], in0=bank[QK[m % 3]][:, :],
                                         scalar=v("aqw" if m < 4 else "akw"), in1=T[:, 4 + m % 2, :],
                                         op0=ALU.mult, op1=ALU.mult).then_inc(sem["a_z0"], 1)

            def a_rope(m):
                p = m % 2
                dve.wait_ge(sem["a_z"], m + 1)
                if m >= 2:
                    dve.wait_ge(sem["a_rope"], m - 1)
                step.mark(dve.tensor_tensor(by_time(T[:, 10 + p, :]), by_time(T[:, 8 + p, :]), cos, ALU.mult))
                dve.wait_ge(sem["a_rot"], m + 1)
                dve.tensor_tensor(by_time(T[:, 12 + p, :]), by_time(bank[4 + p][:, :]), sin, ALU.mult) \
                   .then_inc(sem["a_t2"], 1)
                step.sync()
                dve.wait_ge(sem["a_t2"], m + 1)
                dve.tensor_tensor(kT[:, m * 512:(m + 1) * 512], T[:, 10 + p, :], T[:, 12 + p, :], ALU.add) \
                   .then_inc(sem["a_rope"], 1)

            for m in range(9):
                if m < 8:
                    a_z0(m)
                if m >= 1:
                    a_rope(m - 1)
            dve.wait_ge(sem["a_rope"], 8)

            def heads(t):
                return t.rearrange("p (h k) -> p h k", h=AH)

            def over_keys(t):
                return pat(t, [[1, AH], [0, S]])

            for j in range(NJ):
                dve.wait_ge(sem["a_score"], j + 1)
                for odd in range(2):
                    step.mark(dve.scalar_tensor_tensor(
                        out=pat(T[:, j, :], [[2 * S, AH // 2], [1, S]], odd * S),
                        in0=bank[j + 2 * odd][:, 0:AH // 2 * S].rearrange("p (h k) -> p h k", k=S), scalar=AD ** -0.5,
                        in1=pat(cst[:, C_CAUSAL:C_CAUSAL + S], [[0, AH // 2], [1, S]]), op0=ALU.mult, op1=ALU.add))
                step.sync()
                step(dve.tensor_reduce(am[:, j, :], heads(T[:, j, :]), AX, ALU.max))
                step(dve.tensor_tensor(am[:, j, :], am[:, j, :], v("sink", 0, AH), ALU.max))
                step.mark(dve.tensor_tensor(asink[:, j, :], v("sink", 0, AH), am[:, j, :], ALU.subtract))
                step.sync()
                dve.tensor_tensor(heads(T[:, 2 + j, :]), heads(T[:, j, :]), over_keys(am[:, j, :]), ALU.subtract) \
                   .then_inc(sem["a_sub"], 1)
            for j in range(NJ):
                dve.wait_ge(sem["a_exp"], j + 1)
                step(dve.tensor_reduce(az[:, j, :], heads(T[:, 4 + j, :]), AX, ALU.add))
                step(dve.tensor_tensor(az[:, j, :], az[:, j, :], asink[:, j, :], ALU.add))
                step(dve.reciprocal(az[:, j, :], az[:, j, :]))
                step(dve.tensor_tensor(heads(T[:, 6 + j, :]), heads(T[:, 4 + j, :]), over_keys(az[:, j, :]), ALU.mult))
                dve.wait_ge(sem["a_zero"], 1)
                for b in range(BT):
                    part = slice(b * S, (b + 1) * S)
                    ins = dve.transpose(aprobT[part, j, :, part], heads(T[part, 6 + j, :]))
                ins.then_inc(sem["a_pt"], 1)
            dve.wait_ge(sem["a_pv"], NJ)
            dve.tensor_copy(T[:, 11, :], bank[5][:, :]).then_inc(sem["a_oTd"], 1)
            dve.wait_ge(sem["xb_ready"], 2)
            dve.wait_ge(sem["a_o"], NJ)
            dve.tensor_tensor(xres[:, :, :], xbias[:, :, :], bank[6][:, 0:TOK].rearrange("p (j d) -> p j d", j=NJ),
                              ALU.add).then_inc(sem["x_res"], 1)

            dve.wait_ge(sem["x_res"], 2)
            layernorm(2, xres)

            def over_experts(t):
                return pat(t, [[1, NJ], [0, E]])

            def gate_softmax():
                step(dve.tensor_reduce(gm[:, :], lg[:, :, :], AX, ALU.max))
                dve.tensor_tensor(lg[:, :, :], lg[:, :, :], over_experts(gm[:, :]), ALU.subtract).then_inc(sem["f_sub"], 1)
                gate_softmax.n += 1
                dve.wait_ge(sem["f_exp"], gate_softmax.n)
                step(dve.tensor_reduce(gz[:, :], lg[:, :, :], AX, ALU.add))
                step(dve.reciprocal(gz[:, :], gz[:, :]))
                step(dve.tensor_tensor(lg[:, :, :], lg[:, :, :], over_experts(gz[:, :]), ALU.mult))
                for j in range(NJ):
                    step.mark(dve.max(m8[:, j, :], lg[:, j, :]))
                step.sync()
                for j in range(NJ):
                    step.mark(dve.max_index(i8[:, j, :], m8[:, j, :], lg[:, j, :]))
                step.sync()
                step(dve.tensor_copy(i8f[:, :, :], i8[:, :, :]))

            gate_softmax.n = 0
            def l_rest(i):
                dve.wait_ge(sem["l_hi"], i + 2)
                if i >= 2:
                    dve.wait_ge(sem["l_split"], i)
                at = i // 2 * SK
                dve.tensor_tensor(T[:, 8 + i % 2, :], bank[6 + i % 2][:, :], (vs if i % 2 else ks)[0][:, at:at + SK],
                                  ALU.subtract).then_inc(sem["l_rest"], 1)

            iota = cst[:, C_IOTA:C_IOTA + E]
            dve.wait_ge(sem["f_gate"], 1)
            step(dve.tensor_copy(lg[:, :, :], bank[6][:, 0:NJ * E].rearrange("p (j e) -> p j e", j=NJ)))
            gate_softmax()
            step(dve.tensor_reduce(gm[:, :], m8[:, :, 0:2], AX, ALU.add))
            step(dve.tensor_scalar(gm[:, :], gm[:, :], 1e-9, None, ALU.add))
            step(dve.reciprocal(gm[:, :], gm[:, :]))
            step(dve.tensor_tensor(gw[:, :, :], m8[:, :, 0:2], pat(gm[:, :], [[1, NJ], [0, 2]]), ALU.mult))
            for j in range(NJ):
                for k in range(2):
                    step.mark(dve.tensor_scalar(cw[:, k, j, :], iota, i8f[:, j, k:k + 1], gw[:, j, k:k + 1],
                                                ALU.is_equal, ALU.mult))
            step.sync()
            dve.tensor_tensor(cw[:, 2, :, :], cw[:, 0, :, :], cw[:, 1, :, :], ALU.add).then_inc(sem["f_cw"], 1)
            dve.wait_ge(sem["f_cwps"], 1)
            dve.tensor_copy(cwT[0:E, :], bank[7][0:E, 0:TOK]).then_inc(sem["f_cwT"], 1)
            dve.wait_ge(sem["xb_ready"], 3)
            dve.wait_ge(sem["f_cw"], 1)
            for e in range(E + 1):
                dve.wait_ge(sem["f_y"], e + 1)
                if e:
                    dve.wait_ge(sem["f_acc"], NJ * e)
                for j in range(NJ):
                    ins = (dve.scalar_tensor_tensor(out=facc[:, j, :], in0=bank[4 + e % 2][:, j * D:(j + 1) * D],
                                                       scalar=cw[:, 2, j, e:e + 1] if e < E else 0.1,
                                                       in1=facc[:, j, :], op0=ALU.mult, op1=ALU.add))
                    ins.then_inc(sem["f_acc"], 1)
                if e == 0:
                    step(dve.tensor_tensor(gbias[:, :], v("bih", 0, 4), v("bhh", 0, 4), ALU.add))
                    dve.tensor_scalar(gbias[:, 3:4], gbias[:, 3:4], 2.0, None, ALU.mult).then_inc(sem["l_gbias"], 1)
                    zeroed = (hsp[:, :, :, :], asp[:, :, :, :], negmax[:, :, :], c2[:, :, :])
                    for t in zeroed:
                        dve.memset(t, 0.0).then_inc(sem["l_zero"], 1)
                    dve.memset(ones[:, :], 1.0).then_inc(sem["l_zero"], 1)
                    dve.wait_ge(sem["l_hi"], 1)
                    dve.tensor_tensor(T[:, 10:13, :].rearrange("p n d -> p (n d)")[:, 0:9 * D], lw[:, 4 * D:13 * D],
                                      lsp[:, 0, :], ALU.subtract).then_inc(sem["l_rest"], 1)
                if e < B:
                    l_rest(2 * e)
                    l_rest(2 * e + 1)
            dve.wait_ge(sem["f_acc"], NJ * (E + 1))
            dve.wait_ge(sem["f_b2"], 1)
            dve.tensor_tensor(xres[:, :, :], facc[:, :, :], bank[5][:, 0:TOK].rearrange("p (j d) -> p j d", j=NJ),
                              ALU.add).then_inc(sem["x_res"], 1)

            dve.wait_ge(sem["x_res"], 3)
            layernorm(3, xres)
            dve.wait_ge(sem["l_zero"], 3 + len(zeroed))

            def parts(t, n):
                return pat(t, [[1, n], [n, 3]])

            for g in range(4):
                dve.wait_ge(sem["l_gx"], g + 1)
                whole, rest = (t[:, :, g * B:(g + 1) * B] for t in (gx32, gxrest))
                high, mid, low = (gx[:, 0:S, k, g, :] for k in range(3))
                step.mark(dve.tensor_tensor(mid, whole, high, ALU.subtract))
                step(dve.tensor_tensor(rest, whole, high, ALU.subtract))
                dve.tensor_tensor(low, rest, mid, ALU.subtract).then_inc(sem["l_gxlow"], 1)

            def half(main=None, out=None, gates=None):
                if out:
                    g, t = out
                    dve.wait_ge(sem["v_ps"], nth(g, t))
                    step(dve.tensor_reduce(opre[:, g, :], parts(bank[6][:, 0:1], BH), AX, ALU.add))
                    step.mark(dve.tensor_tensor(opre[:, g, :], opre[:, g, :], rz[:, g, :], ALU.mult))
                if main:
                    g, t = main
                    dve.wait_ge(sem["s_hi"], nth(g, t))
                    dve.tensor_reduce(mc[:, g, :], bank[1][:, 0:BH * KC].rearrange("p (b c) -> p b c", c=KC), AX, ALU.max) \
                       .then_inc(sem["m_c"], 1)
                if out:
                    g, t = out
                    step.sync()
                    dve.tensor_tensor(opre[:, g, :], opre[:, g, :], oh[:, g, :], ALU.add).then_inc(sem["o_pre"], 1)
                    g, t = out
                    dve.wait_ge(sem["at_32"], nth(g, t))
                    dve.tensor_tensor(asp[:, g, 1, :], a32[:, g, :], asp[:, g, 0, :], ALU.subtract).then_inc(sem["at_mid"], 1)
                    step.mark(dve.tensor_tensor(arest[:, g, :], a32[:, g, :], asp[:, g, 0, :], ALU.subtract))
                if main:
                    g, t = main
                    dve.wait_ge(sem["m_t"], nth(g, t))
                    step.mark(dve.tensor_reduce(m1[:, g:g + 1], bank[3][0:BH, 0:P], AX, ALU.max))
                step.sync()
                if main:
                    g, t = main
                    dve.tensor_scalar(negmax[0:BH, g, :], cst[0:BH, C_NEG:C_NEG + BH * KC], m1[:, g:g + 1], None, ALU.mult) \
                       .then_inc(sem["m_d"], 1)
                if out:
                    g, t = out
                    dve.wait_ge(sem["at_mid"], nth(g, t))
                    dve.tensor_tensor(asp[:, g, 2, :], arest[:, g, :], asp[:, g, 1, :], ALU.subtract).then_inc(sem["at_lo"], 1)
                if gates:
                    g, t = gates
                    dve.wait_ge(sem["g_ps"], nth(g, t))
                    dve.tensor_reduce(gsum[:, g, :], parts(bank[GATES[g]][:, 0:1], 4 * BH), AX, ALU.add) \
                       .then_inc(sem["g_sum"], 1)
                if main:
                    g, t = main
                    dve.wait_ge(sem["s_ps"], nth(g, t))
                    dve.tensor_reduce(ssum[:, g, :], parts(bank[2][:, 0:1], BH * KC), AX, ALU.add).then_inc(sem["s_sum"], 1)
                if gates:
                    g, t = gates
                    dve.wait_ge(sem["g_act"], nth(g, t))
                    i, f, o, gg = (gact[:, g, k * BH:(k + 1) * BH] for k in range(4))
                    step.mark(dve.scalar_tensor_tensor(out=fc2[:, g, :], in0=f, scalar=1.0, in1=c2[:, g, :],
                                                       op0=ALU.add, op1=ALU.mult))
                    step.mark(dve.scalar_tensor_tensor(out=ig[:, g, :], in0=i, scalar=1.0, in1=gg,
                                                       op0=ALU.add, op1=ALU.mult))
                    step.sync()
                    dve.scalar_tensor_tensor(out=c2[:, g, :], in0=fc2[:, g, :], scalar=0.5, in1=ig[:, g, :],
                                             op0=ALU.mult, op1=ALU.add).then_inc(sem["c_new"], 1)
                if main:
                    g, t = main
                    dve.wait_ge(sem["e_32"], nth(g, t))
                    dve.tensor_tensor(esp[:, g, 1, :], e32[:, g, :], esp[:, g, 0, :], ALU.subtract).then_inc(sem["e_mid"], 1)
                    step(dve.tensor_tensor(erest[:, g, :], e32[:, g, :], esp[:, g, 0, :], ALU.subtract))
                    dve.wait_ge(sem["e_mid"], nth(g, t))
                    dve.tensor_tensor(esp[:, g, 2, :], erest[:, g, :], esp[:, g, 1, :], ALU.subtract).then_inc(sem["e_lo"], 1)
                if gates:
                    g, t = gates
                    dve.wait_ge(sem["c_tanh"], nth(g, t))
                    dve.scalar_tensor_tensor(out=hsp[:, g, 0, :], in0=o, scalar=1.0, in1=tanhc[:, g, :],
                                             op0=ALU.add, op1=ALU.mult).then_inc(sem["h_hi"], 1)
                    step(dve.scalar_tensor_tensor(out=h32[:, g, :], in0=o, scalar=1.0, in1=tanhc[:, g, :],
                                                  op0=ALU.add, op1=ALU.mult))
                    dve.wait_ge(sem["h_hi"], nth(g, t))
                    dve.tensor_tensor(hsp[:, g, 1, :], h32[:, g, :], hsp[:, g, 0, :], ALU.subtract).then_inc(sem["h_mid"], 1)
                    step(dve.tensor_tensor(hrest[:, g, :], h32[:, g, :], hsp[:, g, 0, :], ALU.subtract))
                    dve.wait_ge(sem["h_mid"], nth(g, t))
                    dve.tensor_tensor(hsp[:, g, 2, :], hrest[:, g, :], hsp[:, g, 1, :], ALU.subtract).then_inc(sem["h_lo"], 1)
                if main:
                    g, t = main
                    dve.wait_ge(sem["oh_ps"], nth(g, t))
                    step.mark(dve.tensor_reduce(oh[:, g, :], parts(bank[5][:, 0:1], BH), AX, ALU.add))
                    dve.wait_ge(sem["z_ps"], nth(g, t))
                    step(dve.tensor_reduce(zs[:, g, :], pat(bank[4][:, 0:1], [[KC, BH], [BH * KC, 3], [1, KC]]),
                                           mybir.AxisListType.XY, ALU.add))
                    step.mark(dve.tensor_scalar(oh[:, g, :], oh[:, g, :], v("bout"), None, ALU.add))
                    step.mark(dve.reciprocal(rz[:, g, :], zs[:, g, :]))

            for t, x in ((up[:, :, :, :], 0.0), (two, 2.0), (shifts[0], SHIFTS[0]), (shifts[1], SHIFTS[1])):
                dve.memset(t, x).then_inc(sem["m_const"], 1)
            dve.tensor_copy(sel[:, :], cst[0:6 * MN, C_SEL:C_SEL + 2 * MN]).then_inc(sem["m_const"], 1)
            lstm_loop(dve, half, step)
            dve.wait_ge(sem["y_tr"], 1)
            dve.tensor_tensor(xres[:, :, :], xres[:, :, :], bank[7][:, 0:TOK].rearrange("p (j d) -> p j d", j=NJ),
                              ALU.add).then_inc(sem["x_res"], 1)

            dve.wait_ge(sem["x_res"], 4)
            layernorm(4, xres)
            z, delta, du = (T[:, i, :] for i in (3, 6, 7))
            for l in range(ML):
                for ch in range(MC):
                    acc = T[:, 0, ch * TOK:(ch + 1) * TOK].rearrange("p (b t) -> p b t", b=B)
                    dve.wait_ge(sem["m_up"], l * MC + ch + 1)
                    for k in range(MK - 1):
                        ins = dve.scalar_tensor_tensor(out=acc, in0=up[:, ch, :, k:k + S],
                                                       scalar=v("convw", (l * MC + ch) * MK + k), in1=acc,
                                                       op0=ALU.mult, op1=ALU.add)
                        if k < MK - 2:
                            step(ins)
                    ins.then_inc(sem["m_conv"], 1)
                dve.wait_ge(sem["m_bc"], l + 1)
                dve.tensor_copy(dts[:, :], bank[2][6 * MN:6 * MN + MR, 0:TOK]).then_inc(sem["m_dts"], 1)
                bc, rest = bank[2][0:6 * MN, 0:TOK], T[0:6 * MN, 15, 0:TOK]
                step(dve.tensor_copy(bcs[:, :], bc))
                for k in (1, 2):
                    for q in range(k, 3):
                        part = slice(q * 2 * MN, (q + 1) * 2 * MN)
                        step.mark(dve.tensor_tensor(rest[part, :], (bc if k == 1 else rest)[part, :], bcs[part, :],
                                                    ALU.subtract))
                    step.sync()
                    for q in range(k, 3):
                        part = slice(q * 2 * MN, (q + 1) * 2 * MN)
                        ins = dve.tensor_copy(bcs[part, :], rest[part, :])
                        if k == 1:
                            step.mark(ins)
                    step.sync()
                ins.then_inc(sem["m_bcs"], 1)
                dve.wait_ge(sem["m_us"], (l + 1) * MC)
                for ch in range(MC):
                    half = slice(ch * TOK, (ch + 1) * TOK)
                    dve.tensor_scalar(T[:, 0, half], T[:, 1, half], v("mD", l * MC + ch), None, ALU.mult) \
                       .then_inc(sem["m_ud"], 1)
                dve.wait_ge(sem["m_e"], l + 1)
                dve.tensor_tensor(z, T[:, 4, :], T[:, 5, :], ALU.mult).then_inc(sem["m_z"], 1)
                dve.wait_ge(sem["m_z"], l + 1)
                for k in range(2):
                    dve.wait_ge(sem["m_sq"], 2 * l + k + 1)
                    step(dve.scalar_tensor_tensor(out=T[:, 4 + k, :], in0=T[:, 14 + k, :], scalar=PLUS[k],
                                                  in1=z if k == 0 else T[:, 4, :], op0=ALU.add, op1=ALU.mult))
                dve.scalar_tensor_tensor(out=delta, in0=T[:, 5, :], scalar=LEAD, in1=T[:, 12, :],
                                         op0=ALU.mult, op1=ALU.add).then_inc(sem["m_delta"], 1)
                dve.wait_ge(sem["m_delta"], 3 * l + 1)
                for ch in (1, 0):
                    half = slice(ch * TOK, (ch + 1) * TOK)
                    dve.tensor_tensor(du[:, half], delta[:, half], T[:, 1, half], ALU.mult).then_inc(sem["m_delta"], 1)
                dve.wait_ge(sem["m_delta"], 3 * l + 3)
                if l:
                    dve.wait_ge(sem["m_y"], l)

                def du_b(i):
                    dve.wait_ge(sem["m_bsb"], l * MNP + i + 1)
                    dve.tensor_tensor(pairs(state[0], i), over_pair(du[:, 0:TOK]), both(T[:, 8 + i % 2, :]), ALU.mult) \
                       .then_inc(sem["m_dbu0"], 1)

                du_b(0)
                for i in range(MNP):
                    n = l * MNP + i
                    if i + 1 < MNP:
                        du_b(i + 1)
                    at = slice(i * 2 * TOK, (i + 1) * 2 * TOK)
                    for ch in range(MC):
                        dve.wait_ge(sem["m_dbu0" if ch == 0 else "m_dbu1"], n + 1)
                        dve.wait_ge(sem["m_dA"], 2 * n + ch + 1)
                        dve.tensor_tensor_scan(out=state[ch][:, at], data0=decay[ch][:, at], data1=state[ch][:, at],
                                               initial=0.0, op0=ALU.mult, op1=ALU.add) \
                           .then_inc(sem["m_scan0" if ch == 0 else "m_scan1"], 1)
                    dve.wait_ge(sem["m_csb"], n + 1)
                    dve.wait_ge(sem["m_scan0"], n + 1)
                    dve.tensor_tensor(pairs(state[0], i), pairs(state[0], i), both(T[:, 10 + i % 2, :]), ALU.mult) \
                       .then_inc(sem["m_hc0"], 1)
                dve.wait_ge(sem["m_y"], l + 1)
                for ch in range(MC):
                    half = slice(ch * TOK, (ch + 1) * TOK)
                    dve.tensor_tensor(T[:, 13, half], bank[0][:, half], T[:, 2, half], ALU.mult).then_inc(sem["m_ys"], 1)
                dve.wait_ge(sem["m_o"], l + 1)
                res = T[:, 3, 0:TOK].rearrange("p (j d) -> p j d", j=NJ)
                step(dve.tensor_tensor(res, xn[:, :, :], bank[4][:, 0:TOK].rearrange("p (j d) -> p j d", j=NJ), ALU.add))
                layernorm(5 + l, res, l)
            dve.wait_ge(sem["ln_xn"], LN_LAST + 1)
            step(dve.tensor_tensor(xres[:, :, :], xres[:, :, :], xn[:, :, :], ALU.add))
            layernorm(5 + ML, xres)
            step(dve.tensor_tensor(facc[:, :, :], xres[:, :, :], pat(r("wob"), [[0, NJ], [1, D]]), ALU.add))
            dve.wait_ge(sem["r_gate"], 1)
            step(dve.tensor_tensor(lg[:, :, :], bank[6][:, 0:NJ * E].rearrange("p (j e) -> p j e", j=NJ),
                                   pat(r("gateb", 0, E), [[0, NJ], [1, E]]), ALU.add))
            gate_softmax()
            for j in range(NJ):
                step.mark(dve.tensor_scalar(oneh[:, j, :], iota, i8f[:, j, 0:1], None, ALU.is_equal))
            step.sync()
            dve.wait_ge(sem["r_a"], 1)
            dve.tensor_tensor(loraa[:, :, :].rearrange("p j (e k) -> p (j e) k", k=LR),
                              bank[7][:, 0:NJ * E * LR].rearrange("p (n k) -> p n k", k=LR),
                              pat(oneh[:, :, :], [[1, NJ * E], [0, LR]]), ALU.mult).then_inc(sem["r_am"], 1)
            dve.wait_ge(sem["r_amps"], 1)
            dve.tensor_copy(cwT[:, :], bank[5][0:E * LR, 0:TOK]).then_inc(sem["r_amT"], 1)
            dve.wait_ge(sem["r_o"], 1)
            dve.tensor_tensor(xres[:, :, :], facc[:, :, :], bank[4][:, 0:TOK].rearrange("p (j d) -> p j d", j=NJ),
                              ALU.add).then_inc(sem["x_res"], 2)

        @block.tensor
        def _(pe):
            def ln_transpose(n):
                pe.wait_ge(sem["ln_xn"], n + 1)
                if n != LN_LAST:
                    for j in range(NJ):
                        ins = pe.transpose(bank[7][:, j * P:(j + 1) * P], xn[:, j, :], ident)
                    ins.then_inc(sem["ln_tr"], 1)

            pe.wait_ge(sem["d_par"], 48)
            cb8 = cst[:, C_CB8:C_CB8 + P]
            pe.matmul(bank[6][:, 0:D], wx[:, 0:D], cb8, start=True, stop=True)
            pe.matmul(bank[6][:, D:2 * D], wx[:, D:2 * D], cb8, start=True, stop=True)
            pe.matmul(bank[6][:, 2 * D:2 * D + 2], cb8, v("bq", 0, 2), start=True, stop=True).then_inc(sem["xw_ps"], 1)
            ln_transpose(0)
            pe.wait_ge(sem["xw_sb"], 1)

            def k_proj(s):
                if s >= 2:
                    pe.wait_ge(sem["k_sq"], s - 1)
                if s == 0:
                    pe.wait_ge(sem["ln_xT"], 1)
                    pe.matmul(bank[0][:, 0:TOK], xw[:, D:2 * D], xnT[:, :], start=True, stop=True) \
                      .then_inc(sem["k_proj"], 1)
                    return
                b = s - 1
                pe.wait_ge(d_ctx[b], 16)
                pe.matmul(bank[s % 2][:, :], xw[:, 0:D], ctxT[:, b * SK:(b + 1) * SK], start=True, stop=True) \
                  .then_inc(sem["k_proj"], 1)
                if b >= 2:
                    pe.wait_ge(sem["v_evac"], b - 1)
                for c in range(KC):
                    at = b * SK + c * P
                    ins = pe.matmul(bank[4 + b % 2][:, c * P:(c + 1) * P], ctxT[:, at:at + P], wx[:, 2 * D:3 * D],
                                    start=True, stop=True)
                ins.then_inc(sem["v_proj"], 1)

            def k_var(s):
                w, p = (TOK if s == 0 else SK), s % 2
                pe.wait_ge(sem["k_sq"], s + 1)
                if s >= 2:
                    pe.wait_ge(sem["k_rstd"], s - 1)
                pe.matmul(bank[2 + p][:, 0:w], cst[:, C_BLK8:C_BLK8 + P], T[:, 2 + p, 0:w], start=True, stop=True) \
                  .then_inc(sem["k_var"], 1)

            for s in range(2 + B):
                if s <= B:
                    k_proj(s)
                if s >= 1:
                    k_var(s - 1)

            def x_scores(i):
                b, g = divmod(i, XG)
                if i == 0:
                    pe.wait_ge(sem["qblk_ready"], B)
                    pe.wait_ge(sem["k_done"], 1 + B)
                    pe.wait_ge(sem["v_evac"], B)
                    pe.wait_ge(sem["k_rstd"], 1 + B)
                if i >= 2:
                    pe.wait_ge(sem["x_max"], i - 1)
                pe.matmul(bank[i % 2][:, :], qblk[:, g, b, :, :], kT[:, b * SK:(b + 1) * SK],
                          start=True, stop=True).then_inc(sem["x_score"], 1)

            def x_transpose(i):
                pe.wait_ge(sem["x_norm"], i + 1)
                if i >= 2:
                    pe.wait_ge(sem["x_pt"], i - 1)
                for c in range(KC):
                    ins = pe.transpose(bank[2 + i % 2][:, c * P:(c + 1) * P], T[:, 4 + i % 2, c * P:(c + 1) * P], ident)
                ins.then_inc(sem["x_tr"], 1)

            def x_pv(i):
                b, g = divmod(i, XG)
                pe.wait_ge(sem["x_pt"], i + 1)
                if g == 0 and b >= 2:
                    pe.wait_ge(sem["x_oT"], b - 1)
                for c in range(KC):
                    ins = pe.matmul(bank[4 + b % 2][32 * g:32 * g + 32, 0:P], vx[:, b * KC + c, 32 * g:32 * g + 32],
                                    T[:, 6 + i % 2, c * P:(c + 1) * P], start=(c == 0), stop=(c == KC - 1))
                ins.then_inc(sem["x_pv"], 1)

            for i in range(B * XG + 3):
                if i < B * XG:
                    x_scores(i)
                if 2 <= i < B * XG + 2:
                    x_transpose(i - 2)
                if i >= 3:
                    x_pv(i - 3)
            pe.wait_ge(sem["x_oT"], B + 1)
            for j in range(NJ):
                ins = pe.matmul(bank[6][:, j * D:(j + 1) * D], oT[:, j * P:(j + 1) * P], wx[:, 3 * D:4 * D],
                                start=True, stop=True)
            ins.then_inc(sem["x_o"], 1)

            ln_transpose(1)

            def a_proj(m):
                if m == 0:
                    pe.wait_ge(sem["a_wc"], 1)
                    pe.wait_ge(sem["ln_xT"], 2)
                if m >= 3:
                    pe.wait_ge(sem["a_z0"], m - 2)
                for h in range(2):
                    ins = pe.matmul(bank[QK[m % 3]][:, h * TOK:(h + 1) * TOK], wqkv[:, (2 * m + h) * P:(2 * m + h + 1) * P],
                                    xnT[:, :], start=True, stop=True)
                ins.then_inc(sem["a_proj"], 1)

            def a_var(m):
                pe.wait_ge(sem["a_sq"], m + 1)
                if m >= 2:
                    pe.wait_ge(sem["a_rstd"], m - 1)
                pe.matmul(bank[2 + m % 2][:, :], cst[:, C_BLK64:C_BLK64 + P], T[:, m % 2, :], start=True, stop=True) \
                  .then_inc(sem["a_var"], 1)

            def a_rot(m):
                pe.wait_ge(sem["a_z"], m + 1)
                if m >= 2:
                    pe.wait_ge(sem["a_t2"], m - 1)
                pe.matmul(bank[4 + m % 2][:, :], cst[:, C_ROT:C_ROT + P], T[:, 8 + m % 2, :], start=True, stop=True) \
                  .then_inc(sem["a_rot"], 1)

            def a_vproj(n):
                at = 2 * AH * AD + (n % 2) * 512
                pe.matmul(bank[4 + n][:, :], xnT[:, (n // 2) * P:(n // 2 + 1) * P], wqkv[:, at:at + 512],
                          start=True, stop=True).then_inc(sem["a_vproj"], 1)

            for m in range(10):
                if m < 8:
                    a_proj(m)
                if 1 <= m <= 8:
                    a_var(m - 1)
                if m >= 2:
                    a_rot(m - 2)
            pe.wait_ge(sem["a_rope"], 8)
            for j in range(NJ):
                for h in range(AH):
                    rowsh = slice(AD * (h % 2), AD * (h % 2) + AD)
                    for b in range(BT):
                        at = (h // 2) * TOK + (j * BT + b) * S
                        ins = pe.matmul(bank[j + 2 * (h % 2)][b * S:(b + 1) * S, h // 2 * S:(h // 2 + 1) * S], kT[rowsh, at:at + S],
                                        kT[rowsh, 4 * 512 + at:4 * 512 + at + S], start=True, stop=True)
                ins.then_inc(sem["a_score"], 1)
            def a_out(j):
                pe.wait_ge(sem["a_oT"], 2 + j)
                if j == 1:
                    pe.wait_ge(sem["a_oTd"], 1)
                for n in range(AH // 2):
                    ins = pe.matmul(bank[6][:, j * D:(j + 1) * D], T[:, 8 + 2 * j + n // 4, (n % 4) * P:(n % 4 + 1) * P],
                                    projT[:, n * D:(n + 1) * D], start=(n == 0), stop=(n == AH // 2 - 1))
                ins.then_inc(sem["a_o"], 1)

            for n in range(4):
                a_vproj(n)
            pe.wait_ge(sem["d_attn"], 32)
            for j in range(NJ):
                pe.wait_ge(sem["a_vev"], 4)
                pe.wait_ge(sem["a_pt"], j + 1)
                for h in range(AH):
                    o = bank[2 + 2 * j + h // 8]
                    ins = pe.matmul(o[AD * (h % 2):AD * (h % 2) + AD, (h // 2 % 4) * P:(h // 2 % 4 + 1) * P],
                                    avals[:, j, h * AD:(h + 1) * AD], aprobT[:, j, h, :], start=True, stop=True)
                ins.then_inc(sem["a_pv"], 1)
                a_out(j)

            ln_transpose(2)
            pe.wait_ge(sem["ln_xT"], 3)
            pe.wait_ge(sem["d_ffn"], 80)
            for j in range(NJ):
                ins = pe.matmul(bank[6][:, j * E:(j + 1) * E], xnT[:, j * P:(j + 1) * P], wg[:, :], start=True, stop=True)
            ins.then_inc(sem["f_gate"], 1)
            pe.wait_ge(sem["d_ffn"], 80)

            def f_hidden(e):
                if e >= 2:
                    pe.wait_ge(sem["f_act"], 2 * (e - 1))
                w = w1[:, e * F:(e + 1) * F] if e < E else ws[:, 0:F]
                for fc in range(FC):
                    half = slice((fc % 2) * TOK, (fc % 2) * TOK + TOK)
                    ins = pe.matmul(bank[2 * (e % 2) + fc // 2][:, half], w[:, fc * P:(fc + 1) * P], xnT[:, :],
                                    start=True, stop=True)
                    if fc % 2:
                        ins.then_inc(sem["f_h"], 1)

            def f_out(e):
                pe.wait_ge(sem["f_act"], 2 * (e + 1))
                if e >= 2:
                    pe.wait_ge(sem["f_acc"], NJ * (e - 1))
                w = w2[:, e * F:(e + 1) * F] if e < E else ws[:, F:2 * F]
                for j in range(NJ):
                    for fc in range(FC):
                        at = (fc % 2) * TOK + j * P
                        ins = pe.matmul(bank[4 + e % 2][:, j * D:(j + 1) * D], T[:, 2 * (e % 2) + fc // 2, at:at + P],
                                        w[:, fc * D:(fc + 1) * D], start=(fc == 0), stop=(fc == FC - 1))
                ins.then_inc(sem["f_y"], 1)

            def l_keys_values(b):
                if b == 0:
                    pe.wait_ge(sem["d_lw"], 16)
                    pe.wait_ge(sem["f_cwT"], 1)
                else:
                    pe.wait_ge(sem["l_rest"], 2 * b)
                pe.matmul(bank[6][:, :], lw[:, 14 * D:15 * D], ctxT[:, b * SK:(b + 1) * SK], start=True, stop=True) \
                  .then_inc(sem["l_kv"], 1)
                if b:
                    pe.wait_ge(sem["l_rest"], 2 * b + 1)
                for c in range(KC):
                    at = b * SK + c * P
                    ins = pe.matmul(bank[7][:, c * P:(c + 1) * P], ctxT[:, at:at + P], lw[:, 13 * D:14 * D],
                                    start=True, stop=True)
                ins.then_inc(sem["l_kv"], 1)

            for e in range(E + 2):
                if e <= E:
                    f_hidden(e)
                if e == 1:
                    pe.wait_ge(sem["f_cw"], 1)
                    for j in range(NJ):
                        ins = pe.transpose(bank[7][0:E, j * P:(j + 1) * P], cw[:, 2, j, :], ident)
                    ins.then_inc(sem["f_cwps"], 1)
                if e >= 1:
                    f_out(e - 1)
                if 1 <= e <= B:
                    l_keys_values(e - 1)
                if e == E:
                    pe.wait_ge(sem["f_acc"], NJ * E)
                    for j in range(NJ):
                        ins = pe.matmul(bank[5][:, j * D:(j + 1) * D], cwT[0:E, j * P:(j + 1) * P], b2[:, :],
                                        start=True, stop=True)
                    ins.then_inc(sem["f_b2"], 1)

            ln_transpose(3)
            pe.wait_ge(sem["ln_xT"], 4)
            for g in range(4):
                pe.matmul(bank[g][:, 0:TOK], lw[:, g * D:(g + 1) * D], xnT[:, :], start=True, stop=True) \
                  .then_inc(sem["l_gxps"], 1)

            def mm(out, lhsT, rhs, start=False, stop=False):
                return pe.matmul(out, lhsT, rhs, start=start, stop=stop, skip_group_check=True)

            def weight(k, m):
                return lsp[:, k, m * D:(m + 1) * D]

            MEETS = ((2, 1), (1, 2), (0, 3))

            def x_gates(g, t):
                mm(bank[GATES[g]][:, 0:12 * BH], identb, gx[:, bass.ds(t, 1), :, :, g * BH:(g + 1) * BH], start=True)

            def h_gates(g):
                for k, n in MEETS:
                    for m in range(4):
                        mm(pat(bank[GATES[g]][:, 0:1], [[4 * BH, n], [1, BH]], m * BH), weight(k, 4 + m), hsp[:, g, 0:n, :])

            def output_gates(gates, part):
                g, t = gates
                (k, n), ready = MEETS[part], ("at_hi", "at_mid", "at_lo")[part]
                if not (isinstance(t, int) and t == 0):
                    pe.wait_ge(sem[ready], nth(g, t - 1))
                for m in range(4):
                    ins = mm(pat(bank[GATES[g]][:, 0:1], [[4 * BH, n], [1, BH]], m * BH), weight(k, m), asp[:, g, 0:n, :],
                             stop=(part == 2))
                if part == 2:
                    ins.then_inc(sem["g_ps"], 1)

            def half(main=None, out=None, gates=None):
                if main is None:
                    if gates:
                        for part in range(3):
                            output_gates(gates, part)
                    return
                g, t = main

                def scores(k, n, start=False):
                    for i in range(BH * KC):
                        at = (g * BH * KC + i) * P
                        mm(pat(bank[2][:, 0:1], [[BH * KC, n]], i), ks[k][:, at:at + P],
                           pat(hsp[:, g, 0, 0:1], [[BH, n]], i // KC), start=(start and i == 0))

                pe.wait_ge(sem["h_hi"], nth(g, t))
                for i in range(BH * KC):
                    at = (g * BH * KC + i) * P
                    ins = mm(bank[1][:, i:i + 1], ks[0][:, at:at + P], hsp[:, g, 0, i // KC:i // KC + 1],
                             start=(i == 0), stop=True)
                ins.then_inc(sem["s_hi"], 1)
                pe.wait_ge(sem["h_mid"], nth(g, t))
                scores(1, 2, True)
                pe.wait_ge(sem["m_c"], nth(g, t))
                pe.transpose(bank[3][0:BH, 0:P], mc[:, g, :], ident).then_inc(sem["m_t"], 1)
                scores(2, 1)
                if gates:
                    output_gates(gates, 0)
                pe.wait_ge(sem["h_lo"], nth(g, t))
                scores(0, 3)
                if gates:
                    output_gates(gates, 1)
                if gates:
                    output_gates(gates, 2)
                pe.wait_ge(sem["m_d"], nth(g, t))
                mm(bank[2][:, 0:BH * KC], ones[:, :], negmax[:, g, :], stop=True).then_inc(sem["s_ps"], 1)
                x_gates(g, t + 1)
                h_gates(g)
                for k, n in MEETS:
                    ins = mm(bank[5][:, 0:n * BH], weight(k, 8), hsp[:, g, 0:n, :].rearrange("p k b -> p (k b)"),
                             start=(k == 2), stop=(k == 0))
                ins.then_inc(sem["oh_ps"], 1)

                def values(k, n):
                    for i in range(BH * KC):
                        at = (g * BH * KC + i) * P
                        ins = mm(pat(bank[6][:, 0:1], [[BH, n]], i // KC), vs[k][:, at:at + P],
                                 pat(esp[:, g, 0, 0:1], [[BH * KC, n]], i), start=(k == 2 and i == 0), stop=(k == 0))
                    return ins

                pe.wait_ge(sem["e_hi"], nth(g, t))
                values(2, 1)
                pe.wait_ge(sem["e_mid"], nth(g, t))
                values(1, 2)
                pe.wait_ge(sem["e_lo"], nth(g, t))
                mm(bank[4][:, 0:3 * BH * KC], ones[:, :], esp[:, g, :, :].rearrange("p k i -> p (k i)"),
                   start=True, stop=True).then_inc(sem["z_ps"], 1)
                values(0, 3).then_inc(sem["v_ps"], 1)

            pe.wait_ge(sem["l_gxlow"], 4)
            pe.wait_ge(sem["l_split"], 2 * B + 1)
            pe.wait_ge(sem["l_zero"], 3 + 4)
            for g in range(2):
                x_gates(g, 0)
                h_gates(g)
            lstm_loop(pe, half)
            pe.wait_ge(sem["y_st"], 2 * S)
            for j in range(NJ):
                ins = pe.transpose(bank[7][:, j * P:(j + 1) * P],
                                   yT[:, j * BT:(j + 1) * BT, :].rearrange("p b t -> p (b t)"), ident)
            ins.then_inc(sem["y_tr"], 1)

            ln_transpose(4)
            pe.wait_ge(sem["d_late"], 64)
            pe.wait_ge(sem["m_const"], MC + 5)
            for l in range(ML):
                pe.wait_ge(sem["ln_xT"], 5 + l)
                if l:
                    pe.wait_ge(sem["m_ys"], l * MC)
                for n in range(2 * MC):
                    ins = pe.matmul(bank[n // 2][:, (n % 2) * TOK:(n % 2 + 1) * TOK],
                                    m_in[:, (4 * l + n) * P:(4 * l + n + 1) * P], xnT[:, :], start=True, stop=True)
                    if n % 2:
                        ins.then_inc(sem["m_uz"], 1)
                if l:
                    pe.wait_ge(sem["m_csb"], l * MNP)
                for ch in range(MC):
                    pe.wait_ge(sem["m_us"], l * MC + ch + 1)
                    at = (l * MC + ch) * (6 * MN + MR)
                    ins = pe.matmul(bank[2][0:6 * MN + MR, 0:TOK], m_x[:, at:at + 6 * MN + MR],
                                    T[:, 1, ch * TOK:(ch + 1) * TOK], start=(ch == 0), stop=(ch == MC - 1))
                ins.then_inc(sem["m_bc"], 1)
                pe.wait_ge(sem["m_dts"], l + 1)
                for ch in range(MC):
                    at = l * MI + ch * P
                    ins = pe.matmul(bank[4][:, ch * TOK:(ch + 1) * TOK], dtw[:, at:at + P], dts[:, :], start=True, stop=True)
                ins.then_inc(sem["m_dps"], 1)
                pe.wait_ge(sem["m_bcs"], l + 1)

                def spread(b, n):
                    for k in range(2):
                        ins = pe.matmul(bank[b][:, k * TOK:(k + 1) * TOK], pat(sel[:, n + k:n + k + 1], [[0, P]]),
                                        bcs[:, :], start=True, stop=True)
                    return ins

                for i in range(MNP + LAG):
                    if i < MNP:
                        n = l * MNP + i
                        if i >= 2:
                            pe.wait_ge(sem["m_bsb"], n - 1)
                            pe.wait_ge(sem["m_csb"], n - 1)
                        spread(2 + i % 2, 2 * i).then_inc(sem["m_bps"], 1)
                        spread(5 + i % 2, MN + 2 * i).then_inc(sem["m_cps"], 1)
                    if i == 0:
                        for ch in range(MC):
                            pe.wait_ge(sem["m_ud"], l * MC + ch + 1)
                            pe.matmul(bank[0][:, ch * TOK:(ch + 1) * TOK], ident, T[:, 0, ch * TOK:(ch + 1) * TOK],
                                      start=(ch == 0), stop=False, skip_group_check=True)
                    if i >= LAG:
                        n = l * MNP + i - LAG
                        for ch in range(MC):
                            pe.wait_ge(sem["m_hc0" if ch == 0 else "m_hc1"], n + 1)
                            for k in range(2):
                                at = (2 * (i - LAG) + k) * TOK
                                ins = pe.matmul(bank[0][:, ch * TOK:(ch + 1) * TOK], ident, state[ch][:, at:at + TOK],
                                                start=False, stop=(i == MNP + LAG - 1),
                                                skip_group_check=True)
                ins.then_inc(sem["m_y"], 1)
                for ch in range(MC):
                    pe.wait_ge(sem["m_ys"], l * MC + ch + 1)
                    at = (l * MC + ch) * D
                    for j in range(NJ):
                        ins = pe.matmul(bank[4][:, j * D:(j + 1) * D], T[:, 13, ch * TOK + j * P:ch * TOK + (j + 1) * P],
                                        m_out[:, at:at + D], start=(ch == 0 and j == 0), stop=(ch == MC - 1),
                                        skip_group_check=True)
                ins.then_inc(sem["m_o"], 1)
                ln_transpose(5 + l)

            ln_transpose(5 + ML)
            pe.wait_ge(sem["ln_xT"], transposed(5 + ML))
            pe.wait_ge(sem["d_late"], 64)
            lora, wi, wo = fw[:, E:E + E * LR], fw[:, E + E * LR:E + E * LR + F], fw[:, E + E * LR + F:]
            for j in range(NJ):
                ins = pe.matmul(bank[6][:, j * E:(j + 1) * E], xnT[:, j * P:(j + 1) * P], fw[:, 0:E], start=True, stop=True)
            ins.then_inc(sem["r_gate"], 1)
            for j in range(NJ):
                ins = pe.matmul(bank[7][:, j * E * LR:(j + 1) * E * LR], xnT[:, j * P:(j + 1) * P], lora,
                                start=True, stop=True)
            ins.then_inc(sem["r_a"], 1)
            for fc in range(FC):
                if fc == FC - 1:
                    pe.wait_ge(sem["r_am"], 1)
                    for j in range(NJ):
                        ins = pe.transpose(bank[5][0:E * LR, j * P:(j + 1) * P], loraa[:, j, :], ident)
                    ins.then_inc(sem["r_amps"], 1)
                pe.matmul(bank[fc][:, 0:TOK], wi[:, fc * P:(fc + 1) * P], xnT[:, :], start=True, stop=False)
            pe.wait_ge(sem["r_amT"], 1)
            for fc in range(FC + 1):
                if fc < FC:
                    pe.matmul(bank[fc][:, 0:TOK], lb[:, fc * P:(fc + 1) * P], cwT[:, :], start=False, stop=True) \
                      .then_inc(sem["r_h"], 1)
                if fc >= 1:
                    pe.wait_ge(sem["r_act"], fc)
                    for j in range(NJ):
                        at = ((fc - 1) % 2) * TOK + j * P
                        ins = pe.matmul(bank[4][:, j * D:(j + 1) * D], T[:, (fc - 1) // 2, at:at + P],
                                        wo[:, (fc - 1) * D:fc * D], start=(fc == 1 and j == 0), stop=(fc == FC),
                                        skip_group_check=True)
            ins.then_inc(sem["r_o"], 1)


def lay_out(i):
    a = {k: np.asarray(x) for k, x in i.items()}

    def wide(m):
        return m.reshape(-1, P, m.shape[-1]).transpose(1, 0, 2).reshape(P, -1)

    ctxT = a["ctx_1024"].reshape(B * SK, D).T
    kv = a["L0_xattn_Wkv"]
    wx = np.concatenate([kv[:D], a["L0_xattn_Wq"], kv[D:].T, a["L0_xattn_Wo"].T], 1)

    def col(x, times=1):
        return np.tile(x, times).reshape(-1, P).T

    n = "L1_attn_"
    parts = {
        "bq": col(a["L0_xattn_bq"]), "bk": col(a["L0_xattn_bkv"][:D]), "bv": col(a["L0_xattn_bkv"][D:]),
        "qw": col(a["L0_xattn_qn_w"], XH), "qb": col(a["L0_xattn_qn_b"], XH),
        "kw": col(a["L0_xattn_kn_w"], XH), "kb": col(a["L0_xattn_kn_b"], XH),
        "aqw": col(a["L0_attn_qn_w"], 2), "aqb": col(a["L0_attn_qn_b"], 2),
        "akw": col(a["L0_attn_kn_w"], 2), "akb": col(a["L0_attn_kn_b"], 2),
        "sink": np.broadcast_to(a["L0_attn_sinks"], (P, AH)),
        "b1": a["L0_ffn_b1"].reshape(E * FC, P).T, "bs1": col(a["L0_ffn_bs1"]),
        "bih": lstm_order(a["L1_xattn_b_ih"]).reshape(4, P).T, "bhh": lstm_order(a["L1_xattn_b_hh"]).reshape(4, P).T,
        "bout": col(a["L1_xattn_b_out"]),
        "convw": a[n + "conv_w"].reshape(ML * MC, P, MK).transpose(1, 0, 2).reshape(P, -1),
        "convb": a[n + "conv_b"].reshape(ML * MC, P).T, "dtb": a[n + "dt_proj_b"].reshape(ML * MC, P).T,
        "mD": a[n + "D"].reshape(ML * MC, P).T,
        "alog": a[n + "A_log"].reshape(ML * MC, P, MN).transpose(1, 0, 2).reshape(P, -1),
        "wib": col(a["L1_ffn_wi_b"]),
    }
    vec = np.concatenate([parts[k].reshape(P, w) for k, w in V_NAMES], 1)
    lines = {"bo": a["L0_xattn_bo"], "projb": a["L0_attn_proj_b"], "bs2": a["L0_ffn_bs2"], "wob": a["L1_ffn_wo_b"],
             "gateb": a["L1_ffn_gate_b"], "lnw": a[n + "ln_w"].reshape(-1), "lnb": a[n + "ln_b"].reshape(-1)}
    rows = np.broadcast_to(np.concatenate([lines[k] for k, _ in R_NAMES]), (P, R_END))
    w_ih = lstm_order(a["L1_xattn_W_ih"])
    xp = a[n + "x_proj_w"].reshape(ML, MC, P, MR + 2 * MN)
    xp = np.concatenate([xp[..., MR:]] * 3 + [xp[..., :MR]], -1).transpose(2, 0, 1, 3).reshape(P, -1)
    outs = {
        "x": a["x"].reshape(TOK, D), "cst": shape_constants(), "vec": vec, "rows": rows, "wx": wx, "ctxT": ctxT,
        "mask": a["mask_BxS2_bk0"].reshape(1, B * SK),
        "qkvT": a["L0_attn_qkv_w"].T, "projT": wide(a["L0_attn_proj_w"].T),
        "wg": a["L0_ffn_Wg"], "w1": a["L0_ffn_W1"].transpose(1, 0, 2).reshape(P, E * F),
        "w2": wide(a["L0_ffn_W2"].reshape(E * F, D)), "b2": a["L0_ffn_b2"],
        "ws": np.concatenate([a["L0_ffn_Ws1"], wide(a["L0_ffn_Ws2"])], 1),
        "lw": np.concatenate([w_ih[:, :D].T, w_ih[:, D:].T, lstm_order(a["L1_xattn_W_hh"]).T,
                              a["L1_xattn_Wout"][:, D:].T, a["L1_xattn_Wout"][:, :D].T, a["L1_xattn_Wq"]], 1),
        "mw": np.concatenate([a[n + "in_proj_w"].transpose(1, 0, 2).reshape(P, -1), xp,
                              a[n + "out_proj_w"].reshape(ML * MC, P, D).transpose(1, 0, 2).reshape(P, -1)], 1),
        "dtw": a[n + "dt_proj_w"].transpose(1, 0, 2).reshape(MR, -1),
        "fw": np.concatenate([a["L1_ffn_gate_W"].T, a["L1_ffn_lora_A"].reshape(E * LR, D).T,
                              a["L1_ffn_wi_W"].T, wide(a["L1_ffn_wo_W"].T)], 1),
        "lb": a["L1_ffn_lora_B"].transpose(0, 2, 1).reshape(E * LR, F),
    }
    return {k: np.ascontiguousarray(x) for k, x in outs.items()}


def lstm_order(w):
    i, f, g, o = np.split(w, 4, 0)
    return np.concatenate([i, f, o, g], 0)


def kernel(**inputs):
    import concourse.bacc as _bacc
    from concourse.bass_utils import run_bass_kernel_spmd as _run

    nc = _bacc.Bacc("TRN2", target_bir_lowering=False, num_devices=1)
    arrays = {f"in_{k}_dram": x for k, x in lay_out(inputs).items()}
    arr = {k[3:-5]: nc.dram_tensor(k, x.shape, mybir.dt.from_np(x.dtype), kind="ExternalInput").ap()
           for k, x in arrays.items()}
    out = nc.dram_tensor("out_0_dram", (TOK, D), F32, kind="ExternalOutput").ap()
    build(nc, arr, out)
    got = _run(nc, [arrays], core_ids=[0])
    return got.results[0]["out_0_dram"].reshape(B, S, D)
```
